# Optimizing a Trainium2 kernel written in Bass

```python
import numpy as np
import jax
import jax.numpy as jnp

def _softmax(x, axis=-1):
    return jax.nn.softmax(x, axis=axis)

def _gelu(x):
    return jax.nn.gelu(x, approximate=True)

def _silu(x):
    return jax.nn.silu(x)

def _sigmoid(x):
    return jax.nn.sigmoid(x)

def _layernorm(x, axis=-1, eps=1e-05):
    m = jnp.mean(x, axis=axis, keepdims=True)
    v = jnp.var(x, axis=axis, keepdims=True)
    return (x - m) / jnp.sqrt(v + eps)

def _scatter_add(tgt, idx, src, axis=0):
    return tgt.at[idx].add(src)

def _segment_sum(src, seg, n):
    return jax.ops.segment_sum(src, seg, n)
kernel_name = 'mk_recurrent_d2_jaxref_r8_aeaab0'

def setup_inputs(seed: int=0):
    np.random.seed(seed)
    _w = jnp.asarray

    def _L0_attn_setup():
        import jax, jax.numpy as jnp
        import numpy as np
        HIDDEN = 256
        N_HEADS = 16
        N_KV_HEADS = 4
        HEAD_DIM = HIDDEN // N_HEADS
        ROPE_THETA = 10000.0
        B, S = (1, 256)

        def _apply_rope(x, position_ids, theta=ROPE_THETA):
            b, s, h, hd = x.shape
            dim_half = hd // 2
            inv_freq = 1.0 / theta ** (jnp.arange(0, dim_half, 2, dtype=jnp.float32) / dim_half)
            freqs = position_ids[:, :, None].astype(jnp.float32) * inv_freq[None, None, :]
            cos = jnp.cos(freqs)[:, :, None, :]
            sin = jnp.sin(freqs)[:, :, None, :]
            x_rot = x[..., :dim_half].reshape(b, s, h, dim_half // 2, 2)
            x0, x1 = (x_rot[..., 0], x_rot[..., 1])
            rotated = jnp.stack([x0 * cos - x1 * sin, x0 * sin + x1 * cos], axis=-1)
            rotated = rotated.reshape(b, s, h, dim_half)
            return jnp.concatenate([rotated, x[..., dim_half:]], axis=-1)
        key = jax.random.key(seed)
        k0, k1, k2, k3, k4 = jax.random.split(key, 5)
        std = 0.02
        return {'hidden_states': jax.random.normal(k0, (B, S, HIDDEN), dtype=jnp.float32), 'Wq': jax.random.normal(k1, (HIDDEN, N_HEADS * HEAD_DIM), dtype=jnp.float32) * std, 'Wk': jax.random.normal(k2, (HIDDEN, N_KV_HEADS * HEAD_DIM), dtype=jnp.float32) * std, 'Wv': jax.random.normal(k3, (HIDDEN, N_KV_HEADS * HEAD_DIM), dtype=jnp.float32) * std, 'Wo': jax.random.normal(k4, (HIDDEN, HIDDEN), dtype=jnp.float32) * std}
    _L0_attn_in = _L0_attn_setup()

    def _L0_ffn_setup():
        import jax, jax.numpy as jnp
        import numpy as np
        HIDDEN = 256
        INTER = 1024
        BATCH, LOCAL_SEQ = (2, 512)
        key = jax.random.key(seed)
        k1, k2, k3 = jax.random.split(key, 3)
        h_shard = jax.random.normal(k1, (BATCH, LOCAL_SEQ, HIDDEN), dtype=jnp.float32)
        w_gate_up = jax.random.normal(k2, (2 * INTER, HIDDEN), dtype=jnp.float32) * 0.02
        w_down = jax.random.normal(k3, (HIDDEN, INTER), dtype=jnp.float32) * 0.02
        return {'h_shard': h_shard, 'w_gate_up': w_gate_up, 'w_down': w_down}
    _L0_ffn_in = _L0_ffn_setup()

    def _L1_attn_setup():
        import jax, jax.numpy as jnp
        import numpy as np
        ROPE_THETA = 10000.0

        def rope(t, rot_dim):
            S = t.shape[-2]
            half = rot_dim // 2
            inv_freq = 1.0 / ROPE_THETA ** (jnp.arange(0, rot_dim, 2, dtype=jnp.float32) / rot_dim)
            freqs = jnp.arange(S, dtype=jnp.float32)[:, None] * inv_freq[None, :]
            freqs = jnp.repeat(freqs, 2, axis=-1)
            cos, sin = (jnp.cos(freqs), jnp.sin(freqs))
            t_rot, t_pass = (t[..., :rot_dim], t[..., rot_dim:])
            x = t_rot.reshape(*t_rot.shape[:-1], half, 2)
            rh = jnp.stack([-x[..., 1], x[..., 0]], axis=-1).reshape(t_rot.shape)
            t_rot = t_rot * cos + rh * sin
            return jnp.concatenate([t_rot, t_pass], axis=-1)

        def feature_map(x):
            norm = jnp.sqrt(jnp.sum(x * x, axis=-1, keepdims=True))
            return x / jnp.maximum(norm, 1e-12)
        key = jax.random.key(seed)
        kx, kwi, kwo = jax.random.split(key, 3)
        B, S, D = (8, 512, 256)
        scale = 0.02
        return {'X': jax.random.normal(kx, (B, S, D), dtype=jnp.float32), 'W_in': jax.random.normal(kwi, (3 * D, D), dtype=jnp.float32) * scale, 'b_in': jnp.zeros((3 * D,), dtype=jnp.float32), 'W_out': jax.random.normal(kwo, (D, D), dtype=jnp.float32) * scale, 'b_out': jnp.zeros((D,), dtype=jnp.float32)}
    _L1_attn_in = _L1_attn_setup()

    def _L1_ffn_setup():
        import jax, jax.numpy as jnp
        import numpy as np
        H, I, E = (256, 512, 8)
        B, S = (2, 256)
        key = jax.random.key(seed)
        ks = jax.random.split(key, 5)
        scale = 0.02
        return {'hidden_states': jax.random.normal(ks[0], (B, S, H), dtype=jnp.float32), 'router_w': jax.random.normal(ks[1], (H, E), dtype=jnp.float32) * scale, 'gate_w': jax.random.normal(ks[2], (E, H, I), dtype=jnp.float32) * scale, 'up_w': jax.random.normal(ks[3], (E, H, I), dtype=jnp.float32) * scale, 'down_w': jax.random.normal(ks[4], (E, I, H), dtype=jnp.float32) * scale}
    _L1_ffn_in = _L1_ffn_setup()
    _d = {'L0_attn_hidden_states': _L0_attn_in['hidden_states'], 'L0_attn_Wq': _L0_attn_in['Wq'], 'L0_attn_Wk': _L0_attn_in['Wk'], 'L0_attn_Wv': _L0_attn_in['Wv'], 'L0_attn_Wo': _L0_attn_in['Wo'], 'L0_ffn_w_gate_up': _L0_ffn_in['w_gate_up'], 'L0_ffn_w_down': _L0_ffn_in['w_down'], 'L1_attn_W_in': _L1_attn_in['W_in'], 'L1_attn_b_in': _L1_attn_in['b_in'], 'L1_attn_W_out': _L1_attn_in['W_out'], 'L1_attn_b_out': _L1_attn_in['b_out'], 'L1_ffn_router_w': _L1_ffn_in['router_w'], 'L1_ffn_gate_w': _L1_ffn_in['gate_w'], 'L1_ffn_up_w': _L1_ffn_in['up_w'], 'L1_ffn_down_w': _L1_ffn_in['down_w']}
    _x0 = _d['L0_attn_hidden_states']
    _d['L0_attn_hidden_states'] = jax.random.normal(jax.random.fold_in(jax.random.key(seed), 1), (2, 512, 256), dtype=_x0.dtype)
    del _x0
    return _d

def reference(L0_attn_hidden_states, L0_attn_Wq, L0_attn_Wk, L0_attn_Wv, L0_attn_Wo, L0_ffn_w_gate_up, L0_ffn_w_down, L1_attn_W_in, L1_attn_b_in, L1_attn_W_out, L1_attn_b_out, L1_ffn_router_w, L1_ffn_gate_w, L1_ffn_up_w, L1_ffn_down_w):

    def _L0_attn_ref(hidden_states, Wq, Wk, Wv, Wo):
        import jax, jax.numpy as jnp
        import numpy as np
        HIDDEN = 256
        N_HEADS = 16
        N_KV_HEADS = 4
        HEAD_DIM = HIDDEN // N_HEADS
        ROPE_THETA = 10000.0
        B, S = (1, 256)

        def _apply_rope(x, position_ids, theta=ROPE_THETA):
            b, s, h, hd = x.shape
            dim_half = hd // 2
            inv_freq = 1.0 / theta ** (jnp.arange(0, dim_half, 2, dtype=jnp.float32) / dim_half)
            freqs = position_ids[:, :, None].astype(jnp.float32) * inv_freq[None, None, :]
            cos = jnp.cos(freqs)[:, :, None, :]
            sin = jnp.sin(freqs)[:, :, None, :]
            x_rot = x[..., :dim_half].reshape(b, s, h, dim_half // 2, 2)
            x0, x1 = (x_rot[..., 0], x_rot[..., 1])
            rotated = jnp.stack([x0 * cos - x1 * sin, x0 * sin + x1 * cos], axis=-1)
            rotated = rotated.reshape(b, s, h, dim_half)
            return jnp.concatenate([rotated, x[..., dim_half:]], axis=-1)
        b, s, _ = hidden_states.shape
        groups = N_HEADS // N_KV_HEADS
        q = (hidden_states @ Wq).reshape(b, s, N_HEADS, HEAD_DIM)
        k = (hidden_states @ Wk).reshape(b, s, N_KV_HEADS, HEAD_DIM)
        v = (hidden_states @ Wv).reshape(b, s, N_KV_HEADS, HEAD_DIM)
        position_ids = jnp.broadcast_to(jnp.arange(s)[None, :], (b, s))
        q = _apply_rope(q, position_ids)
        k = _apply_rope(k, position_ids)
        if groups > 1:
            k = jnp.repeat(k, groups, axis=2)
            v = jnp.repeat(v, groups, axis=2)
        scale = 1.0 / jnp.sqrt(jnp.float32(HEAD_DIM))
        scores = jnp.einsum('bshd,bthd->bhst', q, k) * scale
        attn = jax.nn.softmax(scores, axis=-1)
        out = jnp.einsum('bhst,bthd->bshd', attn, v)
        out = out.reshape(b, s, HIDDEN)
        return out @ Wo

    def _L0_ffn_ref(h_shard, w_gate_up, w_down):
        import jax, jax.numpy as jnp
        import numpy as np
        HIDDEN = 256
        INTER = 1024
        BATCH, LOCAL_SEQ = (2, 512)
        batch, local_seq, hidden = h_shard.shape
        gate_up = jnp.einsum('bsh,oh->bso', h_shard, w_gate_up)
        gate, up = jnp.split(gate_up, 2, axis=-1)
        h = jax.nn.silu(gate) * up
        out = jnp.einsum('bsi,hi->bsh', h, w_down)
        return out

    def _L1_attn_ref(X, W_in, b_in, W_out, b_out):
        import jax, jax.numpy as jnp
        import numpy as np
        ROPE_THETA = 10000.0

        def rope(t, rot_dim):
            S = t.shape[-2]
            half = rot_dim // 2
            inv_freq = 1.0 / ROPE_THETA ** (jnp.arange(0, rot_dim, 2, dtype=jnp.float32) / rot_dim)
            freqs = jnp.arange(S, dtype=jnp.float32)[:, None] * inv_freq[None, :]
            freqs = jnp.repeat(freqs, 2, axis=-1)
            cos, sin = (jnp.cos(freqs), jnp.sin(freqs))
            t_rot, t_pass = (t[..., :rot_dim], t[..., rot_dim:])
            x = t_rot.reshape(*t_rot.shape[:-1], half, 2)
            rh = jnp.stack([-x[..., 1], x[..., 0]], axis=-1).reshape(t_rot.shape)
            t_rot = t_rot * cos + rh * sin
            return jnp.concatenate([t_rot, t_pass], axis=-1)

        def feature_map(x):
            norm = jnp.sqrt(jnp.sum(x * x, axis=-1, keepdims=True))
            return x / jnp.maximum(norm, 1e-12)
        D = X.shape[-1]
        QKV = jnp.einsum('bsd,ed->bse', X, W_in) + b_in
        Q, K, V = jnp.split(QKV, 3, axis=-1)
        rot_dim = D // 2
        Q = rope(Q, rot_dim)
        K = rope(K, rot_dim)
        A = jnp.sum(feature_map(K) * V, axis=-2)
        Y = A[:, None, :] * Q
        Y = jnp.einsum('bsd,ed->bse', Y, W_out) + b_out
        return Y + X

    def _L1_ffn_ref(hidden_states, router_w, gate_w, up_w, down_w):
        import jax, jax.numpy as jnp
        import numpy as np
        H, I, E = (256, 512, 8)
        B, S = (2, 256)
        hidden_shape = hidden_states.shape
        x = hidden_states.reshape(-1, hidden_shape[-1])
        route = jax.nn.sigmoid(x @ router_w)
        max_ind = jnp.argmax(route, axis=1)
        max_prob = jnp.take_along_axis(route, max_ind[:, None], axis=1)
        out = jnp.zeros_like(x)
        num_experts = gate_w.shape[0]
        for e in range(num_experts):
            mask = (max_ind == e)[:, None]
            h = jax.nn.silu(x @ gate_w[e]) * (x @ up_w[e])
            out = out + jnp.where(mask, h @ down_w[e], 0.0)
        out = out * max_prob
        return out.reshape(hidden_shape)
    x = L0_attn_hidden_states
    xn = _layernorm(x, axis=-1)
    s = _L0_attn_ref(xn, L0_attn_Wq, L0_attn_Wk, L0_attn_Wv, L0_attn_Wo)
    g = _silu(_L0_ffn_ref(xn, L0_ffn_w_gate_up, L0_ffn_w_down))
    x = x + s * g
    xn = _layernorm(x, axis=-1)
    s = _L1_attn_ref(xn, L1_attn_W_in, L1_attn_b_in, L1_attn_W_out, L1_attn_b_out)
    g = _silu(_L1_ffn_ref(xn, L1_ffn_router_w, L1_ffn_gate_w, L1_ffn_up_w, L1_ffn_down_w))
    x = x + s * g
    return x

_drawn_inputs = setup_inputs


def setup_inputs(seed=0):
    import zlib

    import numpy as np

    out = dict(_drawn_inputs(seed))
    spreads = {'L1_attn_b_in': (0.0, 0.8), 'L1_attn_b_out': (0.0, 0.8)}
    factors = {'L0_attn_Wq': 8.0,
     'L0_attn_Wk': 8.0,
     'L0_attn_Wv': 8.0,
     'L0_attn_Wo': 8.0,
     'L0_ffn_w_gate_up': 8.0,
     'L0_ffn_w_down': 8.0,
     'L1_attn_W_in': 8.0,
     'L1_attn_W_out': 8.0,
     'L1_ffn_router_w': 8.0,
     'L1_ffn_gate_w': 7.611,
     'L1_ffn_up_w': 7.553,
     'L1_ffn_down_w': 7.551}
    for name, (base, spread) in spreads.items():
        noise = np.random.default_rng([zlib.crc32(name.encode()), seed]).standard_normal(out[name].shape)
        drawn = base * np.exp(spread * noise) if base else spread * noise
        out[name] = jnp.asarray(drawn.astype(out[name].dtype))
    for name, factor in factors.items():
        out[name] = (out[name] * factor).astype(out[name].dtype)
    return out
```

```python
from contextlib import ExitStack

import numpy as np
import concourse.bass as bass
from concourse import mybir

ALU = mybir.AluOpType
ACT = mybir.ActivationFunctionType
F32 = mybir.dt.float32
BF16 = mybir.dt.bfloat16
I32 = mybir.dt.int32
AX = mybir.AxisListType.X

P = 128
B, S, D = 2, 512, 256
TOK = B * S
NT = TOK // P
TB = S // P
KD = D // P
HEADS, KVH, HD = 16, 4, 16
GR = HEADS // KVH
QKH = HEADS + KVH
INTER = 1024
NI = INTER // P
E, EI = 8, 512
KE = EI // P
EW = 2 * KD * EI + KE * D
MT = TOK // P + E - 1
SLOTS = MT * P
SPLIT = 3
NSTACK = 6
KS = NSTACK * HD
KM = KS + SPLIT
VW = 32
LN_EPS = 1e-5
UNITS = B * KVH
STEPS = UNITS * TB
ROT = D // 2


def const_columns():
    widths = [("ident", P), ("before", P), ("ones", P), ("cos0", TB * 8), ("sin0e", TB * 4), ("sin0o", TB * 4),
              ("cos1", TB * ROT), ("sin1e", TB * ROT // 2), ("sin1o", TB * ROT // 2),
              ("desc", E), ("full", NT), ("lower", E * E), ("tile_id", MT)]
    at, out = 0, {}
    for name, w in widths:
        out[name] = (at, w)
        at += w
    return out, at


def constants():
    cols, width = const_columns()
    c = np.zeros((P, width), np.float32)

    def put(name, a):
        lo, w = cols[name]
        c[:, lo:lo + w] = np.asarray(a, np.float32).reshape(-1, w) if np.asarray(a).size != w else np.ravel(a)

    def angles(dim):
        inv = (np.float32(1.0) / np.float32(10000.0) ** (np.arange(0, dim, 2, dtype=np.float32) / np.float32(dim)))
        pos = np.arange(S, dtype=np.float32)
        f = (pos[:, None] * inv[None, :]).astype(np.float32)
        return f.reshape(TB, P, dim // 2).transpose(1, 0, 2)

    p = np.arange(P)
    put("ident", np.eye(P))
    put("before", (p[:, None] < p[None, :]).astype(np.float32))
    put("ones", np.ones((P, P)))
    a = angles(HD // 2)
    put("cos0", np.repeat(np.cos(a), 2, axis=-1).reshape(P, -1))
    put("sin0e", -np.sin(a).reshape(P, -1))
    put("sin0o", np.sin(a).reshape(P, -1))
    a = angles(ROT)
    put("cos1", np.repeat(np.cos(a), 2, axis=-1).reshape(P, -1))
    put("sin1e", -np.sin(a).reshape(P, -1))
    put("sin1o", np.sin(a).reshape(P, -1))
    e = np.arange(E)
    put("desc", E - e)
    put("full", np.arange(NT) * P)
    put("lower", (e[None, :] < e[:, None]).astype(np.float32).ravel())
    put("tile_id", np.arange(MT))
    return c


def attention_plan():
    fill = []
    for b in range(B):
        for i in range(NI):
            fill += [("gate", b * NI + i, k) for k in range(KD)] + [("up", b * NI + i, k) for k in range(KD)]
        for j in range(TB):
            fill += [("down", b * TB + j, i) for i in range(NI)]
    cost = {"gate": 2, "up": 2, "down": 1}
    total = sum(cost[f[0]] for f in fill)
    spent = 0
    after = {}
    for u in range(UNITS):
        after.setdefault(4 * u + 4, []).append(("heads_out", u))
        after.setdefault(4 * u + 5, []).append(("heads_norm", u))
    for b in range(B):
        at = 4 * (TB * b + KVH - 1) + 6
        for k in range(KD):
            after.setdefault(at, []).append(("attn_T", b, k))
        for c in range(TB // 2):
            after.setdefault(at + 1 if b == 0 else at, []).append(("wo", b, c))
    plan = [("score", m) for m in range(16)] + [("max_parts", 0), ("max_rows", 0)]
    for n in range(STEPS + 3):
        u, t = divmod(n, TB)
        step = []
        live = n < STEPS
        budget = total * (n + 1) // STEPS if live else total
        def take(upto):
            nonlocal spent
            while fill and spent < upto:
                f = fill.pop(0)
                spent += cost[f[0]]
                step.append(f)
        if live:
            todo = []
            if u + 1 < UNITS and t < 3:
                lo, hi = (0, 6, 11, 16)[t], (0, 6, 11, 16)[t + 1]
                todo = [("score", 16 * (u + 1) + m) for m in range(lo, hi)]
            q = (budget - spent + 3) // 4
            for hh in range(GR):
                step.append(("prob", n, hh))
                if hh == 1 and n > 0:
                    step.append(("values", n - 1))
                    step += [x for x in after.get(n, []) if x[0] == "heads_out"]
                cut = (len(todo) + (GR - 1 - hh)) // (GR - hh)
                step += todo[:cut]
                todo = todo[cut:]
                take(min(budget, spent + q))
            if u + 1 < UNITS and t == 2:
                step.append(("max_parts", u + 1))
            step += [x for x in after.get(n, []) if x[0] != "heads_out"]
            if u + 1 < UNITS and t == 2:
                take(min(total, spent + 2))
                step.append(("max_rows", u + 1))
        else:
            if n == STEPS:
                step.append(("values", n - 1))
            step += after.get(n, [])
        take(budget)
        plan += step
    assert not fill
    return plan


def two_gated_blocks(nc, x_in, wqkv_in, wo_in, wgu_in, wdn_in, win_in, bin_in, wout_in, bout_in,
                     router_in, experts_in, const_in, out):
    cols, cwidth = const_columns()
    plan = attention_plan()

    xs_dram = nc.dram_tensor("slot_rows", (SLOTS, D), F32, kind="Internal").ap()
    ys_dram = nc.dram_tensor("slot_results", (SLOTS, D), F32, kind="Internal").ap()

    with ExitStack() as ctx:
        def sb(name, shape, dt=F32):
            return ctx.enter_context(nc.sbuf_tensor(name, shape, dt))

        def sem(name):
            return ctx.enter_context(nc.semaphore(name))

        x = sb("x", [P, NT, D])
        xn = sb("xn", [P, NT, D])
        xnT = sb("xnT", [P, KD, TOK])
        gx = sb("gx", [P, NT, D])
        Wm = sb("experts", [P, E * EW])
        Sa = sb("shared", [P, 10240])
        win = sb("win", [P, KD, 3 * D])
        wl0 = sb("wl0", [P, 1280])
        wout = sb("wout", [P, KD, D])
        bin_b = sb("bin_b", [P, 3 * D])
        bout_b = sb("bout_b", [P, D])
        router = sb("router", [P, KD, E])
        cst = sb("cst", [P, cwidth])
        identb = sb("identb", [P, P], BF16)
        tanh_g = sb("tanh_g", [P, 2, 512])
        gated = sb("gated", [P, 2, 512])
        xs = sb("xs", [P, 2, D])
        xsT = sb("xsT", [P, 2, D])
        ysb = sb("ysb", [P, 2, D])
        bn = sb("bn", [P, NT, 6])
        mv = sb("mv", [P, NT, 2])
        st1 = sb("st1", [P, 6, NT])
        small = sb("small", [P, 3, 80])
        smi = sb("smi", [P, NT], I32)
        tile_e = sb("tile_e", [P, MT], I32)
        rsum = sb("rsum", [P, 16])
        nmax = sb("nmax", [P, 16])
        nres = sb("nres", [P, 2, 16])
        mparts = sb("mparts", [P, TB, SPLIT, GR], BF16)
        acol = sb("acol", [P, 4])

        def const(name):
            lo, w = cols[name]
            return cst[:, lo:lo + w]

        ident = const("ident")
        wqkv = wl0[:, 0:768].rearrange("p (k n) -> p k n", k=KD)
        wo = wl0[:, 768:1280].rearrange("p (k n) -> p k n", k=KD)

        at = [EW]

        def in_experts(words):
            at[0] += words
            assert at[0] <= E * EW
            return Wm[:, at[0] - words:at[0]]

        qs = in_experts(8192).bitcast(BF16).rearrange("p (b h s) -> p b h s", b=B, h=HEADS)
        ks = in_experts(2048).bitcast(BF16).rearrange("p (b h s) -> p b h s", b=B, h=KVH)
        hT = in_experts(NI * S).rearrange("p (i s) -> p i s", i=NI)
        qk = in_experts(NT * QKH * HD).rearrange("p (j n) -> p j n", j=NT)
        vaug = in_experts(NT * KVH * VW).rearrange("p (j g c) -> p j g c", j=NT, g=KVH)
        an = in_experts(TB * D).rearrange("p (t n) -> p t n", t=TB)
        anT = in_experts(KD * S).rearrange("p (k s) -> p k s", k=KD)
        oTs = in_experts(S)
        mrow = in_experts(512).bitcast(BF16).rearrange("p (a s) -> p a s", a=2)

        probs = Sa[:, 0:4096].rearrange("p (a h s) -> p a h s", a=2, h=GR)
        stack = Sa[:, 0:TB * QKH * KS // 2].bitcast(BF16).rearrange("p (n c) -> p n c", c=KS)
        wgu = Sa[:, 4096:8192].rearrange("p (k n) -> p k n", k=KD)
        wdn = Sa[:, 8192:10240].rearrange("p (i n) -> p i n", i=NI)
        rot_a = gx[:, 0:5, :].rearrange("p a b -> p (a b)")
        qkv1 = Sa[:, 0:6144].rearrange("p (j n) -> p j n", j=NT)
        kv = Sa[:, 6144:8192].rearrange("p (j n) -> p j n", j=NT)
        rope_t = Sa[:, 8192:10240]
        yg = Sa[:, 0:2048].rearrange("p (j n) -> p j n", j=NT)
        hmT = Sa[:, 8192:9216].rearrange("p (a n) -> p a n", a=2)
        wsc = Sa[:, 9216:10240].rearrange("p (b k n) -> p b k n", b=B, k=KD)
        hm = wl0[:, 0:1024].rearrange("p (a n) -> p a n", a=2)

        ps = ctx.enter_context(nc.psum_tensor("ps", [P, 8, 512], F32))
        misc = ps[:, 5, :]
        miscb = misc.bitcast(BF16)

        x_in_s = [sem(f"x_loaded{b}") for b in range(B)]
        names = ("acol_psum acol_ready act_step attn_T_ready branch_free branch_psum branch_ready const_loaded "
                 "counts down_ready down_tanh dve_step e_down e_gate e_gated e_h e_tanh e_up exp_done "
                 "expert0_loaded experts_here gate_free gate_ready gathered heads_T heads_copied hmT_ready hm_T "
                 "identb_ready ksum_sq kv_ready late_loaded logits logits_exp max_done misc_free mparts_ready "
                 "mrow_psum norm_in norm_ready norm_sqrt onehot out_ready out_stored0 out_stored1 parts_done "
                 "prob_ready qT_psum qT_ready qk_copied qkv1_psum qkv1_ready qkv_psum rope_q rows_norm rstd_ready "
                 "scattered score_ready slots sqrt_done stack_T stack_copied stack_copied2 std_in tanh_done "
                 "tile_experts up_free up_ready v_copied values_done vone w_ready w_tanh wdn_loaded wgu_loaded "
                 "wo_loaded wo_ready wqkv_loaded wsc_ready x1_part xnT_psum xnT_ready xsT_ready xs_T xs_loaded0 "
                 "xs_loaded1 y_ready slots_filled ").split()
        s = {n: sem(n) for n in names}
        row_sem = [sem(f"max_rows_moved{a}") for a in range(2)]
        y_store = [sem(f"y_stored{a}") for a in range(2)]
        exp_loaded = [sem(f"expert{e}_in") for e in range(1, E)]

        block = ctx.enter_context(nc.Block())

        def score_at(m):
            u, r = divmod(m, 16)
            return u // KVH, u % KVH, r // TB, r % TB

        bank_use = {}
        uses = {6: 0, 7: 0}
        misc_use = {}
        for it in plan:
            if it[0] in ("gate", "up") and it[2] == 0:
                b_ = 6 if it[0] == "gate" else 7
            elif it[0] == "down" and it[2] == 0:
                b_ = 6 + it[1] % 2
            elif it[0] in ("max_rows", "heads_norm", "attn_T", "wo"):
                misc_use[it] = len(misc_use)
                continue
            else:
                continue
            bank_use[it[:2]] = (b_, uses[b_])
            uses[b_] += 1
        free_sem = {6: s["gate_free"], 7: s["up_free"]}
        pos = {it: n for n, it in enumerate(plan)}

        @block.sync
        def _(sp):
            sp.dma_start(x[:, 0:TB, :], x_in[:, 0:TB, :]).then_inc(x_in_s[0], 16)
            sp.dma_start(cst[:], const_in).then_inc(s["const_loaded"], 16)
            sp.dma_start(x[:, TB:NT, :], x_in[:, TB:NT, :]).then_inc(x_in_s[1], 16)
            sp.dma_start(wqkv, wqkv_in).then_inc(s["wqkv_loaded"], 16)
            sp.dma_start(wgu, wgu_in).then_inc(s["wgu_loaded"], 16)
            sp.dma_start(wdn, wdn_in).then_inc(s["wdn_loaded"], 16)
            sp.dma_start(wo, wo_in).then_inc(s["wo_loaded"], 16)
            for dst, src in ((win[:], win_in), (wout[:], wout_in), (router[:], router_in),
                             (bin_b[:], bin_in.partition_broadcast(P)), (bout_b[:], bout_in.partition_broadcast(P))):
                sp.dma_start(dst, src).then_inc(s["late_loaded"], 16)
            sp.dma_start(Wm[:, 0:EW], experts_in[0]).then_inc(s["expert0_loaded"], 16)

            sp.dma_start(xs_dram[0:TOK, :].rearrange("(p j) d -> p j d", p=P), x_in).then_inc(s["slots_filled"], 16)
            sp.dma_start(xs_dram[TOK:SLOTS, :].rearrange("(p j) d -> p j d", p=P), x_in[:, 0:MT - NT, :]).then_inc(s["slots_filled"], 16)

            for u in range(UNITS):
                b, g = divmod(u, KVH)
                sp.wait_ge(s["misc_free"], misc_use[("max_rows", u)] + 1)
                for part in range(SPLIT):
                    sp.dma_start(qs[KS + part:KS + part + 1, b, GR * g:GR * g + GR, :],
                                 mrow[GR * part:GR * part + GR, u % 2, :]).then_inc(row_sem[u % 2], 16)

            sp.wait_ge(s["wo_ready"], B * TB // 2)
            sp.wait_ge(s["x1_part"], NT // 2)
            for e in range(1, E):
                sp.dma_start(Wm[:, e * EW:(e + 1) * EW], experts_in[e]).then_inc(exp_loaded[e - 1], 16)

            sp.wait_ge(s["scattered"], 16 * NT)
            for i in range(MT):
                if i >= 2:
                    sp.wait_ge(s["xs_T"], i - 1)
                sp.dma_start(xs[:, i % 2, :], xs_dram[P * i:P * i + P, :]).then_inc(s[f"xs_loaded{i % 2}"], 16)
                if i >= 2:
                    sp.wait_ge(s["y_ready"], i - 1)
                    sp.dma_start(ys_dram[P * (i - 2):P * (i - 1), :], ysb[:, i % 2, :]).then_inc(y_store[i % 2], 16)
            for i in range(MT - 2, MT):
                sp.wait_ge(s["y_ready"], i + 1)
                sp.dma_start(ys_dram[P * i:P * i + P, :], ysb[:, i % 2, :]).then_inc(y_store[i % 2], 16)
            for b in range(B):
                sp.wait_ge(s["out_ready"], b + 1)
                sp.dma_start(out[:, TB * b:TB * b + TB, :], x[:, TB * b:TB * b + TB, :]).then_inc(s[f"out_stored{b}"], 16)
            for b in range(B):
                sp.wait_ge(s[f"out_stored{b}"], 16)

        @block.gpsimd
        def _(pool):
            nc.gpsimd.memset(vaug[:, :, :, HD:VW], 0.0).then_inc(s["vone"], 1)
            pool.wait_ge(s["vone"], 1)
            nc.gpsimd.memset(vaug[:, :, :, HD:HD + 1], 1.0).then_inc(s["vone"], 1)
            pool.wait_ge(s["vone"], 2)
            nc.gpsimd.memset(ks[KS:P, :, :, :], 1.0).then_inc(s["vone"], 1)
            pool.wait_ge(s["slots"], 1)
            pool.wait_ge(s["slots_filled"], 32)
            for j in range(NT):
                nc.gpsimd.indirect_dma_start(
                    out=xs_dram[:, :], out_offset=bass.IndirectOffsetOnAxis(ap=smi[:, j:j + 1], axis=0),
                    in_=xn[:, j, :], in_offset=None).then_inc(s["scattered"], 16)
            for e in range(E):
                pool.wait_ge(exp_loaded[e - 1] if e else s["expert0_loaded"], 16)
                pool.sem_inc(s["experts_here"], 1)
            for a in range(2):
                pool.wait_ge(y_store[a], 16 * ((MT + 1 - a) // 2))
            pool.wait_ge(s["qT_ready"], B * KD)
            for j in range(NT):
                nc.gpsimd.indirect_dma_start(
                    out=yg[:, j, :], out_offset=None,
                    in_=ys_dram[:, :], in_offset=bass.IndirectOffsetOnAxis(ap=smi[:, j:j + 1], axis=0),
                ).then_inc(s["gathered"], 16)

        @block.scalar
        def _(act):
            steps = [0]

            def chain(ins):
                steps[0] += 1
                ins.then_inc(s["act_step"], 1)
                act.wait_ge(s["act_step"], steps[0])

            def root(n):
                act.wait_ge(s["std_in"], n)
                nc.scalar.activation(st1[:, 1, :], st1[:, 0, :], ACT.Sqrt).then_inc(s["sqrt_done"], 1)

            def copy_xnT(n0):
                for b in range(B):
                    for k in range(KD):
                        n = n0 + KD * b + k
                        act.wait_ge(s["xnT_psum"], n + 1)
                        nc.scalar.activation(xnT[:, k, S * b:S * b + S], ps[:, KD * b + k, :], ACT.Copy).then_inc(s["xnT_ready"], 1)

            root(1)
            copy_xnT(0)
            for b in range(B):
                lo = 4 - 4 * b
                act.wait_ge(s["qkv_psum"], TB * (b + 1))
                for c in range(2):
                    nc.scalar.activation(qk[:, TB * b + 2 * c:TB * b + 2 * c + 2, :], ps[:, lo + 2 * c:lo + 2 * c + 2, 0:QKH * HD],
                                         ACT.Copy).then_inc(s["qk_copied"], 1)
                nc.scalar.activation(vaug[:, TB * b:TB * b + TB, :, 0:HD],
                                     ps[:, lo:lo + TB, QKH * HD:QKH * HD + KVH * HD].rearrange("p j (g c) -> p j g c", g=KVH),
                                     ACT.Copy).then_inc(s["v_copied"], 1)
            for b in range(B):
                for c in range(0, 10, 2):
                    n = 10 * b + c
                    act.wait_ge(s["stack_T"], n + 1)
                    dst = qs[0:KS, b, 2 * c:2 * c + 2, :] if c < 8 else ks[0:KS, b, 0:2, :]
                    nc.scalar.activation(dst, ps[0:KS, 4 + n % 4, :].bitcast(BF16).rearrange("p (h s) -> p h s", h=2),
                                         ACT.Copy).then_inc(s["stack_copied"], 1)

            for it in plan:
                kind = it[0]
                if kind == "prob":
                    _, n, hh = it
                    act.wait_ge(s["prob_ready"], 4 * n + hh + 1)
                    if n >= 2 and hh == 0:
                        act.wait_ge(s["values_done"], n - 1)
                    nc.scalar.activation(probs[:, n % 2, hh, :], ps[:, 2 + hh % 2, :], ACT.Exp,
                                         scale=float(HD) ** -0.5).then_inc(s["exp_done"], 1)
                elif kind == "gate" and it[2] == KD - 1:
                    c = it[1]
                    act.wait_ge(s["gate_ready"], c + 1)
                    if c >= 2:
                        act.wait_ge(s["gate_free"], bank_use[("gate", c - 2)][1] + 1)
                    nc.scalar.activation(tanh_g[:, c % 2, :], ps[:, 6, :], ACT.Tanh, scale=0.5).then_inc(s["tanh_done"], 1)
                elif kind == "down" and it[2] == NI - 1:
                    j = it[1]
                    act.wait_ge(s["down_ready"], j + 1)
                    act.wait_ge(s["up_free"], bank_use[("up", NI * (j // TB) + NI - 1)][1] + 1)
                    if j >= 2:
                        bk, n = bank_use[("down", j - 2)]
                        act.wait_ge(free_sem[bk], n + 1)
                    nc.scalar.activation(gated[:, j % 2, 0:D], ps[:, 6 + j % 2, 0:D], ACT.Tanh, scale=0.25).then_inc(s["down_tanh"], 1)
                elif kind == "max_rows":
                    u = it[1]
                    act.wait_ge(s["mrow_psum"], u + 1)
                    if u >= 2:
                        act.wait_ge(row_sem[u % 2], 48 * (u // 2))
                    nc.scalar.activation(mrow[0:SPLIT * GR, u % 2, :], miscb[0:SPLIT * GR, 0:S], ACT.Copy).then_inc(s["misc_free"], 1)
                elif kind == "attn_T":
                    n = KD * it[1] + it[2]
                    act.wait_ge(s["attn_T_ready"], n + 1)
                    if it[1] > 0:
                        act.wait_ge(s["wo_ready"], TB // 2 * it[1])
                    nc.scalar.activation(anT[:, it[2], :], misc, ACT.Copy).then_inc(s["misc_free"], 1)

            root(2)
            copy_xnT(B * KD)
            act.wait_ge(s["logits"], 1)
            nc.scalar.activation(small[:, 0, 0:NT * E], ps[:, 4, 0:NT * E], ACT.Exp, scale=-1.0).then_inc(s["logits_exp"], 1)
            for j in range(NT):
                act.wait_ge(s["rope_q"], j // TB + 1)
                nc.scalar.activation(gated[:, j % 2, 0:D], qkv1[:, j, D:2 * D], ACT.Square, accum_out=st1[:, 2, j:j + 1]).then_inc(s["act_step"], 1)
                steps[0] += 1
                act.wait_ge(s["act_step"], steps[0])
            nc.scalar.activation(st1[:, 4, :], st1[:, 2, :], ACT.Copy).then_inc(s["ksum_sq"], 1)
            act.wait_ge(s["norm_in"], 1)
            nc.scalar.activation(st1[:, 1, :], st1[:, 0, :], ACT.Sqrt).then_inc(s["norm_sqrt"], 1)

            def q_copy(n):
                b, k = divmod(n, KD)
                act.wait_ge(s["qT_psum"], n + 1)
                nc.scalar.activation(xnT[:, k, S * b:S * b + S], ps[:, 7, :], ACT.Copy).then_inc(s["qT_ready"], 1)

            def xsT_copy(i):
                act.wait_ge(s["xs_T"], i + 1)
                if i >= 2:
                    act.wait_ge(s["e_up"], i - 1)
                nc.scalar.activation(xsT[:, i % 2, :], ps[:, 4, 0:D], ACT.Copy).then_inc(s["xsT_ready"], 1)

            for n in range(B * KD):
                q_copy(n)
            xsT_copy(0)
            for i in range(MT):
                act.wait_ge(s["e_gate"], i + 1)
                if i >= 2:
                    act.wait_ge(s["e_h"], i - 1)
                nc.scalar.activation(tanh_g[:, i % 2, :], ps[:, i % 2, :], ACT.Tanh, scale=0.5).then_inc(s["e_tanh"], 1)
                if i + 1 < MT:
                    xsT_copy(i + 1)
                act.wait_ge(s["hm_T"], i + 1)
                if i >= 2:
                    act.wait_ge(s["e_down"], i - 1)
                nc.scalar.activation(hmT[:, i % 2, :], ps[:, 5, :], ACT.Copy).then_inc(s["hmT_ready"], 1)
            for b in range(B):
                act.wait_ge(s["w_ready"], TB * (b + 1))
                nc.scalar.activation(rope_t[:, 1024 * b:1024 * b + 1024], yg[:, TB * b:TB * b + TB, :].rearrange("p j n -> p (j n)"),
                                     ACT.Tanh, scale=0.25).then_inc(s["w_tanh"], 1)

        @block.vector
        def _(dve):
            steps = [0]

            def chain(ins):
                steps[0] += 1
                ins.then_inc(s["dve_step"], 1)
                dve.wait_ge(s["dve_step"], steps[0])

            def inv_root(name, value, signals):
                dve.wait_ge(s[name], value)
                v, y, t = st1[:, 0, :], st1[:, 3, :], st1[:, 4, :]
                chain(nc.vector.reciprocal(y, st1[:, 1, :]))
                chain(nc.vector.tensor_tensor(t, y, y, ALU.mult))
                chain(nc.vector.tensor_tensor(t, t, v, ALU.mult))
                chain(nc.vector.tensor_scalar(t, t, -0.5, 1.5, ALU.mult, ALU.add))
                nc.vector.tensor_tensor(y, y, t, ALU.mult).then_inc(s[signals], 1)

            def layer_norm(n, ready):
                for j in range(NT):
                    ready(j)
                    chain(nc.vector.bn_stats(bn[:, j, :], x[:, j, :]))
                    chain(nc.vector.bn_aggr(mv[:, j, :], bn[:, j, :]))
                nc.vector.tensor_scalar_add(st1[:, 0, :], mv[:, :, 1], LN_EPS).then_inc(s["std_in"], 1)
                inv_root("sqrt_done", n, "rstd_ready")
                dve.wait_ge(s["rstd_ready"], n)
                for j in range(NT):
                    nc.vector.tensor_scalar(xn[:, j, :], x[:, j, :], mv[:, j, 0:1], st1[:, 3, j:j + 1],
                                            ALU.subtract, ALU.mult).then_inc(s["rows_norm"], 1)

            dve.wait_ge(s["const_loaded"], 16)
            nc.vector.tensor_copy(identb[:], ident).then_inc(s["identb_ready"], 1)
            layer_norm(1, lambda j: dve.wait_ge(x_in_s[j // TB], 16))

            for b in range(B):
                rows = qk[:, TB * b:TB * b + TB, :].rearrange("p j (h c) -> p j h c", c=HD)
                rot = rows[:, :, :, 0:8]
                pair = rows[:, :, :, 0:8].rearrange("p j h (r two) -> p j h r two", two=2)
                ta = rot_a[:, 0:TB * QKH * 8].rearrange("p (j h c) -> p j h c", j=TB, h=QKH)
                tb = tanh_g[:].rearrange("p a b -> p (a b)")[:, 0:TB * QKH * 8].rearrange("p (j h c) -> p j h c", j=TB, h=QKH)
                tbp = tb.rearrange("p j h (r two) -> p j h r two", two=2)
                shape4 = [P, TB, QKH, 4]
                cosb = const("cos0").rearrange("p (j o c) -> p j o c", j=TB, o=1).to_broadcast([P, TB, QKH, 8])
                sine = const("sin0e").rearrange("p (j o c) -> p j o c", j=TB, o=1).to_broadcast(shape4)
                sino = const("sin0o").rearrange("p (j o c) -> p j o c", j=TB, o=1).to_broadcast(shape4)
                dve.wait_ge(s["qk_copied"], 2 * (b + 1))
                nc.vector.tensor_tensor(ta, rot, cosb, ALU.mult)
                nc.vector.tensor_tensor(tbp[:, :, :, :, 0], pair[:, :, :, :, 1], sine, ALU.mult)
                chain(nc.vector.tensor_tensor(tbp[:, :, :, :, 1], pair[:, :, :, :, 0], sino, ALU.mult))
                chain(nc.vector.tensor_tensor(rot, ta, tb, ALU.add))
                if b:
                    dve.wait_ge(s["stack_T"], 10 * b)
                heads = qk[:, TB * b:TB * b + TB, :].rearrange("p j (h c) -> p (j h) c", c=HD)
                st = stack
                st4 = stack.rearrange("p (j h) c -> p j h c", j=TB)
                res = rot_a[:, 0:TB * QKH * HD].rearrange("p (n c) -> p n c", c=HD)
                res4 = res.rearrange("p (j h) c -> p j h c", j=TB)

                def slot(a, h0=0, h1=QKH):
                    return st4[:, :, h0:h1, HD * a:HD * a + HD]

                chain(nc.vector.tensor_copy(st[:, :, 0:HD], heads))
                chain(nc.vector.tensor_tensor(res, heads, st[:, :, 0:HD], ALU.subtract))
                chain(nc.vector.tensor_copy(st[:, :, HD:2 * HD], res))
                nc.vector.tensor_tensor(slot(2, 0, HEADS), res4[:, :, 0:HEADS, :], slot(1, 0, HEADS), ALU.subtract)
                nc.vector.tensor_tensor(slot(3, HEADS), res4[:, :, HEADS:, :], slot(1, HEADS), ALU.subtract)
                nc.vector.tensor_copy(slot(3, 0, HEADS), slot(0, 0, HEADS))
                nc.vector.tensor_copy(slot(4, 0, HEADS), slot(0, 0, HEADS))
                nc.vector.tensor_copy(slot(5, 0, HEADS), slot(1, 0, HEADS))
                nc.vector.tensor_copy(slot(2, HEADS), slot(0, HEADS))
                nc.vector.tensor_copy(slot(5, HEADS), slot(0, HEADS))
                nc.vector.tensor_copy(slot(4, HEADS), slot(1, HEADS)).then_inc(s["parts_done"], 1)
                dve.wait_ge(s["parts_done"], b + 1)
                for c in range(1, 10, 2):
                    n = 10 * b + c
                    dve.wait_ge(s["stack_T"], n + 1)
                    dst = qs[0:KS, b, 2 * c:2 * c + 2, :] if c < 8 else ks[0:KS, b, 2:4, :]
                    nc.vector.tensor_copy(dst, ps[0:KS, 4 + n % 4, :].bitcast(BF16).rearrange("p (h s) -> p h s", h=2)
                                          ).then_inc(s["stack_copied2"], 1)

            for it in plan:
                kind = it[0]
                if kind == "score":
                    m = it[1]
                    b, g, hh, t = score_at(m)
                    dve.wait_ge(s["score_ready"], m + 1)
                    if m % 16 == 0 and m:
                        dve.wait_ge(s["mparts_ready"], m // 16)
                    nc.vector.tensor_reduce(nmax[:, 4 * t + hh:4 * t + hh + 1], ps[:, m % 2, :], AX, ALU.max,
                                            negate=True).then_inc(s["max_done"], 1)
                elif kind == "max_parts":
                    u = it[1]
                    dve.wait_ge(s["max_done"], 16 * (u + 1))
                    if u:
                        dve.wait_ge(s["mrow_psum"], u)
                    v = nmax[:].rearrange("p (t h) -> p t h", t=TB)
                    r0 = nres[:, 0, :].rearrange("p (t h) -> p t h", t=TB)
                    chain(nc.vector.tensor_copy(mparts[:, :, 0, :], v))
                    chain(nc.vector.tensor_tensor(r0, v, mparts[:, :, 0, :], ALU.subtract))
                    chain(nc.vector.tensor_copy(mparts[:, :, 1, :], r0))
                    nc.vector.tensor_tensor(mparts[:, :, 2, :], r0, mparts[:, :, 1, :], ALU.subtract).then_inc(s["mparts_ready"], 1)
                elif kind == "up" and it[2] == KD - 1:
                    c = it[1]
                    b, i = divmod(c, NI)
                    dve.wait_ge(s["tanh_done"], c + 1)
                    if i < 2 and b:
                        dve.wait_ge(s["down_tanh"], TB * b)
                    nc.vector.scalar_tensor_tensor(gated[:, c % 2, :], tanh_g[:, c % 2, :], 1.0, ps[:, 6, :], ALU.add, ALU.mult
                                                   ).then_inc(s["gate_free"], 1)
                    dve.wait_ge(s["gate_free"], bank_use[("gate", c)][1] + 1)
                    dve.wait_ge(s["up_ready"], c + 1)
                    if b and i == 0:
                        dve.wait_ge(s["down_ready"], TB * b)
                    nc.vector.tensor_tensor(hT[:, i, :], gated[:, c % 2, :], ps[:, 7, :], ALU.mult).then_inc(s["up_free"], 1)
                    dve.wait_ge(s["up_free"], bank_use[("up", c)][1] + 1)
                elif kind == "down" and it[2] == NI - 1:
                    j = it[1]
                    dve.wait_ge(s["down_tanh"], j + 1)
                    bk, n = bank_use[("down", j)]
                    nc.vector.scalar_tensor_tensor(gx[:, j, :], gated[:, j % 2, 0:D], 1.0, ps[:, bk, 0:D], ALU.add, ALU.mult
                                                   ).then_inc(free_sem[bk], 1)
                elif kind == "heads_out":
                    u = it[1]
                    dve.wait_ge(s["values_done"], TB * (u + 1))
                    if u:
                        dve.wait_ge(s["heads_T"], u)
                    nc.vector.tensor_copy(oTs, ps[:, 4, :]).then_inc(s["heads_copied"], 1)
                elif kind == "heads_norm":
                    u = it[1]
                    b, g = divmod(u, KVH)
                    o4 = misc.rearrange("p (t h c) -> p t h c", t=TB, h=GR)
                    dve.wait_ge(s["heads_T"], u + 1)
                    r = rsum[:].rearrange("p (t h o) -> p t h o", t=TB, o=1)
                    chain(nc.vector.reciprocal(r, o4[:, :, :, HD:HD + 1]))
                    if g == 0 and b:
                        dve.wait_ge(s["attn_T_ready"], KD * b)
                    nc.vector.tensor_tensor(an[:, :, 64 * g:64 * g + 64].rearrange("p t (h c) -> p t h c", h=GR),
                                            o4[:, :, :, 0:HD], r.to_broadcast([P, TB, GR, HD]), ALU.mult).then_inc(s["misc_free"], 1)
                elif kind == "wo":
                    _, b, c = it
                    n = TB // 2 * b + c
                    j = TB * b + 2 * c
                    dve.wait_ge(s["wo_ready"], n + 1)
                    for a in (0, 1):
                        bk, k_ = bank_use[("down", j + a)]
                        dve.wait_ge(free_sem[bk], k_ + 1)
                    t = gx[:, j:j + 2, :].rearrange("p j n -> p (j n)")
                    xx = x[:, j:j + 2, :].rearrange("p j n -> p (j n)")
                    nc.vector.tensor_tensor(t, t, misc, ALU.mult).then_inc(s["misc_free"], 1)
                    dve.wait_ge(s["misc_free"], misc_use[it] + 1)
                    nc.vector.scalar_tensor_tensor(xx, t, 0.25, xx, ALU.mult, ALU.add).then_inc(s["x1_part"], 1)

            dve.wait_ge(s["x1_part"], NT // 2)
            layer_norm(2, lambda j: None)

            lg = small[:, 0, 0:NT * E]
            l3 = lg.rearrange("p (j e) -> p j e", j=NT)
            oh = small[:, 1, 0:NT * E]
            oh3 = oh.rearrange("p (j e) -> p j e", j=NT)
            desc = const("desc").rearrange("p (o e) -> p o e", o=1).to_broadcast([P, NT, E])
            maxp = st1[:, 5, :]
            maxp3 = maxp.rearrange("p (j o) -> p j o", o=1)
            t8 = nres[:, 0, 0:NT]
            t83 = t8.rearrange("p (j o) -> p j o", o=1)
            dve.wait_ge(s["logits_exp"], 1)
            chain(nc.vector.memset(small[:, 1, 64:72], 0.0))
            chain(nc.vector.tensor_scalar_add(lg, lg, 1.0))
            chain(nc.vector.reciprocal(lg, lg))
            chain(nc.vector.tensor_reduce(maxp3, l3, AX, ALU.max))
            chain(nc.vector.tensor_tensor(l3, l3, maxp3.to_broadcast([P, NT, E]), ALU.is_ge))
            chain(nc.vector.tensor_tensor(l3, l3, desc, ALU.mult))
            chain(nc.vector.tensor_reduce(t83, l3, AX, ALU.max))
            nc.vector.tensor_tensor(oh3, desc, t83.to_broadcast([P, NT, E]), ALU.is_equal).then_inc(s["onehot"], 1)
            cnt = small[:, 2, 0:72]
            tot = small[:, 2, 64:72]
            dve.wait_ge(s["counts"], 1)
            chain(nc.vector.tensor_copy(cnt, ps[:, 4, 128:200]))
            big = lg.rearrange("p (e k) -> p e k", e=E)
            tiles = nres[:, 0, 0:8]
            base = nres[:, 0, 8:16]
            end = nres[:, 1, 0:8]
            chain(nc.vector.tensor_tensor(big, tot.rearrange("p (e o) -> p e o", o=1).to_broadcast([P, E, NT]),
                                          const("full").rearrange("p (o k) -> p o k", o=1).to_broadcast([P, E, NT]), ALU.is_gt))
            chain(nc.vector.tensor_reduce(tiles.rearrange("p (e o) -> p e o", o=1), big, AX, ALU.add))
            chain(nc.vector.tensor_tensor(big, const("lower").rearrange("p (e k) -> p e k", e=E),
                                          tiles.rearrange("p (o k) -> p o k", o=1).to_broadcast([P, E, E]), ALU.mult))
            chain(nc.vector.tensor_reduce(base.rearrange("p (e o) -> p e o", o=1), big, AX, ALU.add))
            nc.vector.tensor_tensor(end, base, tiles, ALU.add)
            chain(nc.vector.tensor_scalar_mul(base, base, float(P)))
            c3 = cnt[:, 0:64].rearrange("p (j e) -> p j e", j=NT)
            chain(nc.vector.tensor_tensor(l3, c3, base.rearrange("p (o e) -> p o e", o=1).to_broadcast([P, NT, E]), ALU.add))
            chain(nc.vector.tensor_tensor(l3, l3, oh3, ALU.mult))
            t8b = rsum[:, 0:NT]
            chain(nc.vector.tensor_reduce(t8b.rearrange("p (j o) -> p j o", o=1), l3, AX, ALU.add))
            nc.vector.tensor_copy(smi[:], t8b).then_inc(s["slots"], 1)
            te = tanh_g[:, 0, 0:MT * E].rearrange("p (i e) -> p i e", i=MT)
            tr = tanh_g[:, 0, 256:256 + MT]
            chain(nc.vector.tensor_tensor(te, const("tile_id").rearrange("p (i o) -> p i o", o=1).to_broadcast([P, MT, E]),
                                          end.rearrange("p (o e) -> p o e", o=1).to_broadcast([P, MT, E]), ALU.is_ge))
            chain(nc.vector.tensor_reduce(tr.rearrange("p (i o) -> p i o", o=1), te, AX, ALU.add))
            nc.vector.tensor_scalar_min(tile_e[:], tr, float(E - 1)).then_inc(s["tile_experts"], 1)

            dve.wait_ge(s["late_loaded"], 80)
            for j in range(NT):
                p0 = (0, 2, 5)[j % 3]
                dve.wait_ge(s["qkv1_psum"], j + 1)
                nc.vector.tensor_tensor(qkv1[:, j, :], ps[:, p0:p0 + 2, :].rearrange("p a n -> p (a n)")[:, 0:3 * D], bin_b[:], ALU.add
                                        ).then_inc(s["qkv1_ready"], 1)
            dve.wait_ge(s["qkv1_ready"], NT)
            for b in range(B):
                r2 = qkv1[:, TB * b:TB * b + TB, 0:2 * D].rearrange("p j (q n) -> p j q n", q=2)
                rot = r2[:, :, :, 0:ROT]
                pair = rot.rearrange("p j q (r two) -> p j q r two", two=2)
                n_ = TB * 2 * ROT
                ta = rope_t[:, 0:n_].rearrange("p (j q n) -> p j q n", j=TB, q=2)
                tb = rope_t[:, n_:2 * n_].rearrange("p (j q n) -> p j q n", j=TB, q=2)
                tbp = tb.rearrange("p j q (r two) -> p j q r two", two=2)
                half = [P, TB, 2, ROT // 2]
                cosb = const("cos1").rearrange("p (j o n) -> p j o n", j=TB, o=1).to_broadcast([P, TB, 2, ROT])
                sine = const("sin1e").rearrange("p (j o n) -> p j o n", j=TB, o=1).to_broadcast(half)
                sino = const("sin1o").rearrange("p (j o n) -> p j o n", j=TB, o=1).to_broadcast(half)
                if b:
                    dve.wait_ge(s["rope_q"], b)
                nc.vector.tensor_tensor(ta, rot, cosb, ALU.mult)
                nc.vector.tensor_tensor(tbp[:, :, :, :, 0], pair[:, :, :, :, 1], sine, ALU.mult)
                chain(nc.vector.tensor_tensor(tbp[:, :, :, :, 1], pair[:, :, :, :, 0], sino, ALU.mult))
                nc.vector.tensor_tensor(rot, ta, tb, ALU.add).then_inc(s["rope_q"], 1)
            dve.wait_ge(s["rope_q"], B)
            nc.vector.tensor_tensor(kv, qkv1[:, :, D:2 * D], qkv1[:, :, 2 * D:3 * D], ALU.mult).then_inc(s["kv_ready"], 1)
            dve.wait_ge(s["ksum_sq"], 1)
            nc.vector.tensor_scalar_max(st1[:, 0, :], st1[:, 4, :], 1e-24).then_inc(s["norm_in"], 1)
            inv_root("norm_sqrt", 1, "norm_ready")
            dve.wait_ge(s["acol_psum"], 1)
            nc.vector.tensor_copy(acol[:], ps[:, 7, 0:4]).then_inc(s["acol_ready"], 1)
            dve.wait_ge(s["acol_ready"], 1)
            for b in range(B):
                for k in range(KD):
                    nc.vector.tensor_scalar_mul(wsc[:, b, k, :], wout[:, k, :], acol[:, KD * b + k:KD * b + k + 1]).then_inc(s["wsc_ready"], 1)

            for i in range(MT):
                dve.wait_ge(s["e_tanh"], i + 1)
                if i >= 2:
                    dve.wait_ge(s["hm_T"], i - 1)
                nc.vector.scalar_tensor_tensor(gated[:, i % 2, :], tanh_g[:, i % 2, :], 1.0, ps[:, i % 2, :], ALU.add, ALU.mult
                                               ).then_inc(s["e_gated"], 1)
                dve.wait_ge(s["e_gated"], i + 1)
                dve.wait_ge(s["e_up"], i + 1)
                nc.vector.tensor_tensor(hm[:, i % 2, :], gated[:, i % 2, :], ps[:, 2 + i % 2, :], ALU.mult).then_inc(s["e_h"], 1)
                if i >= 1:
                    k = i - 1
                    dve.wait_ge(s["e_down"], k + 1)
                    if k >= 2:
                        dve.wait_ge(y_store[k % 2], 16 * (k // 2))
                    nc.vector.tensor_copy(ysb[:, k % 2, :], ps[:, 6, 0:D]).then_inc(s["y_ready"], 1)
                if 3 <= i < 3 + NT // 2:
                    c = i - 3
                    two = lambda a: a[:, 2 * c:2 * c + 2, :]
                    p7 = ps[:, 7, :].rearrange("p (j n) -> p j n", j=2)
                    dve.wait_ge(s["branch_psum"], c + 1)
                    nc.vector.tensor_tensor(two(gx), p7, bout_b[:].rearrange("p (o n) -> p o n", o=1).to_broadcast([P, 2, D]), ALU.add
                                            ).then_inc(s["branch_free"], 1)
                    dve.wait_ge(s["branch_free"], c + 1)
                    nc.vector.tensor_tensor(two(gx), two(gx), two(xn), ALU.add).then_inc(s["branch_ready"], 1)
            k = MT - 1
            dve.wait_ge(s["e_down"], k + 1)
            dve.wait_ge(y_store[k % 2], 16 * (k // 2))
            nc.vector.tensor_copy(ysb[:, k % 2, :], ps[:, 6, 0:D]).then_inc(s["y_ready"], 1)

            for b in range(B):
                for j in range(TB * b, TB * b + TB):
                    dve.wait_ge(s["gathered"], 16 * NT)
                    nc.vector.tensor_scalar_mul(yg[:, j, :], yg[:, j, :], maxp[:, j:j + 1]).then_inc(s["w_ready"], 1)
            for b in range(B):
                flat = lambda a: a[:, TB * b:TB * b + TB, :].rearrange("p j n -> p (j n)")
                dve.wait_ge(s["w_tanh"], b + 1)
                chain(nc.vector.scalar_tensor_tensor(flat(yg), rope_t[:, 1024 * b:1024 * b + 1024], 1.0, flat(yg), ALU.add, ALU.mult))
                chain(nc.vector.tensor_tensor(flat(yg), flat(yg), flat(gx), ALU.mult))
                nc.vector.scalar_tensor_tensor(flat(x), flat(yg), 0.25, flat(x), ALU.mult, ALU.add).then_inc(s["out_ready"], 1)

        @block.tensor
        def _(pe):
            def transpose_rows(n0, rows0):
                for b in range(B):
                    pe.wait_ge(s["rows_norm"], rows0 + TB * (b + 1))
                    for k in range(KD):
                        for t in range(TB):
                            last = nc.tensor.transpose(ps[:, KD * b + k, P * t:P * t + P], xn[:, TB * b + t, P * k:P * k + P], ident)
                        last.then_inc(s["xnT_psum"], 1)

            pe.wait_ge(s["const_loaded"], 16)
            pe.wait_ge(s["identb_ready"], 1)
            transpose_rows(0, 0)

            pe.wait_ge(s["wqkv_loaded"], 16)
            for b in range(B):
                pe.wait_ge(s["xnT_ready"], KD * (b + 1) if b == 0 else B * KD)
                for t in range(TB):
                    j = TB * b + t
                    for k in range(KD):
                        last = nc.tensor.matmul(ps[:, 4 - 4 * b + t, 0:384], xnT[:, k, P * j:P * j + P], wqkv[:, k, :],
                                                start=k == 0, stop=k == KD - 1)
                    last.then_inc(s["qkv_psum"], 1)

            for b in range(B):
                pe.wait_ge(s["parts_done"], b + 1)
                for c in range(10):
                    n = 10 * b + c
                    if n < 4:
                        pe.wait_ge(s["qk_copied"], 2)
                        pe.wait_ge(s["v_copied"], 1)
                    elif n % 2 == 0:
                        pe.wait_ge(s["stack_copied"], (n - 4) // 2 + 1)
                    else:
                        pe.wait_ge(s["stack_copied2"], (n - 4) // 2 + 1)
                    for a in range(2):
                        for t in range(TB):
                            at_ = (a * TB + t) * P
                            last = nc.tensor.transpose(ps[:, 4 + n % 4, :].bitcast(BF16)[0:KS, at_:at_ + P],
                                                       stack[:, QKH * t + 2 * c + a, :], identb[:])
                    last.then_inc(s["stack_T"], 1)
            pe.wait_ge(s["stack_copied"], 10)
            pe.wait_ge(s["stack_copied2"], 10)
            pe.wait_ge(s["v_copied"], B)
            pe.wait_ge(s["qk_copied"], 2 * B)
            pe.wait_ge(s["vone"], 3)
            pe.wait_ge(s["wgu_loaded"], 16)
            pe.wait_ge(s["wdn_loaded"], 16)
            pe.wait_ge(s["wo_loaded"], 16)

            def misc_bank(it):
                if misc_use[it]:
                    pe.wait_ge(s["misc_free"], misc_use[it])

            for it in plan:
                kind = it[0]
                if kind == "score":
                    m = it[1]
                    b, g, hh, t = score_at(m)
                    if m >= 2:
                        pe.wait_ge(s["max_done"], m - 1)
                    nc.tensor.matmul(ps[:, m % 2, :], qs[0:KS, b, GR * g + hh, P * t:P * t + P], ks[0:KS, b, g, :],
                                     start=True, stop=True).then_inc(s["score_ready"], 1)
                elif kind == "max_rows":
                    u = it[1]
                    pe.wait_ge(s["mparts_ready"], u + 1)
                    misc_bank(it)
                    for t in range(TB):
                        last = nc.tensor.transpose(miscb[0:SPLIT * GR, P * t:P * t + P],
                                                   mparts[:, t, :, :].rearrange("p a h -> p (a h)"), identb[:])
                    last.then_inc(s["mrow_psum"], 1)
                elif kind == "prob":
                    _, n, hh = it
                    u, t = divmod(n, TB)
                    b, g = divmod(u, KVH)
                    if t == 0 and hh == 0:
                        pe.wait_ge(row_sem[u % 2], 48 * (u // 2 + 1))
                    q = GR * n + hh
                    if q >= 2:
                        pe.wait_ge(s["exp_done"], q - 1)
                    nc.tensor.matmul(ps[:, 2 + hh % 2, :], ks[0:KM, b, g, P * t:P * t + P], qs[0:KM, b, GR * g + hh, :],
                                     start=True, stop=True).then_inc(s["prob_ready"], 1)
                elif kind == "values":
                    n = it[1]
                    u, t = divmod(n, TB)
                    b, g = divmod(u, KVH)
                    pe.wait_ge(s["exp_done"], GR * (n + 1))
                    if t == 0 and u:
                        pe.wait_ge(s["heads_copied"], u)
                    for hh in range(GR):
                        last = nc.tensor.matmul(ps[VW * hh:VW * hh + VW, 4, :], vaug[:, TB * b + t, g, :], probs[:, n % 2, hh, :],
                                                start=t == 0, stop=t == TB - 1)
                    last.then_inc(s["values_done"], 1)
                elif kind == "heads_norm":
                    u = it[1]
                    pe.wait_ge(s["heads_copied"], u + 1)
                    misc_bank(it)
                    for t in range(TB):
                        last = nc.tensor.transpose(misc[:, P * t:P * t + P], oTs[:, P * t:P * t + P], ident)
                    last.then_inc(s["heads_T"], 1)
                elif kind == "attn_T":
                    _, b, k = it
                    pe.wait_ge(s["misc_free"], misc_use[("heads_norm", KVH * b + KVH - 1)] + 1)
                    misc_bank(it)
                    for t in range(TB):
                        last = nc.tensor.transpose(misc[:, P * t:P * t + P], an[:, t, P * k:P * k + P], ident)
                    last.then_inc(s["attn_T_ready"], 1)
                elif kind == "wo":
                    _, b, c = it
                    pe.wait_ge(s["misc_free"], misc_use[("attn_T", b, KD - 1)] + 1)
                    misc_bank(it)
                    for a in range(2):
                        for k in range(KD):
                            at_ = P * (2 * c + a)
                            last = nc.tensor.matmul(misc[:, D * a:D * a + D], anT[:, k, at_:at_ + P], wo[:, k, :],
                                                    start=k == 0, stop=k == KD - 1)
                    last.then_inc(s["wo_ready"], 1)
                elif kind in ("gate", "up"):
                    _, c, k = it
                    b, i = divmod(c, NI)
                    bk, n = bank_use[(kind, c)]
                    if k == 0 and n:
                        pe.wait_ge(free_sem[bk], n)
                    col = P * i + (INTER if kind == "up" else 0)
                    ins = nc.tensor.matmul(ps[:, bk, :], wgu[:, k, col:col + P], xnT[:, k, S * b:S * b + S], start=k == 0, stop=k == KD - 1)
                    if k == KD - 1:
                        ins.then_inc(s[kind + "_ready"], 1)
                elif kind == "down":
                    _, j, i = it
                    bk, n = bank_use[("down", j)]
                    if i == 0:
                        pe.wait_ge(free_sem[bk], n)
                        if j % TB == 0:
                            pe.wait_ge(s["up_free"], bank_use[("up", NI * (j // TB) + NI - 1)][1] + 1)
                    ins = nc.tensor.matmul(ps[:, bk, 0:D], hT[:, i, P * (j % TB):P * (j % TB) + P], wdn[:, i, :],
                                           start=i == 0, stop=i == NI - 1)
                    if i == NI - 1:
                        ins.then_inc(s["down_ready"], 1)

            transpose_rows(B * KD, NT)
            pe.wait_ge(s["late_loaded"], 80)
            pe.wait_ge(s["xnT_ready"], 2 * B * KD)
            pe.wait_ge(s["misc_free"], len(misc_use))
            for bk in (6, 7):
                pe.wait_ge(free_sem[bk], uses[bk])
            pe.wait_ge(s["heads_copied"], UNITS)
            for j in range(NT):
                for k in range(KD):
                    last = nc.tensor.matmul(ps[:, 4, E * j:E * j + E], xnT[:, k, P * j:P * j + P], router[:, k, :],
                                            start=k == 0, stop=k == KD - 1)
            last.then_inc(s["logits"], 1)

            def qkv(j):
                p0 = (0, 2, 5)[j % 3]
                if j >= 3:
                    pe.wait_ge(s["qkv1_ready"], j - 2)
                for lo, hi, bk in ((0, 512, p0), (512, 768, p0 + 1)):
                    for k in range(KD):
                        last = nc.tensor.matmul(ps[:, bk, 0:hi - lo], xnT[:, k, P * j:P * j + P], win[:, k, lo:hi],
                                                start=k == 0, stop=k == KD - 1)
                last.then_inc(s["qkv1_psum"], 1)

            for j in range(3):
                qkv(j)
            pe.wait_ge(s["onehot"], 1)
            nc.tensor.matmul(ps[:, 4, 128:200], const("before"), small[:, 1, 0:72], start=True, stop=False)
            for j in range(NT):
                last = nc.tensor.matmul(ps[:, 4, 128 + E * (j + 1):200].rearrange("p (a e) -> p a e", e=E), const("ones"),
                                        small[:, 1, E * j:E * j + E].rearrange("p (o e) -> p o e", o=1).to_broadcast([P, NT - j, E]),
                                        start=False, stop=j == NT - 1)
            last.then_inc(s["counts"], 1)
            for j in range(3, NT):
                qkv(j)
            pe.wait_ge(s["qkv1_ready"], NT)
            for b in range(B):
                pe.wait_ge(s["rope_q"], b + 1)
                for k in range(KD):
                    n = KD * b + k
                    if n:
                        pe.wait_ge(s["qT_ready"], n)
                    for t in range(TB):
                        last = nc.tensor.transpose(ps[:, 7, P * t:P * t + P], qkv1[:, TB * b + t, P * k:P * k + P], ident)
                    last.then_inc(s["qT_psum"], 1)

            def rows_T(i):
                pe.wait_ge(s[f"xs_loaded{i % 2}"], 16 * (i // 2 + 1))
                if i:
                    pe.wait_ge(s["xsT_ready"], i)
                else:
                    pe.wait_ge(s["slots"], 1)
                for k in range(KD):
                    last = nc.tensor.transpose(ps[:, 4, P * k:P * k + P], xs[:, i % 2, P * k:P * k + P], ident)
                last.then_inc(s["xs_T"], 1)

            pe.wait_ge(s["tile_experts"], 1)
            rows_T(0)
            expert = None
            for i in range(MT + 1):
                if i < MT:
                    chosen = pe.value_load(tile_e[0:1, i:i + 1], min_val=0, max_val=E - 1)
                    pe.wait_ge(s["experts_here"], chosen + 1)
                    base = chosen * EW
                    pe.wait_ge(s["xsT_ready"], i + 1)
                    if i >= 2:
                        pe.wait_ge(s["e_gated"], i - 1)
                    for k in range(KD):
                        last = nc.tensor.matmul(ps[:, i % 2, :], xsT[:, i % 2, P * k:P * k + P], Wm[:, bass.ds(base + EI * k, EI)],
                                                start=k == 0, stop=k == KD - 1)
                    last.then_inc(s["e_gate"], 1)
                if i == 0:
                    pe.wait_ge(s["qT_ready"], B * KD)
                    pe.wait_ge(s["norm_ready"], 1)
                    for b in range(B):
                        for k in range(KD):
                            for t in range(TB):
                                j = TB * b + t
                                last = nc.tensor.matmul(ps[:, 7, KD * b + k:KD * b + k + 1], kv[:, j, P * k:P * k + P], st1[:, 3, j:j + 1],
                                                        start=t == 0, stop=t == TB - 1)
                    last.then_inc(s["acol_psum"], 1)
                if i >= 1:
                    pe.wait_ge(s["e_h"], i)
                    if i >= 2:
                        pe.wait_ge(s["hmT_ready"], i - 1)
                    for k in range(KE):
                        last = nc.tensor.transpose(ps[:, 5, P * k:P * k + P], hm[:, (i - 1) % 2, P * k:P * k + P], ident)
                    last.then_inc(s["hm_T"], 1)
                if i < MT:
                    if i >= 2:
                        pe.wait_ge(s["e_h"], i - 1)
                    for k in range(KD):
                        last = nc.tensor.matmul(ps[:, 2 + i % 2, :], xsT[:, i % 2, P * k:P * k + P], Wm[:, bass.ds(base + EI * (KD + k), EI)],
                                                start=k == 0, stop=k == KD - 1)
                    last.then_inc(s["e_up"], 1)
                if i + 1 < MT:
                    rows_T(i + 1)
                if i >= 1:
                    pe.wait_ge(s["hmT_ready"], i)
                    if i >= 2:
                        pe.wait_ge(s["y_ready"], i - 1)
                    for k in range(KE):
                        last = nc.tensor.matmul(ps[:, 6, 0:D], hmT[:, (i - 1) % 2, P * k:P * k + P],
                                                Wm[:, bass.ds(before + 2 * KD * EI + D * k, D)], start=k == 0, stop=k == KE - 1)
                    last.then_inc(s["e_down"], 1)
                if 2 <= i < 2 + NT // 2:
                    c = i - 2
                    if c == 0:
                        pe.wait_ge(s["wsc_ready"], B * KD)
                    else:
                        pe.wait_ge(s["branch_free"], c)
                    for a in range(2):
                        j = 2 * c + a
                        for k in range(KD):
                            last = nc.tensor.matmul(ps[:, 7, D * a:D * a + D], xnT[:, k, P * j:P * j + P], wsc[:, j // TB, k, :],
                                                    start=k == 0, stop=k == KD - 1)
                    last.then_inc(s["branch_psum"], 1)
                if i < MT:
                    before = base


def kernel(**inputs):
    import concourse.bacc as bacc
    from concourse.bass_utils import run_bass_kernel_spmd

    def deep(w):
        w = np.asarray(w)
        return np.ascontiguousarray(w.reshape(w.shape[0] // P, P, w.shape[1]).transpose(1, 0, 2))

    a = {k: np.asarray(v) for k, v in inputs.items()}
    g, u, d = a["L1_ffn_gate_w"], a["L1_ffn_up_w"], a["L1_ffn_down_w"]
    experts = np.stack([np.concatenate([deep(w[e]).reshape(P, -1) for w in (g, u, d)], axis=1) for e in range(E)])
    arrays = {
        "x": deep(a["L0_attn_hidden_states"].reshape(TOK, D)),
        "wqkv": deep(np.concatenate([a["L0_attn_Wq"], a["L0_attn_Wk"], a["L0_attn_Wv"]], axis=1)),
        "wo": deep(a["L0_attn_Wo"]),
        "wgu": deep(a["L0_ffn_w_gate_up"].T),
        "wdn": deep(a["L0_ffn_w_down"].T),
        "win": deep(a["L1_attn_W_in"].T),
        "b_in": a["L1_attn_b_in"],
        "wout": deep(a["L1_attn_W_out"].T),
        "b_out": a["L1_attn_b_out"],
        "router": deep(a["L1_ffn_router_w"]),
        "experts": experts,
        "const": constants(),
    }
    nc = bacc.Bacc("TRN2", target_bir_lowering=False, num_devices=1)
    args = [nc.dram_tensor(f"in_{n}", v.shape, mybir.dt.from_np(v.dtype), kind="ExternalInput").ap() for n, v in arrays.items()]
    out = nc.dram_tensor("out_x", (P, NT, D), F32, kind="ExternalOutput").ap()
    two_gated_blocks(nc, *args, out)
    r = run_bass_kernel_spmd(nc, [{f"in_{n}": v for n, v in arrays.items()}], core_ids=[0])
    y = r.results[0]["out_x"]
    return np.ascontiguousarray(y.transpose(1, 0, 2)).reshape(B, S, D)
```

```python
from contextlib import ExitStack

import numpy as np
import concourse.bass as bass
from concourse import mybir

ALU = mybir.AluOpType
ACT = mybir.ActivationFunctionType
F32 = mybir.dt.float32
BF16 = mybir.dt.bfloat16
I32 = mybir.dt.int32
AX = mybir.AxisListType.X

P = 128
B, S, D = 2, 512, 256
TOK = B * S
NT = TOK // P
TB = S // P
KD = D // P
HEADS, KVH, HD = 16, 4, 16
GR = HEADS // KVH
QKH = HEADS + KVH
INTER = 1024
NI = INTER // P
E, EI = 8, 512
KE = EI // P
EW = 2 * KD * EI + KE * D
MT = TOK // P + E - 1
SLOTS = MT * P
SPLIT = 3
NSTACK = 6
KS = NSTACK * HD
KM = KS + SPLIT
RW = D + 4
TOKEN_COL, PROB_COL = D, D + 1
XR = TOK // P
FIRST_EXPERTS = 3
SURE = TOK // P
VW = 32
LN_EPS = 1e-5
UNITS = B * KVH
STEPS = UNITS * TB
ROT = D // 2


def const_columns():
    widths = [("ident", P), ("before", P), ("ones", P), ("cos0", TB * 8), ("sin0e", TB * 4), ("sin0o", TB * 4),
              ("cos1", TB * ROT), ("sin1e", TB * ROT // 2), ("sin1o", TB * ROT // 2),
              ("desc", E), ("full", NT), ("lower", E * E), ("tile_id", MT), ("token", NT)]
    at, out = 0, {}
    for name, w in widths:
        out[name] = (at, w)
        at += w
    return out, at


def constants():
    cols, width = const_columns()
    c = np.zeros((P, width), np.float32)

    def put(name, a):
        lo, w = cols[name]
        c[:, lo:lo + w] = np.asarray(a, np.float32).reshape(-1, w) if np.asarray(a).size != w else np.ravel(a)

    def angles(dim):
        inv = (np.float32(1.0) / np.float32(10000.0) ** (np.arange(0, dim, 2, dtype=np.float32) / np.float32(dim)))
        pos = np.arange(S, dtype=np.float32)
        f = (pos[:, None] * inv[None, :]).astype(np.float32)
        return f.reshape(TB, P, dim // 2).transpose(1, 0, 2)

    p = np.arange(P)
    put("ident", np.eye(P))
    put("before", (p[:, None] < p[None, :]).astype(np.float32))
    put("ones", np.ones((P, P)))
    a = angles(HD // 2)
    put("cos0", np.repeat(np.cos(a), 2, axis=-1).reshape(P, -1))
    put("sin0e", -np.sin(a).reshape(P, -1))
    put("sin0o", np.sin(a).reshape(P, -1))
    a = angles(ROT)
    put("cos1", np.repeat(np.cos(a), 2, axis=-1).reshape(P, -1))
    put("sin1e", -np.sin(a).reshape(P, -1))
    put("sin1o", np.sin(a).reshape(P, -1))
    e = np.arange(E)
    put("desc", E - e)
    put("full", np.arange(NT) * P)
    put("lower", (e[None, :] < e[:, None]).astype(np.float32).ravel())
    put("tile_id", np.arange(MT))
    put("token", p[:, None] + P * np.arange(NT)[None, :])
    return c


def empty_row():
    r = np.zeros((P, RW), np.float32)
    r.view(np.int32)[:, TOKEN_COL] = TOK
    return r


SCORES_OF = ((0, 6), (6, 12), (12, 16), (16, 16))


def attention_plan():
    fill = []
    for b in range(B):
        for i in range(NI):
            fill += [("gate", b * NI + i, k) for k in range(KD)] + [("up", b * NI + i, k) for k in range(KD)]
        for j in range(TB):
            fill += [("down", b * TB + j, i) for i in range(NI)]
    cost = {"gate": 2, "up": 2, "down": 1}
    total = sum(cost[f[0]] for f in fill)
    spent = 0
    after = {}

    def due(step, h, *stages):
        after.setdefault((step, h), []).extend(stages)

    for u in range(UNITS - 1):
        due(4 * u + 4, 1, ("heads_out", u))
        due(4 * u + 5, 0, ("heads_norm", u))
    due(3, 3, ("slots", 1))
    for c, where in enumerate(((4, 1), (4, 3), (5, 3), (6, 1), (7, 0), (7, 2), (8, 1), (8, 3), (9, 3), (10, 1))):
        due(*where, ("stack_T", 1, c))
    for step, h, stage in ((17, 2, ("attn_T", 0, 0)), (18, 0, ("attn_T", 0, 1)), (18, 2, ("wo", 0, 0)), (19, 1, ("wo", 0, 1)),
                           (19, 2, ("norm_sums", 0)), (20, 0, ("norm_root", 0)), (20, 2, ("norm_apply", 0)),
                           (21, 2, ("rows_T", 0, 0)), (22, 0, ("rows_T", 0, 1)), (22, 2, ("logits", 0))):
        due(step, h, stage)
    last = B - 1
    due(STEPS - 4, 3, ("attn_T", last, 0))
    due(STEPS - 3, 3, ("wo_half", last))
    end = [("heads_out", UNITS - 1), ("qkv1", 0), ("heads_norm", UNITS - 1), ("qkv1", 1), ("attn_T", last, 1), ("wo", last, 0),
           ("wo", last, 1), ("norm_sums", last), ("norm_root", last), ("norm_apply", last), ("qkv1", 2), ("qkv1", 3),
           ("rope1", 0), ("rows_T", last, 0), ("rows_T", last, 1), ("logits", last)]

    plan = []

    def early(n):
        nonlocal spent
        for _ in range(n):
            f = fill.pop(0)
            spent += cost[f[0]]
            plan.append(f)

    early(2 * KD)
    plan += [("stack_T", 0, c) for c in (8, 0, 1, 9, 2, 3, 4, 5, 6, 7)]
    for m in range(16):
        plan.append(("score", m))
        if m % 2:
            early(1)
    plan += [("max_parts", 0)]
    early(1)
    plan += [("max_rows", 0)]
    early(3)
    start = spent

    def take(upto):
        nonlocal spent
        while fill and spent < upto:
            f = fill.pop(0)
            spent += cost[f[0]]
            plan.append(f)

    for n in range(STEPS):
        u, t = divmod(n, TB)
        budget = start + (total - start) * (n + 1) // STEPS
        share = (budget - spent + GR - 1) // GR
        scores = [("score", 16 * (u + 1) + m) for m in range(*SCORES_OF[t])] if u + 1 < UNITS else []
        for hh in range(GR):
            plan.append(("prob", n, hh))
            if hh == 1 and n > 0:
                plan.append(("values", n - 1))
            cut = -(-len(scores) // (GR - hh if t < 2 else max(2 - hh, 1)))
            plan += scores[:cut]
            scores = scores[cut:]
            if u + 1 < UNITS and t == 2 and hh == 1:
                plan.append(("max_parts", u + 1))
            take(min(budget, spent + share))
            plan += after.pop((n, hh), [])
        if u + 1 < UNITS and t == 2:
            plan.append(("max_rows", u + 1))
        take(budget)
    plan += [("values", STEPS - 1)] + end
    assert not after
    assert not fill
    return plan


def side_work(i):
    return {0: [("norm", 0)], 1: [("sum", 0)], 3: [("branch", 0)], 4: [("branch", 1)], 5: [("branch", 2)], 6: [("branch", 3)]}.get(i, [])


def two_gated_blocks(nc, x_in, wqkv_in, wo_in, wgu_in, wdn_in, win_in, bin_in, wout_in, bout_in,
                     router_in, experts_in, const_in, empty_in, out):
    cols, cwidth = const_columns()
    plan = attention_plan()
    early_c = cols["cos1"][0]

    xs_dram = nc.dram_tensor("slot_rows", (SLOTS, RW), F32, kind="Internal").ap()
    y_dram = nc.dram_tensor("expert_results", (TOK, D), F32, kind="Internal").ap()

    with ExitStack() as ctx:
        def sb(name, shape, dt=F32):
            return ctx.enter_context(nc.sbuf_tensor(name, shape, dt))

        def sem(name):
            return ctx.enter_context(nc.semaphore(name))

        x = sb("x", [P, NT, D])
        xn = sb("xn", [P, NT, RW])
        xnT = sb("xnT", [P, KD, TOK])
        gx = sb("gx", [P, NT, D])
        Wm = sb("experts", [P, E * EW])
        Sa = sb("shared", [P, 10240])
        win = sb("win", [P, KD, 3 * D])
        wl0 = sb("wl0", [P, 1280])
        wout = sb("wout", [P, KD, D])
        bin_b = sb("bin_b", [P, 3 * D])
        bout_b = sb("bout_b", [P, D])
        router = sb("router", [P, KD, E])
        cst = sb("cst", [P, cwidth])
        identb = sb("identb", [P, P], BF16)
        tanh_g = sb("tanh_g", [P, 2, 512])
        gated = sb("gated", [P, 2, 512])
        xs = sb("xs", [P, 3, RW])
        xsT = sb("xsT", [P, 2, D])
        bn = sb("bn", [P, NT, 6])
        mv = sb("mv", [P, NT, 2])
        st1 = sb("st1", [P, 6, NT])
        small = sb("small", [P, 3, 80])
        smi = sb("smi", [P, NT], I32)
        tile_e = sb("tile_e", [P, MT], I32)
        tiles_n = sb("tiles_n", [P, 1], I32)
        rsum = sb("rsum", [P, 16])
        nmax = sb("nmax", [P, 16])
        nres = sb("nres", [P, 2, 16])
        mparts = sb("mparts", [P, TB, SPLIT, GR], BF16)
        acol = sb("acol", [P, 4])

        def slot_row(i, lo=0, hi=RW):
            a = i % XR
            if a < 3:
                return xs[:, a, lo:hi]
            return win[:].rearrange("p k n -> p (k n)")[:, (a - 3) * RW + lo:(a - 3) * RW + hi]

        def const(name):
            lo, w = cols[name]
            return cst[:, lo:lo + w]

        def before_tile(level, shift=0):
            at_ = 14 * E * level + (4 - shift) * E
            return tanh_g[:, 1, at_:at_ + NT * E + E]

        onehot = before_tile(0, -1)
        ident = const("ident")
        wqkv = wl0[:, 0:768].rearrange("p (k n) -> p k n", k=KD)
        wo = wl0[:, 768:1280].rearrange("p (k n) -> p k n", k=KD)

        at = [0]

        def in_experts(words):
            at[0] += words
            assert at[0] <= E * EW
            return Wm[:, at[0] - words:at[0]]

        qs = in_experts(8192).bitcast(BF16).rearrange("p (b h s) -> p b h s", b=B, h=HEADS)
        ks = in_experts(2048).bitcast(BF16).rearrange("p (b h s) -> p b h s", b=B, h=KVH)
        hT = in_experts(NI * S).rearrange("p (i s) -> p i s", i=NI)
        qk = in_experts(NT * QKH * HD).rearrange("p (j n) -> p j n", j=NT)
        vaug = in_experts(NT * KVH * VW).rearrange("p (j g c) -> p j g c", j=NT, g=KVH)
        an = in_experts(TB * D).rearrange("p (t n) -> p t n", t=TB)
        anT = in_experts(KD * S).rearrange("p (k s) -> p k s", k=KD)
        oTs = xs[:].rearrange("p a n -> p (a n)")[:, 0:S]
        mrow = in_experts(512).bitcast(BF16).rearrange("p (a s) -> p a s", a=2)

        late_expert = at[0] // EW
        stack_words = in_experts(TB * QKH * KS // 2)
        stack = stack_words.bitcast(BF16).rearrange("p (n c) -> p n c", c=KS)
        probs = Sa[:, 0:4096].rearrange("p (a h s) -> p a h s", a=2, h=GR)
        wgu = Sa[:, 4096:8192].rearrange("p (k n) -> p k n", k=KD)
        wdn = Sa[:, 8192:10240].rearrange("p (i n) -> p i n", i=NI)
        rot_a = gx[:, 0:5, :].rearrange("p a b -> p (a b)")
        qkv1 = (stack_words[:, 0:TB * 3 * D].rearrange("p (j n) -> p j n", j=TB), Sa[:, 0:TB * 3 * D].rearrange("p (j n) -> p j n", j=TB))
        kv = Sa[:, 6144:8192].rearrange("p (j n) -> p j n", j=NT)
        rope_t = Sa[:, 8192:10240]
        yg = Sa[:, 0:2048].rearrange("p (j n) -> p j n", j=NT)
        yt = Sa[:, 2048:4096].rearrange("p (j n) -> p j n", j=NT)
        ya = Sa[:, 4096:6144].rearrange("p (j n) -> p j n", j=NT)
        hmT = Sa[:, 8192:9216].rearrange("p (a n) -> p a n", a=2)
        wsc = Sa[:, 9216:10240].rearrange("p (b k n) -> p b k n", b=B, k=KD)
        ysb = bin_b[:, 0:2 * D].rearrange("p (a n) -> p a n", a=2)
        squares = wl0[:, 1024:1280]
        hm = wl0[:, 0:1024].rearrange("p (a n) -> p a n", a=2)

        ps = ctx.enter_context(nc.psum_tensor("ps", [P, 8, 512], F32))
        misc = ps[:, 5, :]
        miscb = misc.bitcast(BF16)

        x_in_s = [sem(f"x_loaded{b}") for b in range(B)]
        names = ("acol_psum acol_ready act_step attn_T_ready branch_free branch_psum branch_ready const_loaded "
                 "cos1 counts down_ready down_tanh dve_step e_down e_gate e_gated e_h e_tanh e_up end_free exp_done "
                 "experts_here gate_free gate_ready heads_T heads_copied hmT_ready hm_T identb_ready ksum_sq "
                 "kv_ready late_loaded logits max_done misc_free mparts_ready mrow_psum norm_ready onehot "
                 "out_ready parts_done parts_in pool_step prob_ready product_ready qT_psum qT_ready qk_copied qkv1_psum "
                 "qkv1_ready qkv_psum results_stored rope_q rows_T rows_norm scattered score_ready slots "
                 "slots_copied slots_emptied stack_T stack_copied stack_copied2 std_ready tanh_done tile_experts "
                 "up_free up_ready v_copied values_done vone w_tanh wdn_loaded wgu_loaded wo_loaded wo_ready "
                 "wqkv_loaded wsc_ready x1_part xnT_psum xnT_ready xsT_ready xs_T y_ready ").split()
        s = {n: sem(n) for n in names}
        row_sem = [sem(f"max_rows_moved{a}") for a in range(2)]
        y_store = [sem(f"y_stored{a}") for a in range(2)]
        exp_loaded = [sem(f"expert{e}_in") for e in range(E)]
        x_sem = [sem(f"slot_rows_loaded{a}") for a in range(XR)]
        result_sem = [sem(f"results_loaded{q}") for q in range(NT // 2)]
        out_sem = [sem(f"out_stored{q}") for q in range(NT // 2)]

        block = ctx.enter_context(nc.Block())

        def score_at(m):
            u, r = divmod(m, 16)
            return u // KVH, u % KVH, r // TB, r % TB

        bank_use = {}
        uses = {6: 0, 7: 0}
        misc_use = {}
        end_bank = {("attn_T", B - 1, 1): 2, ("wo", B - 1, 0): 0, ("wo", B - 1, 1): 1, ("rows_T", B - 1, 0): 0, ("rows_T", B - 1, 1): 1,
                    ("logits", B - 1): 2}
        end_use = {it: n for n, it in enumerate(end_bank)}
        for it in plan:
            if it in end_bank:
                continue
            if it[0] in ("gate", "up") and it[2] == 0:
                b_ = 6 if it[0] == "gate" else 7
            elif it[0] == "down" and it[2] == 0:
                b_ = 6 + it[1] % 2
            elif it[0] in ("max_rows", "heads_norm", "attn_T", "wo", "rows_T", "logits") or it[:2] == ("stack_T", 1):
                misc_use[it] = len(misc_use)
                continue
            else:
                continue
            bank_use[it[:2]] = (b_, uses[b_])
            uses[b_] += 1
        def place(it):
            if it in end_bank:
                return ps[:, end_bank[it], :], s["end_free"], end_use[it] + 1
            return misc, s["misc_free"], misc_use[it] + 1

        def qkv1_bank(j):
            lo = 6 if j % 2 == 0 else 3
            return ps[:, lo:lo + 2, :]

        free_sem = {6: s["gate_free"], 7: s["up_free"]}
        stack_order = [it[2] for it in plan if it[:2] == ("stack_T", 0)]
        stack_bank = (4, 5, 2, 3)

        def stacked(b, c, n):
            src = ps[0:KS, stack_bank[n % 4] if b == 0 else 5, :].bitcast(BF16)
            dst = qs[0:KS, b, 2 * c:2 * c + 2, :] if c < 8 else ks[0:KS, b, 2 * c - 16:2 * c - 14, :]
            return src, dst

        def tiles_from(eng, n_tiles, i, tile, drain):
            if i == MT:
                drain(i)
                return
            with eng.If(n_tiles > i):
                tile(i)
                tiles_from(eng, n_tiles, i + 1, tile, drain)
            with eng.Else():
                drain(i)

        def prepare(b, stage, eng, ops, chain):
            rows = qk[:, TB * b:TB * b + TB, :].rearrange("p j (h c) -> p j h c", c=HD)
            heads = qk[:, TB * b:TB * b + TB, :].rearrange("p j (h c) -> p (j h) c", c=HD)
            rot = rows[:, :, :, 0:8]
            pair = rot.rearrange("p j h (r two) -> p j h r two", two=2)
            ta = rot_a[:, 0:TB * QKH * 8].rearrange("p (j h c) -> p j h c", j=TB, h=QKH)
            tb = rot_a[:, TB * QKH * 8:TB * QKH * 16].rearrange("p (j h c) -> p j h c", j=TB, h=QKH)
            tbp = tb.rearrange("p j h (r two) -> p j h r two", two=2)
            res = rot_a[:, 0:TB * QKH * HD].rearrange("p (n c) -> p n c", c=HD)
            res4 = res.rearrange("p (j h) c -> p j h c", j=TB)
            shape4 = [P, TB, QKH, 4]
            angle = lambda name, c, shape: const(name).rearrange("p (j o c) -> p j o c", j=TB, o=1).to_broadcast(shape)
            st4 = stack.rearrange("p (j h) c -> p j h c", j=TB)

            def slot(a, h0=0, h1=QKH):
                return st4[:, :, h0:h1, HD * a:HD * a + HD]

            if stage == 0:
                eng.wait_ge(s["qk_copied"], 2 * (b + 1))
                if b:
                    eng.wait_ge(s["parts_done"], b)
                    eng.wait_ge(s["const_loaded"], 16)
                ops.tensor_tensor(ta, rot, angle("cos0", 8, [P, TB, QKH, 8]), ALU.mult)
                ops.tensor_tensor(tbp[:, :, :, :, 0], pair[:, :, :, :, 1], angle("sin0e", 4, shape4), ALU.mult)
                chain(ops.tensor_tensor(tbp[:, :, :, :, 1], pair[:, :, :, :, 0], angle("sin0o", 4, shape4), ALU.mult))
                chain(ops.tensor_tensor(rot, ta, tb, ALU.add))
            elif stage == 1:
                if b:
                    eng.wait_ge(s["stack_T"], 10 * b)
                chain(ops.tensor_copy(slot(0), rows))
                chain(ops.tensor_tensor(res, heads, stack[:, :, 0:HD], ALU.subtract))
            elif stage == 2:
                ops.tensor_copy(slot(1), res4).then_inc(s["parts_in"], 1)
                eng.wait_ge(s["parts_in"], b + 1)
            else:
                ops.tensor_tensor(slot(2, 0, HEADS), res4[:, :, 0:HEADS, :], slot(1, 0, HEADS), ALU.subtract)
                ops.tensor_tensor(slot(3, HEADS), res4[:, :, HEADS:, :], slot(1, HEADS), ALU.subtract)
                ops.tensor_copy(slot(2, HEADS), slot(0, HEADS))
                ops.tensor_copy(slot(5, HEADS), slot(0, HEADS))
                ops.tensor_copy(slot(4, HEADS), slot(1, HEADS)).then_inc(s["parts_done"], 1)

        @block.sync
        def _(sp):
            sp.dma_start(x[:, 0:TB, :], x_in[:, 0:TB, :]).then_inc(x_in_s[0], 16)
            sp.dma_start(cst[:, 0:early_c], const_in[:, 0:early_c]).then_inc(s["const_loaded"], 16)
            sp.dma_start(wqkv, wqkv_in).then_inc(s["wqkv_loaded"], 16)
            sp.dma_start(x[:, TB:NT, :], x_in[:, TB:NT, :]).then_inc(x_in_s[1], 16)
            sp.dma_start(wgu, wgu_in).then_inc(s["wgu_loaded"], 16)
            sp.dma_start(wdn, wdn_in).then_inc(s["wdn_loaded"], 16)
            sp.dma_start(wo, wo_in).then_inc(s["wo_loaded"], 16)
            for dst, src in ((cst[:, early_c:cwidth], const_in[:, early_c:cwidth]), (router[:], router_in), (win[:], win_in), (wout[:], wout_in),
                             (bin_b[:], bin_in.partition_broadcast(P)), (bout_b[:], bout_in.partition_broadcast(P))):
                sp.dma_start(dst, src).then_inc(s["late_loaded"], 16)
            sp.dma_start(xs_dram.rearrange("(i p) d -> p i d", p=P),
                         empty_in.rearrange("p (o d) -> p o d", o=1).to_broadcast([P, MT, RW])).then_inc(s["slots_emptied"], 16)

            for u in range(UNITS):
                b, g = divmod(u, KVH)
                sp.wait_ge(s["misc_free"], misc_use[("max_rows", u)] + 1)
                for part in range(SPLIT):
                    sp.dma_start(qs[KS + part:KS + part + 1, b, GR * g:GR * g + GR, :],
                                 mrow[GR * part:GR * part + GR, u % 2, :]).then_inc(row_sem[u % 2], 16)

            def expert_here(e):
                sp.wait_ge(exp_loaded[e], 16)
                sp.sem_inc(s["experts_here"], 1)

            def load_rows(i):
                sp.dma_start(slot_row(i), xs_dram[P * i:P * i + P, :]).then_inc(x_sem[i % XR], 16)

            sp.wait_ge(s["wo_ready"], B * TB // 2)
            for e in range(E):
                if e == late_expert:
                    sp.wait_ge(s["qT_psum"], KD)
                    sp.wait_ge(s["ksum_sq"], 1)
                    sp.wait_ge(s["kv_ready"], 1)
                sp.dma_start(Wm[:, e * EW:(e + 1) * EW], experts_in[e]).then_inc(exp_loaded[e], 16)
                if e == FIRST_EXPERTS - 1:
                    sp.wait_ge(s["scattered"], 16 * NT)
                    sp.wait_ge(s["qkv1_psum"], NT)
                    for i in range(XR):
                        load_rows(i)
                    for a in range(FIRST_EXPERTS):
                        expert_here(a)
            for e in range(FIRST_EXPERTS, E):
                expert_here(e)

            def reload_rows(i):
                if i + XR < MT:
                    sp.wait_ge(s["xs_T"], i + 1)
                    sp.wait_ge(y_store[i % 2], 16 * (i // 2 + 1))
                    load_rows(i + XR)

            for i in range(SURE):
                reload_rows(i)
            sp.wait_ge(s["tile_experts"], 1)
            n_tiles = sp.value_load(tiles_n[0:1, 0:1], min_val=SURE, max_val=MT)
            tiles_from(sp, n_tiles, SURE, reload_rows, lambda i: None)

            sp.wait_ge(s["results_stored"], 1)
            for q in range(NT // 2):
                sp.dma_start(yg[:, 2 * q:2 * q + 2, :], y_dram.rearrange("(j p) d -> p j d", p=P)[:, 2 * q:2 * q + 2, :]).then_inc(result_sem[q], 16)
            for q in range(NT // 2):
                sp.wait_ge(s["out_ready"], q + 1)
                sp.dma_start(out[:, 2 * q:2 * q + 2, :], x[:, 2 * q:2 * q + 2, :]).then_inc(out_sem[q], 16)
            for q in range(NT // 2):
                sp.wait_ge(out_sem[q], 16)

        @block.gpsimd
        def _(pool):
            nc.gpsimd.memset(vaug[:, :, :, HD:VW], 0.0).then_inc(s["vone"], 1)
            pool.wait_ge(s["vone"], 1)
            nc.gpsimd.memset(vaug[:, :, :, HD:HD + 1], 1.0).then_inc(s["vone"], 1)
            pool.wait_ge(s["vone"], 2)
            nc.gpsimd.memset(ks[KS:P, :, :, :], 1.0).then_inc(s["vone"], 1)
            pool.wait_ge(s["vone"], 3)
            steps = [0]

            def chain(ins):
                steps[0] += 1
                ins.then_inc(s["pool_step"], 1)
                pool.wait_ge(s["pool_step"], steps[0])

            for stage in range(4):
                prepare(1, stage, pool, nc.gpsimd, chain)

            def key_times_value(b):
                pool.wait_ge(s["rope_q"], b + 1)
                nc.gpsimd.tensor_tensor(kv[:, TB * b:TB * b + TB, :], qkv1[b][:, :, D:2 * D], qkv1[b][:, :, 2 * D:3 * D], ALU.mult
                                        ).then_inc(s["kv_ready"], 1)

            key_times_value(0)
            pool.wait_ge(s["slots"], 1)
            pool.wait_ge(s["slots_emptied"], 16)
            pool.wait_ge(s["rows_norm"], 2 * NT)
            for j in range(NT):
                nc.gpsimd.indirect_dma_start(
                    out=xs_dram[:, :], out_offset=bass.IndirectOffsetOnAxis(ap=smi[:, j:j + 1], axis=0),
                    in_=xn[:, j, :], in_offset=None).then_inc(s["scattered"], 16)
            key_times_value(1)
            def store(i):
                pool.wait_ge(s["y_ready"], i + 1)
                nc.gpsimd.indirect_dma_start(
                    out=y_dram[:, :], out_offset=bass.IndirectOffsetOnAxis(ap=slot_row(i, TOKEN_COL, TOKEN_COL + 1).bitcast(I32), axis=0),
                    in_=ysb[:, i % 2, :], in_offset=None, bounds_check=TOK - 1, oob_is_err=False).then_inc(y_store[i % 2], 16)

            def all_stored(n):
                for a in range(2):
                    pool.wait_ge(y_store[a], 16 * ((n + 1 - a) // 2))
                pool.sem_inc(s["results_stored"], 1)

            for i in range(SURE):
                store(i)
            n_tiles = pool.value_load(tiles_n[0:1, 0:1], min_val=SURE, max_val=MT)
            tiles_from(pool, n_tiles, SURE, store, all_stored)
            for q in range(NT // 2):
                pool.wait_ge(result_sem[q], 16)
                if q == 0:
                    pool.wait_ge(s["branch_ready"], NT // 2)
                nc.gpsimd.tensor_tensor(ya[:, 2 * q:2 * q + 2, :], yg[:, 2 * q:2 * q + 2, :], gx[:, 2 * q:2 * q + 2, :], ALU.mult
                                        ).then_inc(s["product_ready"], 1)

        @block.scalar
        def _(act):
            steps = [0]

            def chain(ins):
                steps[0] += 1
                ins.then_inc(s["act_step"], 1)
                act.wait_ge(s["act_step"], steps[0])

            def apply_norm(b):
                act.wait_ge(s["std_ready"], B + b + 1)
                for j in range(TB * b, TB * b + TB):
                    nc.scalar.activation(xn[:, j, 0:D], x[:, j, :], ACT.Identity, scale=st1[:, 4, j:j + 1], bias=st1[:, 5, j:j + 1]
                                         ).then_inc(s["rows_norm"], 1)

            def copy_xnT(b):
                for k in range(KD):
                    act.wait_ge(s["xnT_psum"], KD * b + k + 1)
                    nc.scalar.activation(xnT[:, k, S * b:S * b + S], ps[:, KD * b + k, :], ACT.Copy).then_inc(s["xnT_ready"], 1)

            copy_xnT(0)
            copy_xnT(1)
            for b in range(B):
                lo = 4 - 4 * b
                act.wait_ge(s["qkv_psum"], TB * (b + 1))
                for c in range(2):
                    nc.scalar.activation(qk[:, TB * b + 2 * c:TB * b + 2 * c + 2, :], ps[:, lo + 2 * c:lo + 2 * c + 2, 0:QKH * HD],
                                         ACT.Copy).then_inc(s["qk_copied"], 1)
                nc.scalar.activation(vaug[:, TB * b:TB * b + TB, :, 0:HD],
                                     ps[:, lo:lo + TB, QKH * HD:QKH * HD + KVH * HD].rearrange("p j (g c) -> p j g c", g=KVH),
                                     ACT.Copy).then_inc(s["v_copied"], 1)
            def slot_copies(b):
                act.wait_ge(s["parts_in"], b + 1)
                st4 = stack.rearrange("p (j h) c -> p j h c", j=TB)
                for to, of in ((3, 0), (4, 0), (5, 1)):
                    nc.scalar.activation(st4[:, :, 0:HEADS, HD * to:HD * to + HD], st4[:, :, 0:HEADS, HD * of:HD * of + HD], ACT.Copy
                                         ).then_inc(s["slots_copied"], 1)

            def key_squares(b):
                for j in range(TB * b, TB * b + TB):
                    act.wait_ge(s["rope_q"], b + 1)
                    chain(nc.scalar.activation(squares, qkv1[b][:, j % TB, D:2 * D], ACT.Square, accum_out=st1[:, 2, j:j + 1]))
                nc.scalar.activation(st1[:, 3, TB * b:TB * b + TB], st1[:, 2, TB * b:TB * b + TB], ACT.Copy).then_inc(s["ksum_sq"], 1)

            slot_copies(0)
            for it in plan:
                kind = it[0]
                if kind == "prob":
                    _, n, hh = it
                    act.wait_ge(s["prob_ready"], 4 * n + hh + 1)
                    if n >= 2 and hh == 0:
                        act.wait_ge(s["values_done"], n - 1)
                    nc.scalar.activation(probs[:, n % 2, hh, :], ps[:, 2 + hh % 2, :], ACT.Exp,
                                         scale=float(HD) ** -0.5).then_inc(s["exp_done"], 1)
                elif kind == "slots":
                    slot_copies(1)
                elif kind == "stack_T":
                    _, b, c = it
                    n = stack_order.index(c) if b == 0 else 10 + c
                    if b or n % 2 == 0:
                        src, dst = stacked(b, c, n)
                        act.wait_ge(s["stack_T"], n + 1)
                        nc.scalar.activation(dst, src.rearrange("p (h s) -> p h s", h=2), ACT.Copy
                                             ).then_inc(s["misc_free" if b else "stack_copied"], 1)
                elif kind == "norm_apply" and it[1] < B - 1:
                    apply_norm(it[1])
                elif kind == "rows_T":
                    _, b, k = it
                    bank, read, _ = place(it)
                    act.wait_ge(s["rows_T"], KD * b + k + 1)
                    nc.scalar.activation(xnT[:, k, S * b:S * b + S], bank, ACT.Copy).then_inc(read, 1)
                elif kind == "logits":
                    b = it[1]
                    bank, read, _ = place(it)
                    act.wait_ge(s["logits"], b + 1)
                    nc.scalar.activation(small[:, 0, 32 * b:32 * b + 32], bank[:, 0:32], ACT.Exp, scale=-1.0).then_inc(read, 1)
                elif kind == "gate" and it[2] == KD - 1:
                    c = it[1]
                    act.wait_ge(s["gate_ready"], c + 1)
                    if c >= 2:
                        act.wait_ge(s["gate_free"], bank_use[("gate", c - 2)][1] + 1)
                    nc.scalar.activation(tanh_g[:, c % 2, :], ps[:, 6, :], ACT.Tanh, scale=0.5).then_inc(s["tanh_done"], 1)
                elif kind == "down" and it[2] == NI - 1:
                    j = it[1]
                    act.wait_ge(s["down_ready"], j + 1)
                    act.wait_ge(s["up_free"], bank_use[("up", NI * (j // TB) + NI - 1)][1] + 1)
                    if j >= 2:
                        bk, n = bank_use[("down", j - 2)]
                        act.wait_ge(free_sem[bk], n + 1)
                    nc.scalar.activation(gated[:, j % 2, 0:D], ps[:, 6 + j % 2, 0:D], ACT.Tanh, scale=0.25).then_inc(s["down_tanh"], 1)
                elif kind == "max_rows":
                    u = it[1]
                    act.wait_ge(s["mrow_psum"], u + 1)
                    if u >= 2:
                        act.wait_ge(row_sem[u % 2], 48 * (u // 2))
                    nc.scalar.activation(mrow[0:SPLIT * GR, u % 2, :], miscb[0:SPLIT * GR, 0:S], ACT.Copy).then_inc(s["misc_free"], 1)
                elif kind == "attn_T":
                    n = KD * it[1] + it[2]
                    act.wait_ge(s["attn_T_ready"], n + 1)
                    if it[1] > 0:
                        act.wait_ge(s["wo_ready"], TB // 2 * it[1])
                    bank, read, _ = place(it)
                    nc.scalar.activation(anT[:, it[2], :], bank, ACT.Copy).then_inc(read, 1)

            def q_copy(n):
                b, k = divmod(n, KD)
                act.wait_ge(s["qT_psum"], n + 1)
                nc.scalar.activation(xnT[:, k, S * b:S * b + S], ps[:, 7, :], ACT.Copy).then_inc(s["qT_ready"], 1)

            def xsT_copy(i):
                act.wait_ge(s["xs_T"], i + 1)
                if i >= 2:
                    act.wait_ge(s["e_up"], i - 1)
                nc.scalar.activation(xsT[:, i % 2, :], ps[:, 4, 0:D], ACT.Copy).then_inc(s["xsT_ready"], 1)

            def hmT_copy(i):
                act.wait_ge(s["hm_T"], i + 1)
                if i >= 2:
                    act.wait_ge(s["e_down"], i - 1)
                nc.scalar.activation(hmT[:, i % 2, :], ps[:, 5, :], ACT.Copy).then_inc(s["hmT_ready"], 1)

            def tile(i):
                act.wait_ge(s["e_gate"], i + 1)
                if i >= 2:
                    act.wait_ge(s["e_h"], i - 1)
                nc.scalar.activation(tanh_g[:, i % 2, :], ps[:, i % 2, :], ACT.Tanh, scale=0.5).then_inc(s["e_tanh"], 1)
                if i:
                    hmT_copy(i - 1)
                if i + 1 < MT:
                    xsT_copy(i + 1)

            key_squares(0)
            for n in range(B * KD):
                q_copy(n)
            xsT_copy(0)
            key_squares(1)
            for i in range(SURE):
                tile(i)
            n_tiles = act.value_load(tiles_n[0:1, 0:1], min_val=SURE, max_val=MT)
            tiles_from(act, n_tiles, SURE, tile, lambda i: hmT_copy(i - 1))
            for q in range(NT // 2):
                act.wait_ge(result_sem[q], 16)
                nc.scalar.activation(yt[:, 2 * q:2 * q + 2, :], yg[:, 2 * q:2 * q + 2, :], ACT.Tanh, scale=0.25).then_inc(s["w_tanh"], 1)

        @block.vector
        def _(dve):
            steps = [0]

            def chain(ins):
                steps[0] += 1
                ins.then_inc(s["dve_step"], 1)
                dve.wait_ge(s["dve_step"], steps[0])

            def inverse_root(j0, j1):
                v, y, t = st1[:, 0, j0:j1], st1[:, 4, j0:j1], st1[:, 1, j0:j1]
                chain(nc.vector.tensor_scalar(t.bitcast(I32), v.bitcast(I32), 1, None, ALU.logical_shift_right))
                chain(nc.vector.tensor_scalar(y.bitcast(I32), t.bitcast(I32), -1.0, float(0x5F3759DF), ALU.mult, ALU.add))
                for _ in range(3):
                    chain(nc.vector.tensor_tensor(t, y, y, ALU.mult))
                    chain(nc.vector.scalar_tensor_tensor(t, t, -0.5, v, ALU.mult, ALU.mult))
                    chain(nc.vector.scalar_tensor_tensor(y, t, 1.5, y, ALU.add, ALU.mult))

            def norm_sums(b):
                j0, j1 = TB * b, TB * b + TB
                for j in range(j0, j1):
                    last = nc.vector.bn_stats(bn[:, j, :], x[:, j, :])
                chain(last)
                for j in range(j0, j1):
                    last = nc.vector.bn_aggr(mv[:, j, :], bn[:, j, :])
                chain(last)

            def norm_root(b):
                j0, j1 = TB * b, TB * b + TB
                chain(nc.vector.tensor_scalar_add(st1[:, 0, j0:j1], mv[:, j0:j1, 1], LN_EPS))
                inverse_root(j0, j1)
                nc.vector.scalar_tensor_tensor(st1[:, 5, j0:j1], mv[:, j0:j1, 0], -1.0, st1[:, 4, j0:j1], ALU.mult, ALU.mult
                                               ).then_inc(s["std_ready"], 1)

            def apply_norm(layer, b):
                dve.wait_ge(s["std_ready"], B * layer + b + 1)
                for j in range(TB * b, TB * b + TB):
                    nc.vector.tensor_scalar(xn[:, j, 0:D], x[:, j, :], st1[:, 4, j:j + 1], st1[:, 5, j:j + 1], ALU.mult, ALU.add
                                            ).then_inc(s["rows_norm"], 1)

            for b in range(B):
                dve.wait_ge(x_in_s[b], 16)
                norm_sums(b)
                norm_root(b)
                apply_norm(0, b)
            dve.wait_ge(s["const_loaded"], 16)
            nc.vector.tensor_copy(identb[:], ident).then_inc(s["identb_ready"], 1)

            def qkv1_bias(j):
                dve.wait_ge(s["qkv1_psum"], j + 1)
                if j == 0:
                    dve.wait_ge(s["stack_T"], 10 * B)
                nc.vector.tensor_tensor(qkv1[j // TB][:, j % TB, :], qkv1_bank(j).rearrange("p a n -> p (a n)")[:, 0:3 * D], bin_b[:], ALU.add
                                        ).then_inc(s["qkv1_ready"], 1)

            def rope1(b):
                r2 = qkv1[b][:, :, 0:2 * D].rearrange("p j (q n) -> p j q n", q=2)
                rot = r2[:, :, :, 0:ROT]
                pair = rot.rearrange("p j q (r two) -> p j q r two", two=2)
                n_ = TB * 2 * ROT
                ta = rope_t[:, 0:n_].rearrange("p (j q n) -> p j q n", j=TB, q=2)
                tb = rope_t[:, n_:2 * n_].rearrange("p (j q n) -> p j q n", j=TB, q=2)
                tbp = tb.rearrange("p j q (r two) -> p j q r two", two=2)
                half = [P, TB, 2, ROT // 2]
                angle = lambda name, shape: const(name).rearrange("p (j o n) -> p j o n", j=TB, o=1).to_broadcast(shape)
                if b:
                    dve.wait_ge(s["rope_q"], b)
                dve.wait_ge(s["qkv1_ready"], TB * (b + 1))
                nc.vector.tensor_tensor(ta, rot, angle("cos1", [P, TB, 2, ROT]), ALU.mult)
                nc.vector.tensor_tensor(tbp[:, :, :, :, 0], pair[:, :, :, :, 1], angle("sin1e", half), ALU.mult)
                chain(nc.vector.tensor_tensor(tbp[:, :, :, :, 1], pair[:, :, :, :, 0], angle("sin1o", half), ALU.mult))
                nc.vector.tensor_tensor(rot, ta, tb, ALU.add).then_inc(s["rope_q"], 1)

            for stage in range(4):
                prepare(0, stage, dve, nc.vector, chain)

            for it in plan:
                kind = it[0]
                if kind == "score":
                    m = it[1]
                    b, g, hh, t = score_at(m)
                    dve.wait_ge(s["score_ready"], m + 1)
                    if m % 16 == 0 and m:
                        dve.wait_ge(s["mparts_ready"], m // 16)
                    nc.vector.tensor_reduce(nmax[:, 4 * t + hh:4 * t + hh + 1], ps[:, m % 2, :], AX, ALU.max,
                                            negate=True).then_inc(s["max_done"], 1)
                elif kind == "stack_T" and it[1] == 0:
                    n = stack_order.index(it[2])
                    if n % 2:
                        src, dst = stacked(0, it[2], n)
                        dve.wait_ge(s["stack_T"], n + 1)
                        nc.vector.tensor_copy(dst, src.rearrange("p (h s) -> p h s", h=2)).then_inc(s["stack_copied2"], 1)
                elif kind == "norm_sums":
                    dve.wait_ge(s["x1_part"], TB // 2 * (it[1] + 1))
                    norm_sums(it[1])
                elif kind == "norm_root":
                    norm_root(it[1])
                elif kind == "norm_apply" and it[1] == B - 1:
                    apply_norm(1, it[1])
                elif kind == "max_parts":
                    u = it[1]
                    dve.wait_ge(s["max_done"], 16 * (u + 1))
                    if u:
                        dve.wait_ge(s["mrow_psum"], u)
                    v = nmax[:].rearrange("p (t h) -> p t h", t=TB)
                    r0 = nres[:, 0, :].rearrange("p (t h) -> p t h", t=TB)
                    chain(nc.vector.tensor_copy(mparts[:, :, 0, :], v))
                    chain(nc.vector.tensor_tensor(r0, v, mparts[:, :, 0, :], ALU.subtract))
                    chain(nc.vector.tensor_copy(mparts[:, :, 1, :], r0))
                    nc.vector.tensor_tensor(mparts[:, :, 2, :], r0, mparts[:, :, 1, :], ALU.subtract).then_inc(s["mparts_ready"], 1)
                elif kind == "up" and it[2] == 0:
                    c = it[1]
                    b, i = divmod(c, NI)
                    dve.wait_ge(s["tanh_done"], c + 1)
                    if i < 2 and b:
                        dve.wait_ge(s["down_tanh"], TB * b)
                    nc.vector.scalar_tensor_tensor(gated[:, c % 2, :], tanh_g[:, c % 2, :], 1.0, ps[:, 6, :], ALU.add, ALU.mult
                                                   ).then_inc(s["gate_free"], 1)
                elif kind == "up" and it[2] == KD - 1:
                    c = it[1]
                    b, i = divmod(c, NI)
                    dve.wait_ge(s["gate_free"], bank_use[("gate", c)][1] + 1)
                    dve.wait_ge(s["up_ready"], c + 1)
                    if b and i == 0:
                        dve.wait_ge(s["down_ready"], TB * b)
                    nc.vector.tensor_tensor(hT[:, i, :], gated[:, c % 2, :], ps[:, 7, :], ALU.mult).then_inc(s["up_free"], 1)
                    dve.wait_ge(s["up_free"], bank_use[("up", c)][1] + 1)
                elif kind == "down" and it[2] == NI - 1:
                    j = it[1]
                    dve.wait_ge(s["down_tanh"], j + 1)
                    if j == 0:
                        dve.wait_ge(s["parts_done"], B)
                    bk, n = bank_use[("down", j)]
                    nc.vector.scalar_tensor_tensor(gx[:, j, :], gated[:, j % 2, 0:D], 1.0, ps[:, bk, 0:D], ALU.add, ALU.mult
                                                   ).then_inc(free_sem[bk], 1)
                elif kind == "heads_out":
                    u = it[1]
                    dve.wait_ge(s["values_done"], TB * (u + 1))
                    if u:
                        dve.wait_ge(s["heads_T"], u)
                    nc.vector.tensor_copy(oTs, ps[:, 4, :]).then_inc(s["heads_copied"], 1)
                elif kind == "heads_norm":
                    u = it[1]
                    b, g = divmod(u, KVH)
                    o4 = misc.rearrange("p (t h c) -> p t h c", t=TB, h=GR)
                    dve.wait_ge(s["heads_T"], u + 1)
                    r = rsum[:].rearrange("p (t h o) -> p t h o", t=TB, o=1)
                    chain(nc.vector.reciprocal(r, o4[:, :, :, HD:HD + 1]))
                    if g == 0 and b:
                        dve.wait_ge(s["attn_T_ready"], KD * b)
                    nc.vector.tensor_tensor(an[:, :, 64 * g:64 * g + 64].rearrange("p t (h c) -> p t h c", h=GR),
                                            o4[:, :, :, 0:HD], r.to_broadcast([P, TB, GR, HD]), ALU.mult).then_inc(s["misc_free"], 1)
                elif kind == "wo":
                    _, b, c = it
                    n = TB // 2 * b + c
                    j = TB * b + 2 * c
                    dve.wait_ge(s["wo_ready"], n + 1)
                    for a in (0, 1):
                        bk, k_ = bank_use[("down", j + a)]
                        dve.wait_ge(free_sem[bk], k_ + 1)
                    t = gx[:, j:j + 2, :].rearrange("p j n -> p (j n)")
                    xx = x[:, j:j + 2, :].rearrange("p j n -> p (j n)")
                    bank, read, value = place(it)
                    nc.vector.tensor_tensor(t, t, bank, ALU.mult).then_inc(read, 1)
                    dve.wait_ge(read, value)
                    nc.vector.scalar_tensor_tensor(xx, t, 0.25, xx, ALU.mult, ALU.add).then_inc(s["x1_part"], 1)
                elif kind == "qkv1":
                    qkv1_bias(it[1])
                elif kind == "rope1":
                    rope1(it[1])

            lg = small[:, 0, 0:NT * E]
            l3 = lg.rearrange("p (j e) -> p j e", j=NT)
            oh3 = onehot[:, 0:NT * E].rearrange("p (j e) -> p j e", j=NT)
            desc = const("desc").rearrange("p (o e) -> p o e", o=1).to_broadcast([P, NT, E])
            maxp3 = xn[:, :, PROB_COL:PROB_COL + 1]
            t8 = nres[:, 0, 0:NT]
            t83 = t8.rearrange("p (j o) -> p j o", o=1)
            dve.wait_ge(s["late_loaded"], 96)
            nc.vector.tensor_copy(xn[:, :, TOKEN_COL:TOKEN_COL + 1].bitcast(I32), const("token").rearrange("p (j o) -> p j o", o=1))
            nc.vector.memset(xn[:, :, PROB_COL + 1:RW], 0.0)
            chain(nc.vector.memset(tanh_g[:, 1, 0:14 * E * 4], 0.0))
            dve.wait_ge(*place(("logits", B - 1))[1:])
            chain(nc.vector.tensor_scalar_add(lg, lg, 1.0))
            chain(nc.vector.reciprocal(lg, lg))
            chain(nc.vector.tensor_reduce(maxp3, l3, AX, ALU.max))
            chain(nc.vector.tensor_tensor(l3, l3, maxp3.to_broadcast([P, NT, E]), ALU.is_ge))
            chain(nc.vector.tensor_tensor(l3, l3, desc, ALU.mult))
            chain(nc.vector.tensor_reduce(t83, l3, AX, ALU.max))
            chain(nc.vector.tensor_tensor(oh3, desc, t83.to_broadcast([P, NT, E]), ALU.is_equal))
            for level in range(2):
                chain(nc.vector.tensor_tensor(before_tile(level + 1), before_tile(level), before_tile(level, 1 << level), ALU.add))
            nc.vector.tensor_tensor(before_tile(3), before_tile(2), before_tile(2, 4), ALU.add).then_inc(s["onehot"], 1)
            qkv1_bias(TB)
            cnt = small[:, 2, 0:72]
            tot = small[:, 2, 64:72]
            dve.wait_ge(s["counts"], 1)
            chain(nc.vector.tensor_copy(cnt, ps[:, 5, 0:72]))
            big = lg.rearrange("p (e k) -> p e k", e=E)
            tiles = nres[:, 0, 0:8]
            base = nres[:, 0, 8:16]
            end = nres[:, 1, 0:8]
            chain(nc.vector.tensor_tensor(big, tot.rearrange("p (e o) -> p e o", o=1).to_broadcast([P, E, NT]),
                                          const("full").rearrange("p (o k) -> p o k", o=1).to_broadcast([P, E, NT]), ALU.is_gt))
            chain(nc.vector.tensor_reduce(tiles.rearrange("p (e o) -> p e o", o=1), big, AX, ALU.add))
            chain(nc.vector.tensor_tensor(big, const("lower").rearrange("p (e k) -> p e k", e=E),
                                          tiles.rearrange("p (o k) -> p o k", o=1).to_broadcast([P, E, E]), ALU.mult))
            chain(nc.vector.tensor_reduce(base.rearrange("p (e o) -> p e o", o=1), big, AX, ALU.add))
            nc.vector.tensor_tensor(end, base, tiles, ALU.add)
            chain(nc.vector.tensor_scalar_mul(base, base, float(P)))
            c3 = cnt[:, 0:64].rearrange("p (j e) -> p j e", j=NT)
            chain(nc.vector.tensor_tensor(l3, c3, base.rearrange("p (o e) -> p o e", o=1).to_broadcast([P, NT, E]), ALU.add))
            chain(nc.vector.tensor_tensor(l3, l3, oh3, ALU.mult))
            t8b = rsum[:, 0:NT]
            chain(nc.vector.tensor_reduce(t8b.rearrange("p (j o) -> p j o", o=1), l3, AX, ALU.add))
            nc.vector.tensor_copy(smi[:], t8b).then_inc(s["slots"], 1)
            te = tanh_g[:, 0, 0:MT * E].rearrange("p (i e) -> p i e", i=MT)
            tr = tanh_g[:, 0, 256:256 + MT]
            chain(nc.vector.tensor_tensor(te, const("tile_id").rearrange("p (i o) -> p i o", o=1).to_broadcast([P, MT, E]),
                                          end.rearrange("p (o e) -> p o e", o=1).to_broadcast([P, MT, E]), ALU.is_ge))
            chain(nc.vector.tensor_reduce(tr.rearrange("p (i o) -> p i o", o=1), te, AX, ALU.add))
            nc.vector.tensor_scalar_min(tile_e[:], tr, float(E - 1))
            nc.vector.tensor_copy(tiles_n[:], end[:, E - 1:E]).then_inc(s["tile_experts"], 1)

            for j in range(TB + 1, NT):
                qkv1_bias(j)
            rope1(1)

            def key_norms():
                dve.wait_ge(s["ksum_sq"], B)
                chain(nc.vector.tensor_scalar_max(st1[:, 0, :], st1[:, 3, :], 1e-24))
                inverse_root(0, NT)
                nc.vector.tensor_copy(st1[:, 2, :], st1[:, 4, :]).then_inc(s["norm_ready"], 1)

            def scaled_output():
                dve.wait_ge(s["acol_psum"], 1)
                nc.vector.tensor_copy(acol[:], ps[:, 7, 0:4]).then_inc(s["acol_ready"], 1)
                dve.wait_ge(s["acol_ready"], 1)
                for b in range(B):
                    for k in range(KD):
                        nc.vector.tensor_scalar_mul(wsc[:, b, k, :], wout[:, k, :], acol[:, KD * b + k:KD * b + k + 1]).then_inc(s["wsc_ready"], 1)

            def branch(c):
                two = lambda a: a[:, 2 * c:2 * c + 2, 0:D]
                p7 = ps[:, 7, :].rearrange("p (j n) -> p j n", j=2)
                dve.wait_ge(s["branch_psum"], c + 1)
                nc.vector.tensor_tensor(two(gx), p7, bout_b[:].rearrange("p (o n) -> p o n", o=1).to_broadcast([P, 2, D]), ALU.add
                                        ).then_inc(s["branch_free"], 1)
                dve.wait_ge(s["branch_free"], c + 1)
                nc.vector.tensor_tensor(two(gx), two(gx), two(xn), ALU.add).then_inc(s["branch_ready"], 1)

            def result(k):
                dve.wait_ge(s["e_down"], k + 1)
                if k >= 2:
                    dve.wait_ge(y_store[k % 2], 16 * (k // 2))
                nc.vector.tensor_scalar_mul(ysb[:, k % 2, :], ps[:, 6, 0:D], slot_row(k, PROB_COL, PROB_COL + 1)).then_inc(s["y_ready"], 1)

            def tile(i):
                dve.wait_ge(s["e_tanh"], i + 1)
                if i >= 2:
                    dve.wait_ge(s["hm_T"], i - 1)
                nc.vector.scalar_tensor_tensor(gated[:, i % 2, :], tanh_g[:, i % 2, :], 1.0, ps[:, i % 2, :], ALU.add, ALU.mult
                                               ).then_inc(s["e_gated"], 1)
                dve.wait_ge(s["e_gated"], i + 1)
                dve.wait_ge(s["e_up"], i + 1)
                nc.vector.tensor_tensor(hm[:, i % 2, :], gated[:, i % 2, :], ps[:, 2 + i % 2, :], ALU.mult).then_inc(s["e_h"], 1)
                if i:
                    result(i - 1)

            for i in range(SURE):
                tile(i)
                for kind, n in side_work(i):
                    if kind == "norm":
                        key_norms()
                    elif kind == "sum":
                        scaled_output()
                    elif kind == "branch":
                        branch(n)
            n_tiles = dve.value_load(tiles_n[0:1, 0:1], min_val=SURE, max_val=MT)
            tiles_from(dve, n_tiles, SURE, tile, lambda i: result(i - 1))

            for q in range(NT // 2):
                two = lambda a: a[:, 2 * q:2 * q + 2, :].rearrange("p j n -> p (j n)")
                dve.wait_ge(s["w_tanh"], q + 1)
                dve.wait_ge(s["product_ready"], q + 1)
                chain(nc.vector.scalar_tensor_tensor(two(ya), two(yt), 1.0, two(ya), ALU.add, ALU.mult))
                nc.vector.scalar_tensor_tensor(two(x), two(ya), 0.25, two(x), ALU.mult, ALU.add).then_inc(s["out_ready"], 1)

        @block.tensor
        def _(pe):
            pe.wait_ge(s["const_loaded"], 16)
            for b in range(B):
                pe.wait_ge(s["rows_norm"], TB * (b + 1))
                for k in range(KD):
                    for t in range(TB):
                        last = nc.tensor.transpose(ps[:, KD * b + k, P * t:P * t + P], xn[:, TB * b + t, P * k:P * k + P], ident)
                    last.then_inc(s["xnT_psum"], 1)
                pe.wait_ge(s["xnT_ready"], KD * (b + 1))
                if b == 0:
                    pe.wait_ge(s["wqkv_loaded"], 16)
                for t in range(TB):
                    j = TB * b + t
                    for k in range(KD):
                        last = nc.tensor.matmul(ps[:, 4 - 4 * b + t, 0:384], xnT[:, k, P * j:P * j + P], wqkv[:, k, :],
                                                start=k == 0, stop=k == KD - 1)
                    last.then_inc(s["qkv_psum"], 1)
            pe.wait_ge(s["qk_copied"], 2)
            pe.wait_ge(s["v_copied"], 1)
            pe.wait_ge(s["wgu_loaded"], 16)
            pe.wait_ge(s["identb_ready"], 1)

            def misc_bank(it):
                if misc_use.get(it):
                    pe.wait_ge(s["misc_free"], misc_use[it])

            def wo_product(b, c, a, k, bank):
                at_ = P * (2 * c + a)
                return nc.tensor.matmul(bank[:, D * a:D * a + D], anT[:, k, at_:at_ + P], wo[:, k, :],
                                        start=k == 0 and a == 0, stop=k == KD - 1 and a == 1)

            def qkv(j):
                bank = qkv1_bank(j)
                if j == 0:
                    pe.wait_ge(s["late_loaded"], 96)
                    for bk in (6, 7):
                        pe.wait_ge(free_sem[bk], uses[bk])
                elif j == 1:
                    pe.wait_ge(s["exp_done"], GR * STEPS)
                    pe.wait_ge(s["heads_copied"], UNITS)
                else:
                    pe.wait_ge(s["qkv1_ready"], j - 1)
                for lo, hi, a in ((0, 512, 0), (512, 768, 1)):
                    for k in range(KD):
                        last = nc.tensor.matmul(bank[:, a, 0:hi - lo], xnT[:, k, P * j:P * j + P], win[:, k, lo:hi],
                                                start=k == 0, stop=k == KD - 1)
                last.then_inc(s["qkv1_psum"], 1)

            for it in plan:
                kind = it[0]
                if kind == "stack_T":
                    _, b, c = it
                    n = stack_order.index(c) if b == 0 else 10 + c
                    if b == 0 and n == 0 or b and c == 0:
                        pe.wait_ge(s["parts_done"], b + 1)
                        pe.wait_ge(s["slots_copied"], 3 * (b + 1))
                    if b:
                        misc_bank(it)
                    elif n >= 4:
                        pe.wait_ge(s["stack_copied2" if n % 2 else "stack_copied"], (n - 4) // 2 + 1)
                    elif n == 2:
                        pe.wait_ge(s["qk_copied"], 2 * B)
                        pe.wait_ge(s["v_copied"], B)
                    src, _ = stacked(b, c, n)
                    for a in range(2):
                        for t in range(TB):
                            at_ = (a * TB + t) * P
                            last = nc.tensor.transpose(src[:, at_:at_ + P], stack[:, QKH * t + 2 * c + a, :], identb[:])
                    last.then_inc(s["stack_T"], 1)
                elif kind == "rows_T":
                    _, b, k = it
                    bank = place(it)[0]
                    pe.wait_ge(s["rows_norm"], NT + TB * (b + 1))
                    misc_bank(it)
                    for t in range(TB):
                        last = nc.tensor.transpose(bank[:, P * t:P * t + P], xn[:, TB * b + t, P * k:P * k + P], ident)
                    last.then_inc(s["rows_T"], 1)
                elif kind == "logits":
                    b = it[1]
                    if b == 0:
                        pe.wait_ge(s["late_loaded"], 96)
                    bank = place(it)[0]
                    if bank is misc:
                        pe.wait_ge(*place(("rows_T", b, KD - 1))[1:])
                    for k in range(KD):
                        pe.wait_ge(*place(("rows_T", b, k))[1:])
                        for t in range(TB):
                            j = TB * b + t
                            last = nc.tensor.matmul(bank[:, E * t:E * t + E], xnT[:, k, P * j:P * j + P], router[:, k, :],
                                                    start=k == 0 and t == 0, stop=k == KD - 1 and t == TB - 1)
                    last.then_inc(s["logits"], 1)
                elif kind == "score":
                    m = it[1]
                    b, g, hh, t = score_at(m)
                    if m == 0:
                        pe.wait_ge(s["stack_copied"], 5)
                        pe.wait_ge(s["stack_copied2"], 5)
                        pe.wait_ge(s["vone"], 3)
                    if m == 16 * KVH:
                        pe.wait_ge(s["misc_free"], misc_use[("stack_T", 1, 9)] + 1)
                    if m >= 2:
                        pe.wait_ge(s["max_done"], m - 1)
                    nc.tensor.matmul(ps[:, m % 2, :], qs[0:KS, b, GR * g + hh, P * t:P * t + P], ks[0:KS, b, g, :],
                                     start=True, stop=True).then_inc(s["score_ready"], 1)
                elif kind == "max_rows":
                    u = it[1]
                    pe.wait_ge(s["mparts_ready"], u + 1)
                    misc_bank(it)
                    for t in range(TB):
                        last = nc.tensor.transpose(miscb[0:SPLIT * GR, P * t:P * t + P],
                                                   mparts[:, t, :, :].rearrange("p a h -> p (a h)"), identb[:])
                    last.then_inc(s["mrow_psum"], 1)
                elif kind == "prob":
                    _, n, hh = it
                    u, t = divmod(n, TB)
                    b, g = divmod(u, KVH)
                    if t == 0 and hh == 0:
                        pe.wait_ge(row_sem[u % 2], 48 * (u // 2 + 1))
                    q = GR * n + hh
                    if q >= 2:
                        pe.wait_ge(s["exp_done"], q - 1)
                    nc.tensor.matmul(ps[:, 2 + hh % 2, :], ks[0:KM, b, g, P * t:P * t + P], qs[0:KM, b, GR * g + hh, :],
                                     start=True, stop=True).then_inc(s["prob_ready"], 1)
                elif kind == "values":
                    n = it[1]
                    u, t = divmod(n, TB)
                    b, g = divmod(u, KVH)
                    pe.wait_ge(s["exp_done"], GR * (n + 1))
                    if t == 0 and u:
                        pe.wait_ge(s["heads_copied"], u)
                    for hh in range(GR):
                        last = nc.tensor.matmul(ps[VW * hh:VW * hh + VW, 4, :], vaug[:, TB * b + t, g, :], probs[:, n % 2, hh, :],
                                                start=t == 0, stop=t == TB - 1)
                    last.then_inc(s["values_done"], 1)
                elif kind == "heads_norm":
                    u = it[1]
                    pe.wait_ge(s["heads_copied"], u + 1)
                    misc_bank(it)
                    for t in range(TB):
                        last = nc.tensor.transpose(misc[:, P * t:P * t + P], oTs[:, P * t:P * t + P], ident)
                    last.then_inc(s["heads_T"], 1)
                elif kind == "attn_T":
                    _, b, k = it
                    bank = place(it)[0]
                    g = (KVH // KD) * (k + 1) - 1 if b == B - 1 else KVH - 1
                    pe.wait_ge(s["misc_free"], misc_use[("heads_norm", KVH * b + g)] + 1)
                    misc_bank(it)
                    for t in range(TB):
                        last = nc.tensor.transpose(bank[:, P * t:P * t + P], an[:, t, P * k:P * k + P], ident)
                    last.then_inc(s["attn_T_ready"], 1)
                elif kind == "wo_half":
                    b = it[1]
                    pe.wait_ge(*place(("attn_T", b, 0))[1:])
                    pe.wait_ge(s["max_done"], 16 * UNITS)
                    for c in range(TB // 2):
                        for a in range(2):
                            wo_product(b, c, a, 0, place(("wo", b, c))[0])
                elif kind == "wo":
                    _, b, c = it
                    pe.wait_ge(*place(("attn_T", b, KD - 1))[1:])
                    pe.wait_ge(s["wo_loaded"], 16)
                    misc_bank(it)
                    for a in range(2):
                        for k in range(1 if b == B - 1 else 0, KD):
                            last = wo_product(b, c, a, k, place(it)[0])
                    last.then_inc(s["wo_ready"], 1)
                elif kind == "qkv1":
                    qkv(it[1])
                elif kind in ("gate", "up"):
                    _, c, k = it
                    b, i = divmod(c, NI)
                    bk, n = bank_use[(kind, c)]
                    if k == 0 and n:
                        pe.wait_ge(free_sem[bk], n)
                    col = P * i + (INTER if kind == "up" else 0)
                    ins = nc.tensor.matmul(ps[:, bk, :], wgu[:, k, col:col + P], xnT[:, k, S * b:S * b + S], start=k == 0, stop=k == KD - 1)
                    if k == KD - 1:
                        ins.then_inc(s[kind + "_ready"], 1)
                elif kind == "down":
                    _, j, i = it
                    bk, n = bank_use[("down", j)]
                    if i == 0:
                        pe.wait_ge(free_sem[bk], n)
                        if j == 0:
                            pe.wait_ge(s["wdn_loaded"], 16)
                    if j % TB == 0:
                        pe.wait_ge(s["up_free"], bank_use[("up", NI * (j // TB) + i)][1] + 1)
                    ins = nc.tensor.matmul(ps[:, bk, 0:D], hT[:, i, P * (j % TB):P * (j % TB) + P], wdn[:, i, :],
                                           start=i == 0, stop=i == NI - 1)
                    if i == NI - 1:
                        ins.then_inc(s["down_ready"], 1)

            qkv(TB)
            pe.wait_ge(s["onehot"], 1)
            nc.tensor.matmul(ps[:, 5, 0:NT * E + E], const("before"), onehot, start=True, stop=False)
            nc.tensor.matmul(ps[:, 5, 0:NT * E + E], const("ones"), before_tile(3), start=False, stop=True).then_inc(s["counts"], 1)
            for j in range(TB + 1, NT):
                qkv(j)

            def rows_T(i):
                pe.wait_ge(x_sem[i % XR], 16 * (i // XR + 1))
                if i:
                    pe.wait_ge(s["xsT_ready"], i)
                for k in range(KD):
                    last = nc.tensor.transpose(ps[:, 4, P * k:P * k + P], slot_row(i, P * k, P * k + P), ident)
                last.then_inc(s["xs_T"], 1)

            def hidden_T(i):
                pe.wait_ge(s["e_h"], i + 1)
                if i:
                    pe.wait_ge(s["hmT_ready"], i)
                for k in range(KE):
                    last = nc.tensor.transpose(ps[:, 5, P * k:P * k + P], hm[:, i % 2, P * k:P * k + P], ident)
                last.then_inc(s["hm_T"], 1)

            def down(i):
                pe.wait_ge(s["hmT_ready"], i + 1)
                if i:
                    pe.wait_ge(s["y_ready"], i)
                for k in range(KE):
                    last = nc.tensor.matmul(ps[:, 6, 0:D], hmT[:, i % 2, P * k:P * k + P],
                                            Wm[:, bass.ds(base[i] + 2 * KD * EI + D * k, D)], start=k == 0, stop=k == KE - 1)
                last.then_inc(s["e_down"], 1)

            base = {}

            def tile(i):
                chosen = pe.value_load(tile_e[0:1, i:i + 1], min_val=0, max_val=E - 1)
                pe.wait_ge(s["experts_here"], chosen + 1)
                base[i] = chosen * EW
                pe.wait_ge(s["xsT_ready"], i + 1)
                if i >= 2:
                    pe.wait_ge(s["e_gated"], i - 1)
                for k in range(KD):
                    last = nc.tensor.matmul(ps[:, i % 2, :], xsT[:, i % 2, P * k:P * k + P], Wm[:, bass.ds(base[i] + EI * k, EI)],
                                            start=k == 0, stop=k == KD - 1)
                last.then_inc(s["e_gate"], 1)
                if i:
                    hidden_T(i - 1)
                if i >= 2:
                    pe.wait_ge(s["e_h"], i - 1)
                for k in range(KD):
                    last = nc.tensor.matmul(ps[:, 2 + i % 2, :], xsT[:, i % 2, P * k:P * k + P], Wm[:, bass.ds(base[i] + EI * (KD + k), EI)],
                                            start=k == 0, stop=k == KD - 1)
                last.then_inc(s["e_up"], 1)
                if i + 1 < MT:
                    rows_T(i + 1)
                if i:
                    down(i - 1)

            def q_T(n):
                b, k = divmod(n, KD)
                pe.wait_ge(s["rope_q"], b + 1)
                if n:
                    pe.wait_ge(s["qT_ready"], n)
                for t in range(TB):
                    last = nc.tensor.transpose(ps[:, 7, P * t:P * t + P], qkv1[b][:, t, P * k:P * k + P], ident)
                last.then_inc(s["qT_psum"], 1)

            def token_sum():
                pe.wait_ge(s["qT_ready"], B * KD)
                pe.wait_ge(s["norm_ready"], 1)
                pe.wait_ge(s["kv_ready"], B)
                for b in range(B):
                    for k in range(KD):
                        for t in range(TB):
                            j = TB * b + t
                            last = nc.tensor.matmul(ps[:, 7, KD * b + k:KD * b + k + 1], kv[:, j, P * k:P * k + P], st1[:, 2, j:j + 1],
                                                    start=t == 0, stop=t == TB - 1)
                last.then_inc(s["acol_psum"], 1)

            def branch(c):
                if c == 0:
                    pe.wait_ge(s["wsc_ready"], B * KD)
                else:
                    pe.wait_ge(s["branch_free"], c)
                for a in range(2):
                    j = 2 * c + a
                    for k in range(KD):
                        last = nc.tensor.matmul(ps[:, 7, D * a:D * a + D], xnT[:, k, P * j:P * j + P], wsc[:, j // TB, k, :],
                                                start=k == 0, stop=k == KD - 1)
                last.then_inc(s["branch_psum"], 1)

            pe.wait_ge(s["tile_experts"], 1)
            pe.wait_ge(s["slots"], 1)
            pe.wait_ge(s["qkv1_ready"], NT)
            for n in range(B * KD):
                q_T(n)
            rows_T(0)
            for i in range(SURE):
                tile(i)
                for kind, n in side_work(i):
                    if kind == "sum":
                        token_sum()
                    elif kind == "branch":
                        branch(n)
            n_tiles = pe.value_load(tiles_n[0:1, 0:1], min_val=SURE, max_val=MT)

            def rest(i):
                hidden_T(i - 1)
                down(i - 1)

            tiles_from(pe, n_tiles, SURE, tile, rest)


def kernel(**inputs):
    import concourse.bacc as bacc
    from concourse.bass_utils import run_bass_kernel_spmd

    def deep(w):
        w = np.asarray(w)
        return np.ascontiguousarray(w.reshape(w.shape[0] // P, P, w.shape[1]).transpose(1, 0, 2))

    a = {k: np.asarray(v) for k, v in inputs.items()}
    g, u, d = a["L1_ffn_gate_w"], a["L1_ffn_up_w"], a["L1_ffn_down_w"]
    experts = np.stack([np.concatenate([deep(w[e]).reshape(P, -1) for w in (g, u, d)], axis=1) for e in range(E)])
    arrays = {
        "x": deep(a["L0_attn_hidden_states"].reshape(TOK, D)),
        "wqkv": deep(np.concatenate([a["L0_attn_Wq"], a["L0_attn_Wk"], a["L0_attn_Wv"]], axis=1)),
        "wo": deep(a["L0_attn_Wo"]),
        "wgu": deep(a["L0_ffn_w_gate_up"].T),
        "wdn": deep(a["L0_ffn_w_down"].T),
        "win": deep(a["L1_attn_W_in"].T),
        "b_in": a["L1_attn_b_in"],
        "wout": deep(a["L1_attn_W_out"].T),
        "b_out": a["L1_attn_b_out"],
        "router": deep(a["L1_ffn_router_w"]),
        "experts": experts,
        "const": constants(),
        "empty": empty_row(),
    }
    nc = bacc.Bacc("TRN2", target_bir_lowering=False, num_devices=1)
    args = [nc.dram_tensor(f"in_{n}", v.shape, mybir.dt.from_np(v.dtype), kind="ExternalInput").ap() for n, v in arrays.items()]
    out = nc.dram_tensor("out_x", (P, NT, D), F32, kind="ExternalOutput").ap()
    two_gated_blocks(nc, *args, out)
    r = run_bass_kernel_spmd(nc, [{f"in_{n}": v for n, v in arrays.items()}], core_ids=[0])
    y = r.results[0]["out_x"]
    return np.ascontiguousarray(y.transpose(1, 0, 2)).reshape(B, S, D)
```

```python
from contextlib import ExitStack

import numpy as np
import concourse.bass as bass
from concourse import mybir

ALU = mybir.AluOpType
ACT = mybir.ActivationFunctionType
F32 = mybir.dt.float32
BF16 = mybir.dt.bfloat16
F32R = mybir.dt.float32r
I32 = mybir.dt.int32
AX = mybir.AxisListType.X

P = 128
B, S, D = 2, 512, 256
TOK = B * S
NT = TOK // P
TB = S // P
KD = D // P
HEADS, KVH, HD = 16, 4, 16
GR = HEADS // KVH
QKH = HEADS + KVH
INTER = 1024
NI = INTER // P
E, EI = 8, 512
KE = EI // P
EW = 2 * KD * EI + KE * D
MT = TOK // P + E - 1
SLOTS = MT * P
SPLIT = 3
WARM_UP = 14
NSTACK = 6
KS = NSTACK * HD
KM = KS + SPLIT
RW = D + 4
TOKEN_COL, PROB_COL = D, D + 1
XR = TOK // P
FIRST_EXPERTS = 3
SURE = TOK // P
VW = 32
QK_AT = 8192 + 2048 + NI * S
WGU_AT = 4096
LN_EPS = 1e-5
UNITS = B * KVH
STEPS = UNITS * TB
ROT = D // 2


def const_columns():
    widths = [("ident", P), ("before", P), ("ones", P), ("cos0", TB * 8), ("sin0e", TB * 4), ("sin0o", TB * 4),
              ("cos1", TB * ROT), ("sin1e", TB * ROT // 2), ("sin1o", TB * ROT // 2),
              ("desc", E), ("full", NT), ("lower", E * E), ("tile_id", MT), ("token", NT)]
    at, out = 0, {}
    for name, w in widths:
        out[name] = (at, w)
        at += w
    return out, at


def constants():
    cols, width = const_columns()
    c = np.zeros((P, width), np.float32)

    def put(name, a):
        lo, w = cols[name]
        c[:, lo:lo + w] = np.asarray(a, np.float32).reshape(-1, w) if np.asarray(a).size != w else np.ravel(a)

    def angles(dim):
        inv = (np.float32(1.0) / np.float32(10000.0) ** (np.arange(0, dim, 2, dtype=np.float32) / np.float32(dim)))
        pos = np.arange(S, dtype=np.float32)
        f = (pos[:, None] * inv[None, :]).astype(np.float32)
        return f.reshape(TB, P, dim // 2).transpose(1, 0, 2)

    p = np.arange(P)
    put("ident", np.eye(P))
    put("before", (p[:, None] < p[None, :]).astype(np.float32))
    put("ones", np.ones((P, P)))
    a = angles(HD // 2)
    put("cos0", np.repeat(np.cos(a), 2, axis=-1).reshape(P, -1))
    put("sin0e", -np.sin(a).reshape(P, -1))
    put("sin0o", np.sin(a).reshape(P, -1))
    a = angles(ROT)
    put("cos1", np.repeat(np.cos(a), 2, axis=-1).reshape(P, -1))
    put("sin1e", -np.sin(a).reshape(P, -1))
    put("sin1o", np.sin(a).reshape(P, -1))
    e = np.arange(E)
    put("desc", E - e)
    put("full", np.arange(NT) * P)
    put("lower", (e[None, :] < e[:, None]).astype(np.float32).ravel())
    put("tile_id", np.arange(MT))
    put("token", p[:, None] + P * np.arange(NT)[None, :])
    return c


def empty_row():
    r = np.zeros((P, RW), np.float32)
    r.view(np.int32)[:, TOKEN_COL] = TOK
    return r


SCORES_OF = ((0, 4), (4, 9), (9, 13), (13, 16))


SLACK, AHEAD = 5, 16


class Clock:
    PE = {"prob": .22, "score": .22, "values": .9, "stack_T": .45, "gate": .65, "up": .65, "down": .43, "heads_norm": .43, "max_rows": .22,
          "attn_T": .43, "wo": 1.7, "wo_half": 1.7, "rows_T": .43, "logits": 3.4}
    AFTER = .07
    ROWS_MOVED = 3.7

    def __init__(self):
        self.now = {"pe": 0., "act": 0., "dve": 0.}
        self.done = {}

    def needs(self, item):
        kind = item[0]
        if kind == "prob":
            _, n, hh = item
            out = [("exp", GR * n + hh - 2)]
            return out + [("moved", n // TB)] if hh == 0 and n % TB == 0 else out
        if kind == "score":
            return [("max", item[1] - 2)]
        if kind == "values":
            return [("exp", GR * item[1] + GR - 1)] + ([("oTs", item[1] // TB - 1)] if item[1] % TB == 0 else [])
        if kind in ("gate", "up", "down"):
            bank = {"gate": "bank6", "up": "bank7"}.get(kind, "bank" + str(6 + item[1] % 2))
            return [(bank,)] if item[2] == 0 else []
        if kind == "heads_norm":
            return [("oTs", item[1]), ("misc",)]
        if kind == "max_rows":
            return [("parts", item[1]), ("misc",)]
        if kind in ("stack_T", "attn_T", "wo", "rows_T", "logits"):
            return [("misc",)]
        return []

    def start(self, item):
        return max([self.now["pe"]] + [self.done.get(k, 0.) for k in self.needs(item)])

    def other(self, engine, time, what, since=0.):
        self.now[engine] = max(self.now[engine], since + self.AFTER) + time
        self.done[what] = self.now[engine] + self.AFTER

    def run(self, item):
        kind = item[0]
        if kind in self.PE:
            self.now["pe"] = self.start(item) + self.PE[kind]
        t = self.now["pe"]
        if kind == "prob":
            self.other("act", .48, ("exp", GR * item[1] + item[2]), t)
        elif kind == "score":
            self.other("dve", .6, ("max", item[1]), t)
        elif kind == "gate" and item[2]:
            self.other("act", .48, ("tanh",), t)
        elif kind == "up":
            self.other("dve", .6, ("bank7",) if item[2] else ("bank6",), t if item[2] else self.done[("tanh",)])
        elif kind == "down" and item[2] == NI - 1:
            self.other("act", .27, ("tanh",), t)
            self.other("dve", .34, ("bank" + str(6 + item[1] % 2),), self.done[("tanh",)])
        elif kind == "heads_out":
            self.other("dve", .6, ("oTs", item[1]), t)
        elif kind == "max_parts":
            self.other("dve", .85, ("parts", item[1]))
        elif kind == "max_rows":
            self.other("act", .48, ("misc",), t)
            self.done[("moved", item[1])] = self.now["act"] + self.ROWS_MOVED
        elif kind in ("heads_norm", "wo"):
            self.other("dve", {"heads_norm": .8, "wo": 1.3}[kind], ("misc",), t)
        elif kind in ("stack_T", "attn_T", "rows_T", "logits"):
            self.other("act", {"stack_T": .9, "logits": .1}.get(kind, .48), ("misc",), t)
        elif kind == "round":
            self.other("act", .48, ("rounded",))
        elif kind == "norm_apply":
            self.other("act", 2., ("norm",))
        elif kind in ("slots", "norm_sums", "norm_root"):
            self.other("dve", {"slots": .55, "norm_sums": 1.2, "norm_root": .7}[kind], (kind,))


def attention_plan():
    fill = []
    for b in range(B):
        for i in range(NI):
            fill += [("gate", b * NI + i, k) for k in range(KD)] + [("up", b * NI + i, k) for k in range(KD)]
        for j in range(TB):
            fill += [("down", b * TB + j, i) for i in range(NI)]
    cost = {"gate": 3, "up": 3, "down": 2}
    total = sum(cost[f[0]] for f in fill)
    spent = 0
    after = {}

    def due(step, h, *stages):
        after.setdefault((step, h), []).extend(stages)

    for u in range(UNITS - 1):
        due(4 * u + 4, 1, ("heads_out", u))
        due(4 * u + 5, 0, ("heads_norm", u))
    for n, (to, of) in enumerate(((3, 0), (4, 0), (5, 1))):
        due(0, n + 1, ("slots", to, of))
    for c, where in enumerate(((1, 1), (2, 1), (3, 1), (4, 0), (5, 3), (6, 1), (7, 1), (8, 1), (9, 3), (10, 1))):
        due(*where, ("stack_T", 1, c))
    due(8, 0, ("round", 1, 0))
    due(8, 3, ("round", 1, 1))
    for step, h, stage in ((17, 2, ("attn_T", 0, 0)), (18, 0, ("attn_T", 0, 1)), (18, 2, ("wo", 0, 0)), (19, 1, ("wo", 0, 1)),
                           (19, 0, ("norm_sums", 0, 0)), (19, 3, ("norm_sums", 0, 1)), (20, 0, ("norm_root", 0, 0)),
                           (20, 1, ("norm_root", 0, 1)), (20, 2, ("norm_root", 0, 2)), (20, 3, ("norm_root", 0, 3)),
                           (21, 0, ("norm_apply", 0)),
                           (21, 2, ("rows_T", 0, 0)), (22, 0, ("rows_T", 0, 1)), (22, 2, ("logits", 0))):
        due(step, h, stage)
    last = B - 1
    due(STEPS - 4, 3, ("attn_T", last, 0))
    due(STEPS - 3, 3, ("wo_half", last))
    end = [("heads_out", UNITS - 1), ("qkv1", 0), ("heads_norm", UNITS - 1), ("qkv1", 1), ("routing_start",), ("attn_T", last, 1), ("wo", last, 0),
           ("norm_sums", last, 0), ("wo", last, 1), ("norm_sums", last, 1),
           *[("norm_root", last, stage) for stage in range(4)], ("norm_apply", last), ("qkv1", 2), ("qkv1", 3),
           ("rope1", 0), ("rows_T", last, 0), ("rows_T", last, 1), ("logits", last)]

    plan = []

    def early(n):
        nonlocal spent
        for _ in range(n):
            f = fill.pop(0)
            spent += cost[f[0]]
            plan.append(f)

    early(2 * KD)
    plan += [("stack_T", 0, c) for c in (8, 0, 1, 9, 2, 3, 4, 5, 6, 7)]
    for m in range(16):
        plan.append(("score", m))
        if m in (7, 11):
            early(1)
    plan += [("max_parts", 0)]
    early(2)
    plan += [("max_rows", 0)]
    early(4)
    start = spent

    clock = Clock()

    def put(item, pace):
        nonlocal spent
        while fill and (spent < pace - SLACK or spent < pace + AHEAD and clock.start(item) > clock.now["pe"] + 0.1
                        and clock.start(fill[0]) < clock.start(item) - 0.1):
            f = fill.pop(0)
            spent += cost[f[0]]
            clock.run(f)
            plan.append(f)
        clock.run(item)
        plan.append(item)

    for n in range(STEPS):
        u, t = divmod(n, TB)
        due_from, due_to = (16 * ((n + 1) // TB + 1) + m for m in SCORES_OF[(n + 1) % TB])
        scores = [("score", m) for m in range(due_from, due_to) if m < 16 * UNITS]
        if n == 0:
            scores = [("score", 16 + m) for m in range(SCORES_OF[1][1])]
        for hh in range(GR):
            pace = start + (total - start) * (GR * n + hh + 1) / (GR * STEPS)
            items = [("prob", n, hh)]
            if hh == 1 and n > 0:
                items.append(("values", n - 1))
            cut = -(-len(scores) // (GR - hh))
            items += scores[:cut]
            scores = scores[cut:]
            if u + 1 < UNITS and (t, hh) == (TB - 1, 0):
                items.append(("max_rows", u + 1))
            if u + 1 < UNITS and (t, hh) == (TB - 2, 2):
                items.append(("max_parts", u + 1))
            for item in items + after.pop((n, hh), []):
                put(item, pace)
    plan += fill
    fill = []
    plan += [("values", STEPS - 1)] + end
    assert not after
    assert not fill
    return plan


def side_work(i):
    return {0: [("q", 2)], 1: [("q", 3), ("norm", 1)], 2: [("sum", 1)], 3: [("branch", 2)], 4: [("branch", 3)]}.get(i, [])


def two_gated_blocks(nc, x_in, wqkv_in, wo_in, wgu_in, wdn_in, win_in, bin_in, wout_in, bout_in,
                     router_in, experts_in, const_in, empty_in, out):
    cols, cwidth = const_columns()
    plan = attention_plan()
    early_c = cols["cos1"][0]

    xs_dram = nc.dram_tensor("slot_rows", (SLOTS, RW), F32, kind="Internal").ap()
    y_dram = nc.dram_tensor("expert_results", (TOK, D), F32, kind="Internal").ap()

    with ExitStack() as ctx:
        def sb(name, shape, dt=F32):
            return ctx.enter_context(nc.sbuf_tensor(name, shape, dt))

        def sem(name):
            return ctx.enter_context(nc.semaphore(name))

        def two_views(name, shape, parts):
            with nc.sbuf_tensor(name, shape, F32) as whole:
                pass
            assert sum(words for words, _ in parts) == int(np.prod(shape[1:]))
            return [whole] + [sb(f"{name}_{n}", [P, words], dt) for n, (words, dt) in enumerate(parts)]

        x = sb("x", [P, NT, D])
        xn, x_high0, w_high_rest = two_views("xn", [P, NT, RW], [(TB * RW, F32R), (TB * RW, F32R)])
        xnT, x_low_words = two_views("xnT", [P, KD, TOK], [(KD * TOK, F32R)])
        gx = sb("gx", [P, NT, D])
        Wm, _, x_high1, _ = two_views("experts", [P, E * EW], [(QK_AT, F32), (KD * S, F32R), (E * EW - QK_AT - KD * S, F32)])
        Sa, _, w_low_words, _ = two_views("shared", [P, 10240], [(WGU_AT, F32), (2 * KD * INTER, F32R), (10240 - WGU_AT - 2 * KD * INTER, F32)])
        late, w_high_words = two_views("late_weights", [P, 3 * INTER], [(3 * INTER, F32R)])
        wl0 = sb("wl0", [P, 1280])
        win = late[:, 0:6 * D].rearrange("p (k n) -> p k n", k=KD)
        wout = late[:, 6 * D:8 * D].rearrange("p (k n) -> p k n", k=KD)
        bin_b = late[:, 8 * D:11 * D]
        bout_b = late[:, 11 * D:12 * D]
        router = sb("router", [P, KD, E])
        cst = sb("cst", [P, cwidth])
        identb = sb("identb", [P, P], BF16)
        tanh_g = sb("tanh_g", [P, 2, 512])
        gated = sb("gated", [P, 2, 512])
        xs = sb("xs", [P, 3, RW])
        xsT = sb("xsT", [P, 2, D])
        bn = sb("bn", [P, NT, 6])
        mv = sb("mv", [P, NT, 2])
        st1 = sb("st1", [P, 6, NT])
        small = sb("small", [P, 3, 80])
        smi = sb("smi", [P, NT], I32)
        tile_e = sb("tile_e", [P, MT], I32)
        tiles_n = sb("tiles_n", [P, 1], I32)
        rsum = sb("rsum", [P, 16])
        nmax = sb("nmax", [P, 16])
        nres = sb("nres", [P, 2, 16])
        mparts = sb("mparts", [P, TB, SPLIT, GR], BF16)
        acol = sb("acol", [P, 4])

        def slot_row(i, lo=0, hi=RW):
            a = i % XR
            if a < 3:
                return xs[:, a, lo:hi]
            return late[:, (a - 3) * RW + lo:(a - 3) * RW + hi]

        def const(name):
            lo, w = cols[name]
            return cst[:, lo:lo + w]

        def before_tile(level, shift=0):
            at_ = 14 * E * level + (4 - shift) * E
            return tanh_g[:, 1, at_:at_ + NT * E + E]

        onehot = before_tile(0, -1)
        ident = const("ident")
        wqkv = wl0[:, 0:768].rearrange("p (k n) -> p k n", k=KD)
        wo = wl0[:, 768:1280].rearrange("p (k n) -> p k n", k=KD)

        at = [0]

        def in_experts(words):
            at[0] += words
            assert at[0] <= E * EW
            return Wm[:, at[0] - words:at[0]]

        qs = in_experts(8192).bitcast(BF16).rearrange("p (b h s) -> p b h s", b=B, h=HEADS)
        ks = in_experts(2048).bitcast(BF16).rearrange("p (b h s) -> p b h s", b=B, h=KVH)
        hT = in_experts(NI * S).rearrange("p (i s) -> p i s", i=NI)
        assert at[0] == QK_AT
        qk = in_experts(NT * QKH * HD).rearrange("p (j n) -> p j n", j=NT)
        vaug = in_experts(NT * KVH * VW).rearrange("p (j g c) -> p j g c", j=NT, g=KVH)
        an = in_experts(TB * D).rearrange("p (t n) -> p t n", t=TB)
        anT = in_experts(KD * S).rearrange("p (k s) -> p k s", k=KD)
        oTs = xs[:].rearrange("p a n -> p (a n)")[:, 0:S]
        mrow = in_experts(512).bitcast(BF16).rearrange("p (a s) -> p a s", a=2)

        late_expert = at[0] // EW
        stack_words = in_experts(TB * QKH * KS // 2)
        stack = stack_words.bitcast(BF16).rearrange("p (n c) -> p n c", c=KS)
        probs = Sa[:, 0:4096].rearrange("p (a h s) -> p a h s", a=2, h=GR)
        wgu = Sa[:, WGU_AT:WGU_AT + 2 * KD * INTER].rearrange("p (k n) -> p k n", k=KD)
        wdn = Sa[:, 8192:10240].rearrange("p (i n) -> p i n", i=NI)
        rot_a = gx[:, 0:5, :].rearrange("p a b -> p (a b)")
        qkv1 = (stack_words[:, 0:TB * 3 * D].rearrange("p (j n) -> p j n", j=TB), Sa[:, 0:TB * 3 * D].rearrange("p (j n) -> p j n", j=TB))
        kv = Sa[:, 6144:8192].rearrange("p (j n) -> p j n", j=NT)
        rope_t = Sa[:, 8192:10240]
        yg = Sa[:, 0:2048].rearrange("p (j n) -> p j n", j=NT)
        ya = Sa[:, 4096:6144].rearrange("p (j n) -> p j n", j=NT)
        hmT = Sa[:, 8192:9216].rearrange("p (a n) -> p a n", a=2)
        wsc = Sa[:, 9216:10240].rearrange("p (b k n) -> p b k n", b=B, k=KD)
        ysb = bin_b[:, 0:2 * D].rearrange("p (a n) -> p a n", a=2)
        ytanh = bin_b[:, 2 * D:3 * D]
        squares = wl0[:, 1024:1280]
        hm = wl0[:, 0:1024].rearrange("p (a n) -> p a n", a=2)

        def w_high(k, lo, hi):
            if (k, lo // INTER) == (KD - 1, 1):
                return w_high_rest[:, lo - INTER:hi - INTER]
            return w_high_words[:, 2 * INTER * k + lo:2 * INTER * k + hi]

        def w_low(k, lo, hi):
            return w_low_words[:, 2 * INTER * k + lo:2 * INTER * k + hi]

        def x_high(b, k):
            return (x_high1 if b else x_high0)[:, S * k:S * k + S]

        def x_low(b, k):
            return x_low_words[:, TOK * k + S * b:TOK * k + S * b + S]

        weight_pieces = [(k, INTER * half) for half in range(2) for k in range(KD)]

        ps = ctx.enter_context(nc.psum_tensor("ps", [P, 8, 512], F32))
        misc = ps[:, 5, :]
        miscb = misc.bitcast(BF16)

        x_in_s = [sem(f"x_loaded{b}") for b in range(B)]
        names = ("acol_psum acol_ready act_step attn_T_ready branch_free branch_psum branch_ready const_loaded "
                 "cos1 counts down_ready down_tanh dve_step e_down e_gate e_gated e_h e_tanh e_up end_free exp_done first_part "
                 "experts_here gate_free gate_ready heads_T heads_copied hmT_ready hm_T identb_ready ksum_sq "
                 "kv_ready kv_summed late_loaded layer1_loaded w_high_ready w_low_ready x_high_ready x_low_ready logits max_done misc_free mparts_ready mrow_psum  onehot "
                 "out_ready parts_done parts_in pool_step prob_ready product_done product_ready qT_psum qT_ready qk_copied qkv1_psum "
                 "qkv1_ready qkv_psum results_stored rope_q rows_T rows_norm scattered score_ready slots "
                 "slots_copied slots_emptied stack_T stack_copied stack_copied2 std_ready tanh_done tile_experts "
                 "up_free up_ready v_copied values_done vone wdn_loaded wgu_loaded wo_loaded wo_ready "
                 "wqkv_loaded wsc_ready x1_part xnT_psum xnT_ready xsT_ready xs_T y_half y_ready y_tanh ").split()
        s = {n: sem(n) for n in names}
        row_sem = [sem(f"max_rows_moved{a}") for a in range(2)]
        y_store = [sem(f"y_stored{a}") for a in range(2)]
        exp_loaded = [sem(f"expert{e}_in") for e in range(E)]
        x_sem = [sem(f"slot_rows_loaded{a}") for a in range(XR)]
        result_sem = [sem(f"results_loaded{q}") for q in range(NT // 2)]
        out_sem = [sem(f"out_stored{q}") for q in range(NT // 2)]

        block = ctx.enter_context(nc.Block())

        def score_at(m):
            u, r = divmod(m, 16)
            return u // KVH, u % KVH, r // TB, r % TB

        bank_use = {}
        uses = {6: 0, 7: 0}
        misc_use = {}
        end_bank = {("attn_T", B - 1, 1): 2, ("wo", B - 1, 0): 0, ("wo", B - 1, 1): 1, ("rows_T", B - 1, 0): 0, ("rows_T", B - 1, 1): 1,
                    ("logits", B - 1): 2}
        end_use = {it: n for n, it in enumerate(end_bank)}
        for it in plan:
            if it in end_bank:
                continue
            if it[0] in ("gate", "up") and it[2] == 0:
                b_ = 6 if it[0] == "gate" else 7
            elif it[0] == "down" and it[2] == 0:
                b_ = 6 + it[1] % 2
            elif it[0] in ("max_rows", "heads_norm", "attn_T", "wo", "rows_T", "logits") or it[:2] == ("stack_T", 1):
                misc_use[it] = len(misc_use)
                continue
            else:
                continue
            bank_use[it[:2]] = (b_, uses[b_])
            uses[b_] += 1
        def place(it):
            if it in end_bank:
                return ps[:, end_bank[it], :], s["end_free"], end_use[it] + 1
            return misc, s["misc_free"], misc_use[it] + 1

        branch_bank = (7, 6, 7, 7)
        q_bank = (0, 1, 7, 7)

        def qkv1_bank(j):
            lo = 6 if j % 2 == 0 else 3
            return ps[:, lo:lo + 2, :]

        free_sem = {6: s["gate_free"], 7: s["up_free"]}
        stack_order = [it[2] for it in plan if it[:2] == ("stack_T", 0)]
        stack_bank = (4, 5, 2, 3)

        def stacked(b, c, n):
            src = ps[0:KS, stack_bank[n % 4] if b == 0 else 5, :].bitcast(BF16)
            dst = qs[0:KS, b, 2 * c:2 * c + 2, :] if c < 8 else ks[0:KS, b, 2 * c - 16:2 * c - 14, :]
            return src, dst

        def tiles_from(eng, n_tiles, i, tile, drain):
            if i == MT:
                drain(i)
                return
            with eng.If(n_tiles > i):
                tile(i)
                tiles_from(eng, n_tiles, i + 1, tile, drain)
            with eng.Else():
                drain(i)

        def place_in_stack(a, h0=0, h1=QKH):
            return stack.rearrange("p (j h) c -> p j h c", j=TB)[:, :, h0:h1, HD * a:HD * a + HD]

        def prepare(b, stage, eng, ops, chain):
            rows = qk[:, TB * b:TB * b + TB, :].rearrange("p j (h c) -> p j h c", c=HD)
            heads = qk[:, TB * b:TB * b + TB, :].rearrange("p j (h c) -> p (j h) c", c=HD)
            rot = rows[:, :, :, 0:8]
            pair = rot.rearrange("p j h (r two) -> p j h r two", two=2)
            ta = rot_a[:, 0:TB * QKH * 8].rearrange("p (j h c) -> p j h c", j=TB, h=QKH)
            tb = rot_a[:, TB * QKH * 8:TB * QKH * 16].rearrange("p (j h c) -> p j h c", j=TB, h=QKH)
            tbp = tb.rearrange("p j h (r two) -> p j h r two", two=2)
            res = rot_a[:, 0:TB * QKH * HD].rearrange("p (n c) -> p n c", c=HD)
            res4 = res.rearrange("p (j h) c -> p j h c", j=TB)
            shape4 = [P, TB, QKH, 4]
            angle = lambda name, c, shape: const(name).rearrange("p (j o c) -> p j o c", j=TB, o=1).to_broadcast(shape)
            slot = place_in_stack

            if stage == 0:
                eng.wait_ge(s["qk_copied"], 2 * (b + 1))
                if b:
                    eng.wait_ge(s["parts_done"], b)
                    eng.wait_ge(s["const_loaded"], 16)
                ops.tensor_tensor(ta, rot, angle("cos0", 8, [P, TB, QKH, 8]), ALU.mult)
                ops.tensor_tensor(tbp[:, :, :, :, 0], pair[:, :, :, :, 1], angle("sin0e", 4, shape4), ALU.mult)
                chain(ops.tensor_tensor(tbp[:, :, :, :, 1], pair[:, :, :, :, 0], angle("sin0o", 4, shape4), ALU.mult))
                chain(ops.tensor_tensor(rot, ta, tb, ALU.add))
            elif stage == 1:
                if b:
                    eng.wait_ge(s["stack_T"], 10 * b)
                ops.tensor_copy(slot(0), rows).then_inc(s["first_part"], 1)
                eng.wait_ge(s["first_part"], b + 1)
                chain(ops.tensor_tensor(res, heads, stack[:, :, 0:HD], ALU.subtract))
            elif stage == 2:
                ops.tensor_copy(slot(1), res4).then_inc(s["parts_in"], 1)
                eng.wait_ge(s["parts_in"], b + 1)
            else:
                ops.tensor_tensor(slot(2, 0, HEADS), res4[:, :, 0:HEADS, :], slot(1, 0, HEADS), ALU.subtract)
                ops.tensor_tensor(slot(3, HEADS), res4[:, :, HEADS:, :], slot(1, HEADS), ALU.subtract)
                ops.tensor_copy(slot(2, HEADS), slot(0, HEADS))
                ops.tensor_copy(slot(5, HEADS), slot(0, HEADS))
                ops.tensor_copy(slot(4, HEADS), slot(1, HEADS)).then_inc(s["parts_done"], 1)

        @block.sync
        def _(sp):
            sp.dma_start(x[:, 0:TB, :], x_in[:, 0:TB, :]).then_inc(x_in_s[0], 16)
            sp.dma_start(cst[:, 0:early_c], const_in[:, 0:early_c]).then_inc(s["const_loaded"], 16)
            sp.dma_start(wqkv, wqkv_in).then_inc(s["wqkv_loaded"], 16)
            sp.dma_start(x[:, TB:NT, :], x_in[:, TB:NT, :]).then_inc(x_in_s[1], 16)
            sp.dma_start(wgu, wgu_in).then_inc(s["wgu_loaded"], 16)
            sp.dma_start(wdn, wdn_in).then_inc(s["wdn_loaded"], 16)
            sp.dma_start(wo, wo_in).then_inc(s["wo_loaded"], 16)
            sp.dma_start(cst[:, early_c:cwidth], const_in[:, early_c:cwidth]).then_inc(s["late_loaded"], 16)
            sp.dma_start(router[:], router_in).then_inc(s["late_loaded"], 16)
            sp.dma_start(xs_dram.rearrange("(i p) d -> p i d", p=P),
                         empty_in.rearrange("p (o d) -> p o d", o=1).to_broadcast([P, MT, RW])).then_inc(s["slots_emptied"], 16)

            for u in range(UNITS):
                b, g = divmod(u, KVH)
                sp.wait_ge(s["misc_free"], misc_use[("max_rows", u)] + 1)
                for part in range(SPLIT):
                    sp.dma_start(qs[KS + part:KS + part + 1, b, GR * g:GR * g + GR, :],
                                 mrow[GR * part:GR * part + GR, u % 2, :]).then_inc(row_sem[u % 2], 16)

            sp.wait_ge(s["up_ready"], B * NI)
            for dst, src in ((win, win_in), (wout, wout_in), (bin_b, bin_in.partition_broadcast(P)), (bout_b, bout_in.partition_broadcast(P))):
                sp.dma_start(dst, src).then_inc(s["layer1_loaded"], 16)

            def expert_here(e):
                sp.wait_ge(exp_loaded[e], 16)
                sp.sem_inc(s["experts_here"], 1)

            def load_rows(i):
                sp.dma_start(slot_row(i), xs_dram[P * i:P * i + P, :]).then_inc(x_sem[i % XR], 16)

            sp.wait_ge(s["wo_ready"], B * TB // 2)
            for e in range(E):
                if e == late_expert:
                    sp.wait_ge(s["qT_psum"], KD)
                    sp.wait_ge(s["ksum_sq"], 1)
                    sp.wait_ge(s["kv_ready"], 1)
                sp.dma_start(Wm[:, e * EW:(e + 1) * EW], experts_in[e]).then_inc(exp_loaded[e], 16)
                if e == FIRST_EXPERTS - 1:
                    sp.wait_ge(s["scattered"], 16 * NT)
                    sp.wait_ge(s["qkv1_psum"], NT)
                    for i in range(XR):
                        load_rows(i)
                    for a in range(FIRST_EXPERTS):
                        expert_here(a)
            for e in range(FIRST_EXPERTS, E):
                expert_here(e)

            def reload_rows(i):
                if i + XR < MT:
                    sp.wait_ge(s["xs_T"], i + 1)
                    sp.wait_ge(y_store[i % 2], 16 * (i // 2 + 1))
                    load_rows(i + XR)

            for i in range(SURE):
                reload_rows(i)
            sp.wait_ge(s["tile_experts"], 1)
            n_tiles = sp.value_load(tiles_n[0:1, 0:1], min_val=SURE, max_val=MT)
            tiles_from(sp, n_tiles, SURE, reload_rows, lambda i: None)

            sp.wait_ge(s["results_stored"], 1)
            for q in range(NT // 2):
                sp.dma_start(yg[:, 2 * q:2 * q + 2, :], y_dram.rearrange("(j p) d -> p j d", p=P)[:, 2 * q:2 * q + 2, :]).then_inc(result_sem[q], 16)
            for q in range(NT // 2):
                sp.wait_ge(s["out_ready"], q + 1)
                sp.dma_start(out[:, 2 * q:2 * q + 2, :], x[:, 2 * q:2 * q + 2, :]).then_inc(out_sem[q], 16)
            for q in range(NT // 2):
                sp.wait_ge(out_sem[q], 16)

        @block.gpsimd
        def _(pool):
            nc.gpsimd.memset(vaug[:, :, :, HD:VW], 0.0).then_inc(s["vone"], 1)
            pool.wait_ge(s["vone"], 1)
            nc.gpsimd.memset(vaug[:, :, :, HD:HD + 1], 1.0).then_inc(s["vone"], 1)
            pool.wait_ge(s["vone"], 2)
            nc.gpsimd.memset(ks[KS:P, :, :, :], 1.0).then_inc(s["vone"], 1)
            pool.wait_ge(s["vone"], 3)
            def lower_weights(piece):
                k, lo = weight_pieces[piece]
                pool.wait_ge(s["w_high_ready"], piece + 1)
                w = wgu[:, k, lo:lo + INTER]
                nc.gpsimd.tensor_tensor(w_low(k, lo, lo + INTER), w, w_high(k, lo, lo + INTER).bitcast(F32), ALU.subtract).then_inc(s["w_low_ready"], 1)

            def lower_rows(b):
                for k in range(KD):
                    pool.wait_ge(s["x_high_ready"], KD * b + k + 1)
                    pool.wait_ge(s["qkv_psum"], TB * (b + 1))
                    xk = xnT[:, k, S * b:S * b + S]
                    nc.gpsimd.tensor_tensor(x_low(b, k), xk, x_high(b, k).bitcast(F32), ALU.subtract).then_inc(s["x_low_ready"], 1)

            lower_weights(0)
            lower_weights(1)
            lower_rows(0)
            lower_weights(2)
            lower_weights(3)

            steps = [0]

            def chain(ins):
                steps[0] += 1
                ins.then_inc(s["pool_step"], 1)
                pool.wait_ge(s["pool_step"], steps[0])

            for stage in range(4):
                prepare(1, stage, pool, nc.gpsimd, chain)
            lower_rows(1)

            def key_times_value(b):
                pool.wait_ge(s["rope_q"], b + 1)
                nc.gpsimd.tensor_tensor(kv[:, TB * b:TB * b + TB, :], qkv1[b][:, :, D:2 * D], qkv1[b][:, :, 2 * D:3 * D], ALU.mult
                                        ).then_inc(s["kv_ready"], 1)

            key_times_value(0)
            pool.wait_ge(s["slots"], 1)
            pool.wait_ge(s["slots_emptied"], 16)
            pool.wait_ge(s["rows_norm"], 2 * NT)
            for j in range(NT):
                nc.gpsimd.indirect_dma_start(
                    out=xs_dram[:, :], out_offset=bass.IndirectOffsetOnAxis(ap=smi[:, j:j + 1], axis=0),
                    in_=xn[:, j, :], in_offset=None).then_inc(s["scattered"], 16)
            key_times_value(1)
            def store(i):
                pool.wait_ge(s["y_ready"], i + 1)
                nc.gpsimd.indirect_dma_start(
                    out=y_dram[:, :], out_offset=bass.IndirectOffsetOnAxis(ap=slot_row(i, TOKEN_COL, TOKEN_COL + 1).bitcast(I32), axis=0),
                    in_=ysb[:, i % 2, :], in_offset=None, bounds_check=TOK - 1, oob_is_err=False).then_inc(y_store[i % 2], 16)

            def all_stored(n):
                for a in range(2):
                    pool.wait_ge(y_store[a], 16 * ((n + 1 - a) // 2))
                pool.sem_inc(s["results_stored"], 1)

            for i in range(SURE):
                store(i)
            n_tiles = pool.value_load(tiles_n[0:1, 0:1], min_val=SURE, max_val=MT)
            tiles_from(pool, n_tiles, SURE, store, all_stored)
            for q in range(NT // 2 - 1, NT // 2):
                pool.wait_ge(result_sem[q], 16)
                pool.wait_ge(s["branch_ready"], NT // 2)
                nc.gpsimd.tensor_tensor(ya[:, 2 * q:2 * q + 2, :], yg[:, 2 * q:2 * q + 2, :], gx[:, 2 * q:2 * q + 2, :], ALU.mult
                                        ).then_inc(s["product_ready"], 1)

        @block.scalar
        def _(act):
            steps = [0]

            def chain(ins):
                steps[0] += 1
                ins.then_inc(s["act_step"], 1)
                act.wait_ge(s["act_step"], steps[0])

            def apply_norm(b):
                act.wait_ge(s["std_ready"], B + b + 1)
                act.wait_ge(s["up_ready"], NI)
                for j in range(TB * b, TB * b + TB):
                    nc.scalar.activation(xn[:, j, 0:D], x[:, j, :], ACT.Identity, scale=st1[:, 4, j:j + 1], bias=st1[:, 5, j:j + 1]
                                         ).then_inc(s["rows_norm"], 1)

            for k in range(KD):
                act.wait_ge(s["xnT_psum"], k + 1)
                nc.scalar.activation(xnT[:, k, 0:S], ps[:, k, :], ACT.Copy).then_inc(s["xnT_ready"], 1)
            def projections(b):
                lo = 4 - 4 * b
                act.wait_ge(s["qkv_psum"], TB * (b + 1))
                for c in range(2):
                    nc.scalar.activation(qk[:, TB * b + 2 * c:TB * b + 2 * c + 2, :], ps[:, lo + 2 * c:lo + 2 * c + 2, 0:QKH * HD],
                                         ACT.Copy).then_inc(s["qk_copied"], 1)
                nc.scalar.activation(vaug[:, TB * b:TB * b + TB, :, 0:HD],
                                     ps[:, lo:lo + TB, QKH * HD:QKH * HD + KVH * HD].rearrange("p j (g c) -> p j g c", g=KVH),
                                     ACT.Copy).then_inc(s["v_copied"], 1)
            def round_weights(piece):
                k, lo = weight_pieces[piece]
                nc.scalar.activation(w_high(k, lo, lo + INTER), wgu[:, k, lo:lo + INTER], ACT.Copy).then_inc(s["w_high_ready"], 1)

            def round_rows(b, k):
                act.wait_ge(s["xnT_ready"], KD * (b + 1))
                nc.scalar.activation(x_high(b, k), xnT[:, k, S * b:S * b + S], ACT.Copy).then_inc(s["x_high_ready"], 1)

            act.wait_ge(s["wgu_loaded"], 16)
            round_weights(0)
            round_weights(1)
            for k in range(KD):
                round_rows(0, k)
            round_weights(2)
            projections(0)
            act.wait_ge(s["xnT_psum"], B * KD)
            round_weights(3)
            act.wait_ge(s["first_part"], 1)
            for to in (3, 4):
                nc.scalar.activation(place_in_stack(to, 0, HEADS), place_in_stack(0, 0, HEADS), ACT.Copy).then_inc(s["slots_copied"], 1)
            projections(1)

            def key_squares(b):
                for j in range(TB * b, TB * b + TB):
                    act.wait_ge(s["rope_q"], b + 1)
                    chain(nc.scalar.activation(squares, qkv1[b][:, j % TB, D:2 * D], ACT.Square, accum_out=st1[:, 2, j:j + 1]))
                nc.scalar.activation(st1[:, 3, TB * b:TB * b + TB], st1[:, 2, TB * b:TB * b + TB], ACT.Copy).then_inc(s["ksum_sq"], 1)

            for it in plan:
                kind = it[0]
                if kind == "round":
                    act.wait_ge(s["parts_done"], 1)
                    round_rows(*it[1:])
                elif kind == "prob":
                    _, n, hh = it
                    act.wait_ge(s["prob_ready"], 4 * n + hh + 1)
                    if n >= 2 and hh == 0:
                        act.wait_ge(s["values_done"], n - 1)
                    nc.scalar.activation(probs[:, n % 2, hh, :], ps[:, 2 + hh % 2, :], ACT.Exp,
                                         scale=float(HD) ** -0.5).then_inc(s["exp_done"], 1)
                elif kind == "stack_T":
                    _, b, c = it
                    n = stack_order.index(c) if b == 0 else 10 + c
                    if b or n % 2 == 0:
                        src, dst = stacked(b, c, n)
                        act.wait_ge(s["stack_T"], n + 1)
                        nc.scalar.activation(dst, src.rearrange("p (h s) -> p h s", h=2), ACT.Copy
                                             ).then_inc(s["misc_free" if b else "stack_copied"], 1)
                elif kind == "norm_apply" and it[1] < B - 1:
                    apply_norm(it[1])
                elif kind == "rows_T":
                    _, b, k = it
                    bank, read, _ = place(it)
                    act.wait_ge(s["rows_T"], KD * b + k + 1)
                    nc.scalar.activation(xnT[:, k, S * b:S * b + S], bank, ACT.Copy).then_inc(read, 1)
                elif kind == "logits":
                    b = it[1]
                    bank, read, _ = place(it)
                    act.wait_ge(s["logits"], b + 1)
                    nc.scalar.activation(small[:, 0, 32 * b:32 * b + 32], bank[:, 0:32], ACT.Exp, scale=-1.0).then_inc(read, 1)
                elif kind == "gate" and it[2] == KD - 1:
                    c = it[1]
                    act.wait_ge(s["gate_ready"], c + 1)
                    if c >= 2:
                        act.wait_ge(s["gate_free"], bank_use[("gate", c - 2)][1] + 1)
                    nc.scalar.activation(tanh_g[:, c % 2, :], ps[:, 6, :], ACT.Tanh, scale=0.5).then_inc(s["tanh_done"], 1)
                elif kind == "down" and it[2] == NI - 1:
                    j = it[1]
                    act.wait_ge(s["down_ready"], j + 1)
                    act.wait_ge(s["up_free"], bank_use[("up", NI * (j // TB) + NI - 1)][1] + 1)
                    if j >= 2:
                        bk, n = bank_use[("down", j - 2)]
                        act.wait_ge(free_sem[bk], n + 1)
                    nc.scalar.activation(gated[:, j % 2, 0:D], ps[:, 6 + j % 2, 0:D], ACT.Tanh, scale=0.25).then_inc(s["down_tanh"], 1)
                elif kind == "max_rows":
                    u = it[1]
                    act.wait_ge(s["mrow_psum"], u + 1)
                    if u >= 2:
                        act.wait_ge(row_sem[u % 2], 48 * (u // 2))
                    nc.scalar.activation(mrow[0:SPLIT * GR, u % 2, :], miscb[0:SPLIT * GR, 0:S], ACT.Copy).then_inc(s["misc_free"], 1)
                elif kind == "attn_T":
                    n = KD * it[1] + it[2]
                    act.wait_ge(s["attn_T_ready"], n + 1)
                    if it[1] > 0:
                        act.wait_ge(s["wo_ready"], TB // 2 * it[1])
                    bank, read, _ = place(it)
                    nc.scalar.activation(anT[:, it[2], :], bank, ACT.Copy).then_inc(read, 1)

            def q_copy(n):
                b, k = divmod(n, KD)
                act.wait_ge(s["qT_psum"], n + 1)
                nc.scalar.activation(xnT[:, k, S * b:S * b + S], ps[:, q_bank[n], :], ACT.Copy).then_inc(s["qT_ready"], 1)

            def xsT_copy(i):
                act.wait_ge(s["xs_T"], i + 1)
                if i >= 2:
                    act.wait_ge(s["e_up"], i - 1)
                nc.scalar.activation(xsT[:, i % 2, :], ps[:, 4, 0:D], ACT.Copy).then_inc(s["xsT_ready"], 1)

            def hmT_copy(i):
                act.wait_ge(s["hm_T"], i + 1)
                if i >= 2:
                    act.wait_ge(s["e_down"], i - 1)
                nc.scalar.activation(hmT[:, i % 2, :], ps[:, 5, :], ACT.Copy).then_inc(s["hmT_ready"], 1)

            def result_tanh(k):
                act.wait_ge(s["y_half"], k + 1)
                if k:
                    act.wait_ge(s["y_ready"], k)
                nc.scalar.activation(ytanh, ysb[:, k % 2, :], ACT.Tanh).then_inc(s["y_tanh"], 1)

            def tile(i):
                act.wait_ge(s["e_gate"], i + 1)
                if i >= 2:
                    act.wait_ge(s["e_h"], i - 1)
                nc.scalar.activation(tanh_g[:, i % 2, :], ps[:, i % 2, :], ACT.Tanh, scale=0.5).then_inc(s["e_tanh"], 1)
                if i:
                    hmT_copy(i - 1)
                if i + 1 < MT:
                    xsT_copy(i + 1)
                if i:
                    result_tanh(i - 1)

            def rest(i):
                hmT_copy(i - 1)
                result_tanh(i - 1)

            key_squares(0)
            q_copy(0)
            q_copy(1)
            xsT_copy(0)
            for i in range(SURE):
                tile(i)
                if i == 0:
                    key_squares(1)
                for kind, n in side_work(i):
                    if kind == "q":
                        q_copy(n)
            n_tiles = act.value_load(tiles_n[0:1, 0:1], min_val=SURE, max_val=MT)
            tiles_from(act, n_tiles, SURE, tile, rest)

        @block.vector
        def _(dve):
            steps = [0]

            def chain(ins):
                steps[0] += 1
                ins.then_inc(s["dve_step"], 1)
                dve.wait_ge(s["dve_step"], steps[0])

            def inverse_root(j0, j1, stage):
                v, y, t = st1[:, 0, j0:j1], st1[:, 4, j0:j1], st1[:, 1, j0:j1]
                if stage == 0:
                    chain(nc.vector.tensor_scalar(t.bitcast(I32), v.bitcast(I32), 1, None, ALU.logical_shift_right))
                    chain(nc.vector.tensor_scalar(y.bitcast(I32), t.bitcast(I32), -1.0, float(0x5F3759DF), ALU.mult, ALU.add))
                else:
                    chain(nc.vector.tensor_tensor(t, y, y, ALU.mult))
                    chain(nc.vector.scalar_tensor_tensor(t, t, -0.5, v, ALU.mult, ALU.mult))
                    chain(nc.vector.scalar_tensor_tensor(y, t, 1.5, y, ALU.add, ALU.mult))

            def norm_sums(j0, j1):
                for j in range(j0, j1):
                    last = nc.vector.bn_stats(bn[:, j, :], x[:, j, :])
                chain(last)
                for j in range(j0, j1):
                    last = nc.vector.bn_aggr(mv[:, j, :], bn[:, j, :])
                chain(last)

            def norm_root(b, stage):
                j0, j1 = TB * b, TB * b + TB
                if stage == 0:
                    chain(nc.vector.tensor_scalar_add(st1[:, 0, j0:j1], mv[:, j0:j1, 1], LN_EPS))
                inverse_root(j0, j1, stage)
                if stage == 3:
                    nc.vector.scalar_tensor_tensor(st1[:, 5, j0:j1], mv[:, j0:j1, 0], -1.0, st1[:, 4, j0:j1], ALU.mult, ALU.mult
                                                   ).then_inc(s["std_ready"], 1)

            def apply_norm(layer, b):
                dve.wait_ge(s["std_ready"], B * layer + b + 1)
                for j in range(TB * b, TB * b + TB):
                    nc.vector.tensor_scalar(xn[:, j, 0:D], x[:, j, :], st1[:, 4, j:j + 1], st1[:, 5, j:j + 1], ALU.mult, ALU.add
                                            ).then_inc(s["rows_norm"], 1)

            for b in range(B):
                dve.wait_ge(x_in_s[b], 16)
                norm_sums(TB * b, TB * b + TB)
                for stage in range(4):
                    norm_root(b, stage)
                apply_norm(0, b)
            dve.wait_ge(s["const_loaded"], 16)
            nc.vector.tensor_copy(identb[:], ident).then_inc(s["identb_ready"], 1)

            for k in range(KD):
                dve.wait_ge(s["xnT_psum"], KD + k + 1)
                nc.vector.tensor_copy(xnT[:, k, S:2 * S], ps[:, KD + k, :]).then_inc(s["xnT_ready"], 1)

            def qkv1_bias(j):
                dve.wait_ge(s["qkv1_psum"], j + 1)
                if j == 0:
                    dve.wait_ge(s["stack_T"], 10 * B)
                nc.vector.tensor_tensor(qkv1[j // TB][:, j % TB, :], qkv1_bank(j).rearrange("p a n -> p (a n)")[:, 0:3 * D], bin_b, ALU.add
                                        ).then_inc(s["qkv1_ready"], 1)

            def rope1(b):
                r2 = qkv1[b][:, :, 0:2 * D].rearrange("p j (q n) -> p j q n", q=2)
                rot = r2[:, :, :, 0:ROT]
                pair = rot.rearrange("p j q (r two) -> p j q r two", two=2)
                n_ = TB * 2 * ROT
                ta = rope_t[:, 0:n_].rearrange("p (j q n) -> p j q n", j=TB, q=2)
                tb = rope_t[:, n_:2 * n_].rearrange("p (j q n) -> p j q n", j=TB, q=2)
                tbp = tb.rearrange("p j q (r two) -> p j q r two", two=2)
                half = [P, TB, 2, ROT // 2]
                angle = lambda name, shape: const(name).rearrange("p (j o n) -> p j o n", j=TB, o=1).to_broadcast(shape)
                if b:
                    dve.wait_ge(s["rope_q"], b)
                dve.wait_ge(s["qkv1_ready"], TB * (b + 1))
                nc.vector.tensor_tensor(ta, rot, angle("cos1", [P, TB, 2, ROT]), ALU.mult)
                nc.vector.tensor_tensor(tbp[:, :, :, :, 0], pair[:, :, :, :, 1], angle("sin1e", half), ALU.mult)
                chain(nc.vector.tensor_tensor(tbp[:, :, :, :, 1], pair[:, :, :, :, 0], angle("sin1o", half), ALU.mult))
                nc.vector.tensor_tensor(rot, ta, tb, ALU.add).then_inc(s["rope_q"], 1)

            for stage in range(4):
                prepare(0, stage, dve, nc.vector, chain)
            nc.vector.tensor_copy(place_in_stack(5, 0, HEADS), place_in_stack(1, 0, HEADS)).then_inc(s["slots_copied"], 1)

            for it in plan:
                kind = it[0]
                if kind == "score":
                    m = it[1]
                    b, g, hh, t = score_at(m)
                    dve.wait_ge(s["score_ready"], m + 1)
                    if m % 16 == 0 and m:
                        dve.wait_ge(s["mparts_ready"], m // 16)
                    nc.vector.tensor_reduce(nmax[:, 4 * t + hh:4 * t + hh + 1], ps[:, m % 2, :], AX, ALU.max,
                                            negate=True).then_inc(s["max_done"], 1)
                elif kind == "stack_T" and it[1] == 0:
                    n = stack_order.index(it[2])
                    if n % 2:
                        src, dst = stacked(0, it[2], n)
                        dve.wait_ge(s["stack_T"], n + 1)
                        nc.vector.tensor_copy(dst, src.rearrange("p (h s) -> p h s", h=2)).then_inc(s["stack_copied2"], 1)
                elif kind == "slots":
                    to, of = it[1:]
                    dve.wait_ge(s["parts_in"], B)
                    nc.vector.tensor_copy(place_in_stack(to, 0, HEADS), place_in_stack(of, 0, HEADS)).then_inc(s["slots_copied"], 1)
                elif kind == "norm_sums":
                    _, b, c = it
                    dve.wait_ge(s["x1_part"], TB // 2 * b + c + 1)
                    norm_sums(TB * b + 2 * c, TB * b + 2 * c + 2)
                elif kind == "norm_root":
                    norm_root(it[1], it[2])
                elif kind == "norm_apply" and it[1] == B - 1:
                    apply_norm(1, it[1])
                elif kind == "max_parts":
                    u = it[1]
                    dve.wait_ge(s["max_done"], 16 * (u + 1))
                    if u:
                        dve.wait_ge(s["mrow_psum"], u)
                    v = nmax[:].rearrange("p (t h) -> p t h", t=TB)
                    r0 = nres[:, 0, :].rearrange("p (t h) -> p t h", t=TB)
                    chain(nc.vector.tensor_copy(mparts[:, :, 0, :], v))
                    chain(nc.vector.tensor_tensor(r0, v, mparts[:, :, 0, :], ALU.subtract))
                    chain(nc.vector.tensor_copy(mparts[:, :, 1, :], r0))
                    nc.vector.tensor_tensor(mparts[:, :, 2, :], r0, mparts[:, :, 1, :], ALU.subtract).then_inc(s["mparts_ready"], 1)
                elif kind == "up" and it[2] == 0:
                    c = it[1]
                    b, i = divmod(c, NI)
                    dve.wait_ge(s["tanh_done"], c + 1)
                    if i < 2 and b:
                        dve.wait_ge(s["down_tanh"], TB * b)
                    nc.vector.scalar_tensor_tensor(gated[:, c % 2, :], tanh_g[:, c % 2, :], 1.0, ps[:, 6, :], ALU.add, ALU.mult
                                                   ).then_inc(s["gate_free"], 1)
                elif kind == "up" and it[2] == KD - 1:
                    c = it[1]
                    b, i = divmod(c, NI)
                    dve.wait_ge(s["gate_free"], bank_use[("gate", c)][1] + 1)
                    dve.wait_ge(s["up_ready"], c + 1)
                    if b and i == 0:
                        dve.wait_ge(s["down_ready"], TB * b)
                    nc.vector.tensor_tensor(hT[:, i, :], gated[:, c % 2, :], ps[:, 7, :], ALU.mult).then_inc(s["up_free"], 1)
                    dve.wait_ge(s["up_free"], bank_use[("up", c)][1] + 1)
                elif kind == "down" and it[2] == NI - 1:
                    j = it[1]
                    dve.wait_ge(s["down_tanh"], j + 1)
                    if j == 0:
                        dve.wait_ge(s["parts_done"], B)
                    bk, n = bank_use[("down", j)]
                    nc.vector.scalar_tensor_tensor(gx[:, j, :], gated[:, j % 2, 0:D], 1.0, ps[:, bk, 0:D], ALU.add, ALU.mult
                                                   ).then_inc(free_sem[bk], 1)
                elif kind == "heads_out":
                    u = it[1]
                    dve.wait_ge(s["values_done"], TB * (u + 1))
                    if u:
                        dve.wait_ge(s["heads_T"], u)
                    nc.vector.tensor_copy(oTs, ps[:, 4, :]).then_inc(s["heads_copied"], 1)
                elif kind == "heads_norm":
                    u = it[1]
                    b, g = divmod(u, KVH)
                    o4 = misc.rearrange("p (t h c) -> p t h c", t=TB, h=GR)
                    dve.wait_ge(s["heads_T"], u + 1)
                    r = rsum[:].rearrange("p (t h o) -> p t h o", t=TB, o=1)
                    chain(nc.vector.reciprocal(r, o4[:, :, :, HD:HD + 1]))
                    if g == 0 and b:
                        dve.wait_ge(s["attn_T_ready"], KD * b)
                    nc.vector.tensor_tensor(an[:, :, 64 * g:64 * g + 64].rearrange("p t (h c) -> p t h c", h=GR),
                                            o4[:, :, :, 0:HD], r.to_broadcast([P, TB, GR, HD]), ALU.mult).then_inc(s["misc_free"], 1)
                elif kind == "wo":
                    _, b, c = it
                    n = TB // 2 * b + c
                    j = TB * b + 2 * c
                    dve.wait_ge(s["wo_ready"], n + 1)
                    for a in (0, 1):
                        bk, k_ = bank_use[("down", j + a)]
                        dve.wait_ge(free_sem[bk], k_ + 1)
                    t = gx[:, j:j + 2, :].rearrange("p j n -> p (j n)")
                    xx = x[:, j:j + 2, :].rearrange("p j n -> p (j n)")
                    bank, read, value = place(it)
                    nc.vector.tensor_tensor(t, t, bank, ALU.mult).then_inc(read, 1)
                    dve.wait_ge(read, value)
                    nc.vector.scalar_tensor_tensor(xx, t, 0.25, xx, ALU.mult, ALU.add).then_inc(s["x1_part"], 1)
                elif kind == "qkv1":
                    qkv1_bias(it[1])
                elif kind == "rope1":
                    rope1(it[1])
                elif kind == "routing_start":
                    dve.wait_ge(s["late_loaded"], 32)
                    nc.vector.tensor_copy(xn[:, :, TOKEN_COL:TOKEN_COL + 1].bitcast(I32), const("token").rearrange("p (j o) -> p j o", o=1))
                    nc.vector.memset(xn[:, :, PROB_COL + 1:RW], 0.0)
                    chain(nc.vector.memset(tanh_g[:, 1, 0:14 * E * 4], 0.0))

            lg = small[:, 0, 0:NT * E]
            l3 = lg.rearrange("p (j e) -> p j e", j=NT)
            oh3 = onehot[:, 0:NT * E].rearrange("p (j e) -> p j e", j=NT)
            desc = const("desc").rearrange("p (o e) -> p o e", o=1).to_broadcast([P, NT, E])
            maxp3 = xn[:, :, PROB_COL:PROB_COL + 1]
            t8 = nres[:, 0, 0:NT]
            t83 = t8.rearrange("p (j o) -> p j o", o=1)
            dve.wait_ge(*place(("logits", B - 1))[1:])
            chain(nc.vector.tensor_scalar_add(lg, lg, 1.0))
            chain(nc.vector.reciprocal(lg, lg))
            chain(nc.vector.tensor_reduce(maxp3, l3, AX, ALU.max))
            chain(nc.vector.tensor_tensor(l3, l3, maxp3.to_broadcast([P, NT, E]), ALU.is_ge))
            nc.vector.tensor_scalar_mul(maxp3, maxp3, 0.25)
            chain(nc.vector.tensor_tensor(l3, l3, desc, ALU.mult))
            chain(nc.vector.tensor_reduce(t83, l3, AX, ALU.max))
            chain(nc.vector.tensor_tensor(oh3, desc, t83.to_broadcast([P, NT, E]), ALU.is_equal))
            for level in range(2):
                chain(nc.vector.tensor_tensor(before_tile(level + 1), before_tile(level), before_tile(level, 1 << level), ALU.add))
            nc.vector.tensor_tensor(before_tile(3), before_tile(2), before_tile(2, 4), ALU.add).then_inc(s["onehot"], 1)
            qkv1_bias(TB)
            cnt = small[:, 2, 0:72]
            tot = small[:, 2, 64:72]
            dve.wait_ge(s["counts"], 1)
            chain(nc.vector.tensor_copy(cnt, ps[:, 5, 0:72]))
            big = lg.rearrange("p (e k) -> p e k", e=E)
            tiles = nres[:, 0, 0:8]
            base = nres[:, 0, 8:16]
            end = nres[:, 1, 0:8]
            chain(nc.vector.tensor_tensor(big, tot.rearrange("p (e o) -> p e o", o=1).to_broadcast([P, E, NT]),
                                          const("full").rearrange("p (o k) -> p o k", o=1).to_broadcast([P, E, NT]), ALU.is_gt))
            chain(nc.vector.tensor_reduce(tiles.rearrange("p (e o) -> p e o", o=1), big, AX, ALU.add))
            chain(nc.vector.tensor_tensor(big, const("lower").rearrange("p (e k) -> p e k", e=E),
                                          tiles.rearrange("p (o k) -> p o k", o=1).to_broadcast([P, E, E]), ALU.mult))
            chain(nc.vector.tensor_reduce(base.rearrange("p (e o) -> p e o", o=1), big, AX, ALU.add))
            nc.vector.tensor_tensor(end, base, tiles, ALU.add)
            chain(nc.vector.tensor_scalar_mul(base, base, float(P)))
            c3 = cnt[:, 0:64].rearrange("p (j e) -> p j e", j=NT)
            chain(nc.vector.tensor_tensor(l3, c3, base.rearrange("p (o e) -> p o e", o=1).to_broadcast([P, NT, E]), ALU.add))
            chain(nc.vector.tensor_tensor(l3, l3, oh3, ALU.mult))
            t8b = rsum[:, 0:NT]
            chain(nc.vector.tensor_reduce(t8b.rearrange("p (j o) -> p j o", o=1), l3, AX, ALU.add))
            nc.vector.tensor_copy(smi[:], t8b).then_inc(s["slots"], 1)
            te = tanh_g[:, 0, 0:MT * E].rearrange("p (i e) -> p i e", i=MT)
            tr = tanh_g[:, 0, 256:256 + MT]
            chain(nc.vector.tensor_tensor(te, const("tile_id").rearrange("p (i o) -> p i o", o=1).to_broadcast([P, MT, E]),
                                          end.rearrange("p (o e) -> p o e", o=1).to_broadcast([P, MT, E]), ALU.is_ge))
            chain(nc.vector.tensor_reduce(tr.rearrange("p (i o) -> p i o", o=1), te, AX, ALU.add))
            nc.vector.tensor_scalar_min(tile_e[:], tr, float(E - 1))
            nc.vector.tensor_copy(tiles_n[:], end[:, E - 1:E]).then_inc(s["tile_experts"], 1)

            def key_norms(b):
                dve.wait_ge(s["ksum_sq"], b + 1)
                chain(nc.vector.tensor_scalar_max(st1[:, 0, TB * b:TB * b + TB], st1[:, 3, TB * b:TB * b + TB], 1e-24))
                for stage in range(4):
                    inverse_root(TB * b, TB * b + TB, stage)

            def sum_tiles(b):
                dve.wait_ge(s["kv_ready"], b + 1)
                j0 = TB * b
                chain(nc.vector.tensor_scalar_mul(kv[:, j0, :], kv[:, j0, :], st1[:, 4, j0:j0 + 1]))
                for j in range(j0 + 1, j0 + TB):
                    ins = nc.vector.scalar_tensor_tensor(kv[:, j0, :], kv[:, j, :], st1[:, 4, j:j + 1], kv[:, j0, :], ALU.mult, ALU.add)
                    if j < j0 + TB - 1:
                        chain(ins)
                ins.then_inc(s["kv_summed"], 1)

            def scaled_output(b):
                dve.wait_ge(s["acol_psum"], b + 1)
                nc.vector.tensor_copy(acol[:, KD * b:KD * b + KD], ps[:, 7 if b else 5, 0:KD]).then_inc(s["acol_ready"], 1)
                dve.wait_ge(s["acol_ready"], b + 1)
                for k in range(KD):
                    nc.vector.tensor_scalar_mul(wsc[:, b, k, :], wout[:, k, :], acol[:, KD * b + k:KD * b + k + 1]).then_inc(s["wsc_ready"], 1)

            def branch(c):
                two = lambda a: a[:, 2 * c:2 * c + 2, 0:D]
                bank = ps[:, branch_bank[c], :].rearrange("p (j n) -> p j n", j=2)
                dve.wait_ge(s["branch_psum"], c + 1)
                nc.vector.tensor_tensor(two(gx), bank, bout_b.rearrange("p (o n) -> p o n", o=1).to_broadcast([P, 2, D]), ALU.add
                                        ).then_inc(s["branch_free"], 1)
                dve.wait_ge(s["branch_free"], c + 1)
                nc.vector.tensor_tensor(two(gx), two(gx), two(xn), ALU.add).then_inc(s["branch_ready"], 1)

            qkv1_bias(TB + 1)
            key_norms(0)
            qkv1_bias(TB + 2)
            sum_tiles(0)
            qkv1_bias(TB + 3)
            scaled_output(0)
            branch(0)
            branch(1)
            rope1(1)

            def result(k):
                dve.wait_ge(s["e_down"], k + 1)
                if k >= 2:
                    dve.wait_ge(y_store[k % 2], 16 * (k // 2))
                nc.vector.tensor_scalar_mul(ysb[:, k % 2, :], ps[:, 6, 0:D], slot_row(k, PROB_COL, PROB_COL + 1)).then_inc(s["y_half"], 1)
                dve.wait_ge(s["y_tanh"], k + 1)
                nc.vector.scalar_tensor_tensor(ysb[:, k % 2, :], ytanh, 1.0, ysb[:, k % 2, :], ALU.add, ALU.mult).then_inc(s["y_ready"], 1)

            def tile(i):
                dve.wait_ge(s["e_tanh"], i + 1)
                if i >= 2:
                    dve.wait_ge(s["hm_T"], i - 1)
                nc.vector.scalar_tensor_tensor(gated[:, i % 2, :], tanh_g[:, i % 2, :], 1.0, ps[:, i % 2, :], ALU.add, ALU.mult
                                               ).then_inc(s["e_gated"], 1)
                dve.wait_ge(s["e_gated"], i + 1)
                dve.wait_ge(s["e_up"], i + 1)
                nc.vector.tensor_tensor(hm[:, i % 2, :], gated[:, i % 2, :], ps[:, 2 + i % 2, :], ALU.mult).then_inc(s["e_h"], 1)
                if i:
                    result(i - 1)

            for i in range(SURE):
                tile(i)
                for kind, n in side_work(i):
                    if kind == "norm":
                        key_norms(n)
                        sum_tiles(n)
                    elif kind == "sum":
                        scaled_output(n)
                    elif kind == "branch":
                        branch(n)
            n_tiles = dve.value_load(tiles_n[0:1, 0:1], min_val=SURE, max_val=MT)
            tiles_from(dve, n_tiles, SURE, tile, lambda i: result(i - 1))

            def total(q):
                if q == NT // 2 - 1:
                    dve.wait_ge(s["product_ready"], 1)
                else:
                    dve.wait_ge(s["product_done"], q + 1)
                nc.vector.tensor_tensor(x[:, 2 * q:2 * q + 2, :], ya[:, 2 * q:2 * q + 2, :], x[:, 2 * q:2 * q + 2, :], ALU.add
                                        ).then_inc(s["out_ready"], 1)

            for q in range(NT // 2):
                if q < NT // 2 - 1:
                    dve.wait_ge(result_sem[q], 16)
                    nc.vector.tensor_tensor(ya[:, 2 * q:2 * q + 2, :], yg[:, 2 * q:2 * q + 2, :], gx[:, 2 * q:2 * q + 2, :], ALU.mult
                                            ).then_inc(s["product_done"], 1)
                if q:
                    total(q - 1)
            total(NT // 2 - 1)

        @block.tensor
        def _(pe):
            pe.wait_ge(s["const_loaded"], 16)
            for _ in range(WARM_UP):
                nc.tensor.transpose(ps[:, 7, 0:P], ident, ident)
            for b in range(B):
                for t in range(TB):
                    pe.wait_ge(s["rows_norm"], TB * b + t + 1)
                    for k in range(KD):
                        last = nc.tensor.transpose(ps[:, KD * b + k, P * t:P * t + P], xn[:, TB * b + t, P * k:P * k + P], ident)
                        if t == TB - 1:
                            last.then_inc(s["xnT_psum"], 1)
                pe.wait_ge(s["xnT_ready"], KD * (b + 1))
                if b == 0:
                    pe.wait_ge(s["wqkv_loaded"], 16)
                for t in range(TB):
                    j = TB * b + t
                    for k in range(KD):
                        last = nc.tensor.matmul(ps[:, 4 - 4 * b + t, 0:384], xnT[:, k, P * j:P * j + P], wqkv[:, k, :],
                                                start=k == 0, stop=k == KD - 1)
                    last.then_inc(s["qkv_psum"], 1)
            pe.wait_ge(s["qk_copied"], 2)
            pe.wait_ge(s["v_copied"], 1)
            pe.wait_ge(s["wgu_loaded"], 16)
            pe.wait_ge(s["identb_ready"], 1)

            def misc_bank(it):
                if misc_use.get(it):
                    pe.wait_ge(s["misc_free"], misc_use[it])

            def wo_product(b, c, a, k, bank):
                at_ = P * (2 * c + a)
                return nc.tensor.matmul(bank[:, D * a:D * a + D], anT[:, k, at_:at_ + P], wo[:, k, :],
                                        start=k == 0 and a == 0, stop=k == KD - 1 and a == 1)

            def qkv(j):
                bank = qkv1_bank(j)
                if j == 0:
                    pe.wait_ge(s["layer1_loaded"], 64)
                    for bk in (6, 7):
                        pe.wait_ge(free_sem[bk], uses[bk])
                elif j == 1:
                    pe.wait_ge(s["exp_done"], GR * STEPS)
                    pe.wait_ge(s["heads_copied"], UNITS)
                else:
                    pe.wait_ge(s["qkv1_ready"], j - 1)
                for lo, hi, a in ((0, 512, 0), (512, 768, 1)):
                    for k in range(KD):
                        last = nc.tensor.matmul(bank[:, a, 0:hi - lo], xnT[:, k, P * j:P * j + P], win[:, k, lo:hi],
                                                start=k == 0, stop=k == KD - 1)
                last.then_inc(s["qkv1_psum"], 1)

            for it in plan:
                kind = it[0]
                if kind == "stack_T":
                    _, b, c = it
                    n = stack_order.index(c) if b == 0 else 10 + c
                    if b == 0 and n == 0 or b and c == 0:
                        pe.wait_ge(s["parts_done"], b + 1)
                        pe.wait_ge(s["slots_copied"], 3 * (b + 1))
                    if b:
                        misc_bank(it)
                    elif n >= 4:
                        pe.wait_ge(s["stack_copied2" if n % 2 else "stack_copied"], (n - 4) // 2 + 1)
                    elif n == 2:
                        pe.wait_ge(s["qk_copied"], 2 * B)
                        pe.wait_ge(s["v_copied"], B)
                    src, _ = stacked(b, c, n)
                    for a in range(2):
                        for t in range(TB):
                            at_ = (a * TB + t) * P
                            last = nc.tensor.transpose(src[:, at_:at_ + P], stack[:, QKH * t + 2 * c + a, :], identb[:])
                    last.then_inc(s["stack_T"], 1)
                elif kind == "rows_T":
                    _, b, k = it
                    bank = place(it)[0]
                    pe.wait_ge(s["rows_norm"], NT + TB * (b + 1))
                    misc_bank(it)
                    for t in range(TB):
                        last = nc.tensor.transpose(bank[:, P * t:P * t + P], xn[:, TB * b + t, P * k:P * k + P], ident)
                    last.then_inc(s["rows_T"], 1)
                elif kind == "logits":
                    b = it[1]
                    if b == 0:
                        pe.wait_ge(s["late_loaded"], 32)
                    bank = place(it)[0]
                    if bank is misc:
                        pe.wait_ge(*place(("rows_T", b, KD - 1))[1:])
                    for k in range(KD):
                        pe.wait_ge(*place(("rows_T", b, k))[1:])
                        for t in range(TB):
                            j = TB * b + t
                            last = nc.tensor.matmul(bank[:, E * t:E * t + E], xnT[:, k, P * j:P * j + P], router[:, k, :],
                                                    start=k == 0 and t == 0, stop=k == KD - 1 and t == TB - 1)
                    last.then_inc(s["logits"], 1)
                elif kind == "score":
                    m = it[1]
                    b, g, hh, t = score_at(m)
                    if m == 0:
                        pe.wait_ge(s["stack_copied"], 5)
                        pe.wait_ge(s["stack_copied2"], 5)
                        pe.wait_ge(s["vone"], 3)
                    if m == 16 * KVH:
                        pe.wait_ge(s["misc_free"], misc_use[("stack_T", 1, 9)] + 1)
                    if m >= 2:
                        pe.wait_ge(s["max_done"], m - 1)
                    nc.tensor.matmul(ps[:, m % 2, :], qs[0:KS, b, GR * g + hh, P * t:P * t + P], ks[0:KS, b, g, :],
                                     start=True, stop=True).then_inc(s["score_ready"], 1)
                elif kind == "max_rows":
                    u = it[1]
                    pe.wait_ge(s["mparts_ready"], u + 1)
                    misc_bank(it)
                    for t in range(TB):
                        last = nc.tensor.transpose(miscb[0:SPLIT * GR, P * t:P * t + P],
                                                   mparts[:, t, :, :].rearrange("p a h -> p (a h)"), identb[:])
                    last.then_inc(s["mrow_psum"], 1)
                elif kind == "prob":
                    _, n, hh = it
                    u, t = divmod(n, TB)
                    b, g = divmod(u, KVH)
                    if t == 0 and hh == 0:
                        pe.wait_ge(row_sem[u % 2], 48 * (u // 2 + 1))
                    q = GR * n + hh
                    if q >= 2:
                        pe.wait_ge(s["exp_done"], q - 1)
                    nc.tensor.matmul(ps[:, 2 + hh % 2, :], ks[0:KM, b, g, P * t:P * t + P], qs[0:KM, b, GR * g + hh, :],
                                     start=True, stop=True).then_inc(s["prob_ready"], 1)
                elif kind == "values":
                    n = it[1]
                    u, t = divmod(n, TB)
                    b, g = divmod(u, KVH)
                    pe.wait_ge(s["exp_done"], GR * (n + 1))
                    if t == 0 and u:
                        pe.wait_ge(s["heads_copied"], u)
                    for hh in range(GR):
                        last = nc.tensor.matmul(ps[VW * hh:VW * hh + VW, 4, :], vaug[:, TB * b + t, g, :], probs[:, n % 2, hh, :],
                                                start=t == 0, stop=t == TB - 1)
                    last.then_inc(s["values_done"], 1)
                elif kind == "heads_norm":
                    u = it[1]
                    pe.wait_ge(s["heads_copied"], u + 1)
                    misc_bank(it)
                    for t in range(TB):
                        last = nc.tensor.transpose(misc[:, P * t:P * t + P], oTs[:, P * t:P * t + P], ident)
                    last.then_inc(s["heads_T"], 1)
                elif kind == "attn_T":
                    _, b, k = it
                    bank = place(it)[0]
                    g = (KVH // KD) * (k + 1) - 1 if b == B - 1 else KVH - 1
                    pe.wait_ge(s["misc_free"], misc_use[("heads_norm", KVH * b + g)] + 1)
                    misc_bank(it)
                    for t in range(TB):
                        last = nc.tensor.transpose(bank[:, P * t:P * t + P], an[:, t, P * k:P * k + P], ident)
                    last.then_inc(s["attn_T_ready"], 1)
                elif kind == "wo_half":
                    b = it[1]
                    pe.wait_ge(*place(("attn_T", b, 0))[1:])
                    pe.wait_ge(s["max_done"], 16 * UNITS)
                    for c in range(TB // 2):
                        for a in range(2):
                            wo_product(b, c, a, 0, place(("wo", b, c))[0])
                elif kind == "wo":
                    _, b, c = it
                    pe.wait_ge(*place(("attn_T", b, KD - 1))[1:])
                    pe.wait_ge(s["wo_loaded"], 16)
                    misc_bank(it)
                    for a in range(2):
                        for k in range(1 if b == B - 1 else 0, KD):
                            last = wo_product(b, c, a, k, place(it)[0])
                    last.then_inc(s["wo_ready"], 1)
                elif kind == "qkv1":
                    qkv(it[1])
                elif kind in ("gate", "up"):
                    _, c, k = it
                    b, i = divmod(c, NI)
                    bk, n = bank_use[(kind, c)]
                    if k == 0 and n:
                        pe.wait_ge(free_sem[bk], n)
                    half = int(kind == "up")
                    if c == 0:
                        pe.wait_ge(s["w_low_ready"], weight_pieces.index((k, INTER * half)) + 1)
                    if i == 0:
                        pe.wait_ge(s["x_low_ready"], KD * b + k + 1)
                    col = P * i + INTER * half
                    w_parts = [w_high(k, col, col + P), w_low(k, col, col + P)]
                    x_parts = [x_high(b, k), x_low(b, k)]
                    for n_, (w_, x_) in enumerate(((0, 0), (0, 1), (1, 0))):
                        ins = nc.tensor.matmul(ps[:, bk, :], w_parts[w_], x_parts[x_], start=k == 0 and n_ == 0, stop=k == KD - 1 and n_ == 2)
                    if k == KD - 1:
                        ins.then_inc(s[kind + "_ready"], 1)
                elif kind == "down":
                    _, j, i = it
                    bk, n = bank_use[("down", j)]
                    if i == 0:
                        pe.wait_ge(free_sem[bk], n)
                        if j == 0:
                            pe.wait_ge(s["wdn_loaded"], 16)
                    if j % TB == 0:
                        pe.wait_ge(s["up_free"], bank_use[("up", NI * (j // TB) + i)][1] + 1)
                    ins = nc.tensor.matmul(ps[:, bk, 0:D], hT[:, i, P * (j % TB):P * (j % TB) + P], wdn[:, i, :],
                                           start=i == 0, stop=i == NI - 1)
                    if i == NI - 1:
                        ins.then_inc(s["down_ready"], 1)

            qkv(TB)
            pe.wait_ge(s["onehot"], 1)
            nc.tensor.matmul(ps[:, 5, 0:NT * E + E], const("before"), onehot, start=True, stop=False)
            nc.tensor.matmul(ps[:, 5, 0:NT * E + E], const("ones"), before_tile(3), start=False, stop=True).then_inc(s["counts"], 1)
            qkv(TB + 1)
            qkv(TB + 2)

            def rows_T(i):
                pe.wait_ge(x_sem[i % XR], 16 * (i // XR + 1))
                if i:
                    pe.wait_ge(s["xsT_ready"], i)
                for k in range(KD):
                    last = nc.tensor.transpose(ps[:, 4, P * k:P * k + P], slot_row(i, P * k, P * k + P), ident)
                last.then_inc(s["xs_T"], 1)

            def hidden_T(i):
                pe.wait_ge(s["e_h"], i + 1)
                if i:
                    pe.wait_ge(s["hmT_ready"], i)
                for k in range(KE):
                    last = nc.tensor.transpose(ps[:, 5, P * k:P * k + P], hm[:, i % 2, P * k:P * k + P], ident)
                last.then_inc(s["hm_T"], 1)

            def down(i):
                pe.wait_ge(s["hmT_ready"], i + 1)
                if i:
                    pe.wait_ge(s["y_half"], i)
                else:
                    pe.wait_ge(s["branch_free"], 2)
                for k in range(KE):
                    last = nc.tensor.matmul(ps[:, 6, 0:D], hmT[:, i % 2, P * k:P * k + P],
                                            Wm[:, bass.ds(base[i] + 2 * KD * EI + D * k, D)], start=k == 0, stop=k == KE - 1)
                last.then_inc(s["e_down"], 1)

            base = {}

            def tile(i):
                chosen = pe.value_load(tile_e[0:1, i:i + 1], min_val=0, max_val=E - 1)
                pe.wait_ge(s["experts_here"], chosen + 1)
                base[i] = chosen * EW
                pe.wait_ge(s["xsT_ready"], i + 1)
                if i >= 2:
                    pe.wait_ge(s["e_gated"], i - 1)
                for k in range(KD):
                    last = nc.tensor.matmul(ps[:, i % 2, :], xsT[:, i % 2, P * k:P * k + P], Wm[:, bass.ds(base[i] + EI * k, EI)],
                                            start=k == 0, stop=k == KD - 1)
                last.then_inc(s["e_gate"], 1)
                if i:
                    hidden_T(i - 1)
                if i >= 2:
                    pe.wait_ge(s["e_h"], i - 1)
                for k in range(KD):
                    last = nc.tensor.matmul(ps[:, 2 + i % 2, :], xsT[:, i % 2, P * k:P * k + P], Wm[:, bass.ds(base[i] + EI * (KD + k), EI)],
                                            start=k == 0, stop=k == KD - 1)
                last.then_inc(s["e_up"], 1)
                if i + 1 < MT:
                    rows_T(i + 1)
                if i:
                    down(i - 1)

            def q_T(n):
                b, k = divmod(n, KD)
                pe.wait_ge(s["rope_q"], b + 1)
                if n == KD:
                    pe.wait_ge(s["branch_free"], 1)
                elif n > KD:
                    pe.wait_ge(s["qT_ready"], n)
                for t in range(TB):
                    last = nc.tensor.transpose(ps[:, q_bank[n], P * t:P * t + P], qkv1[b][:, t, P * k:P * k + P], ident)
                last.then_inc(s["qT_psum"], 1)

            def token_sum(b):
                if b:
                    pe.wait_ge(s["qT_ready"], B * KD)
                pe.wait_ge(s["kv_summed"], b + 1)
                for k in range(KD):
                    last = nc.tensor.matmul(ps[:, 7 if b else 5, k:k + 1], kv[:, TB * b, P * k:P * k + P], const("ones")[:, 0:1],
                                            start=True, stop=True)
                last.then_inc(s["acol_psum"], 1)

            def branch(c):
                pe.wait_ge(s["wsc_ready"], KD * (2 * c // TB + 1))
                pe.wait_ge(s["qT_ready"], KD * (2 * c // TB + 1))
                if c >= 2:
                    pe.wait_ge(s["branch_free"], c)
                for a in range(2):
                    j = 2 * c + a
                    for k in range(KD):
                        last = nc.tensor.matmul(ps[:, branch_bank[c], D * a:D * a + D], xnT[:, k, P * j:P * j + P], wsc[:, j // TB, k, :],
                                                start=k == 0, stop=k == KD - 1)
                last.then_inc(s["branch_psum"], 1)

            q_T(0)
            q_T(1)
            qkv(TB + 3)
            token_sum(0)
            pe.wait_ge(s["qkv1_ready"], NT - 1)
            branch(0)
            branch(1)
            pe.wait_ge(s["qkv1_ready"], NT)
            pe.wait_ge(s["qT_ready"], KD)
            pe.wait_ge(s["slots"], 1)
            rows_T(0)
            pe.wait_ge(s["tile_experts"], 1)
            for i in range(SURE):
                tile(i)
                for kind, n in side_work(i):
                    if kind == "q":
                        q_T(n)
                    elif kind == "sum":
                        token_sum(n)
                    elif kind == "branch":
                        branch(n)
            n_tiles = pe.value_load(tiles_n[0:1, 0:1], min_val=SURE, max_val=MT)

            def rest(i):
                hidden_T(i - 1)
                down(i - 1)

            tiles_from(pe, n_tiles, SURE, tile, rest)


def kernel(**inputs):
    import concourse.bacc as bacc
    from concourse.bass_utils import run_bass_kernel_spmd

    def deep(w):
        w = np.asarray(w)
        return np.ascontiguousarray(w.reshape(w.shape[0] // P, P, w.shape[1]).transpose(1, 0, 2))

    a = {k: np.asarray(v) for k, v in inputs.items()}
    g, u, d = a["L1_ffn_gate_w"], a["L1_ffn_up_w"], a["L1_ffn_down_w"]
    experts = np.stack([np.concatenate([deep(w[e]).reshape(P, -1) for w in (g, u, d)], axis=1) for e in range(E)])
    arrays = {
        "x": deep(a["L0_attn_hidden_states"].reshape(TOK, D)),
        "wqkv": deep(np.concatenate([a["L0_attn_Wq"], a["L0_attn_Wk"], a["L0_attn_Wv"]], axis=1)),
        "wo": deep(a["L0_attn_Wo"]),
        "wgu": deep(a["L0_ffn_w_gate_up"].T),
        "wdn": deep(a["L0_ffn_w_down"].T),
        "win": deep(a["L1_attn_W_in"].T),
        "b_in": a["L1_attn_b_in"],
        "wout": deep(a["L1_attn_W_out"].T),
        "b_out": a["L1_attn_b_out"],
        "router": deep(a["L1_ffn_router_w"]),
        "experts": experts,
        "const": constants(),
        "empty": empty_row(),
    }
    nc = bacc.Bacc("TRN2", target_bir_lowering=False, num_devices=1)
    args = [nc.dram_tensor(f"in_{n}", v.shape, mybir.dt.from_np(v.dtype), kind="ExternalInput").ap() for n, v in arrays.items()]
    out = nc.dram_tensor("out_x", (P, NT, D), F32, kind="ExternalOutput").ap()
    two_gated_blocks(nc, *args, out)
    r = run_bass_kernel_spmd(nc, [{f"in_{n}": v for n, v in arrays.items()}], core_ids=[0])
    y = r.results[0]["out_x"]
    return np.ascontiguousarray(y.transpose(1, 0, 2)).reshape(B, S, D)
```
